# Optimizing a Trainium2 kernel written in Bass

```python
import numpy as np
import jax
import jax.numpy as jnp

def _softmax(x, axis=-1):
    return jax.nn.softmax(x, axis=axis)

def _gelu(x):
    return jax.nn.gelu(x, approximate=True)

def _silu(x):
    return jax.nn.silu(x)

def _sigmoid(x):
    return jax.nn.sigmoid(x)

def _layernorm(x, axis=-1, eps=1e-05):
    m = jnp.mean(x, axis=axis, keepdims=True)
    v = jnp.var(x, axis=axis, keepdims=True)
    return (x - m) / jnp.sqrt(v + eps)

def _scatter_add(tgt, idx, src, axis=0):
    return tgt.at[idx].add(src)

def _segment_sum(src, seg, n):
    return jax.ops.segment_sum(src, seg, n)
kernel_name = 'mk_seq_postln_d1_jaxref_r8_51db84'

def setup_inputs(seed: int=0):
    np.random.seed(seed)
    _w = jnp.asarray

    def _L0_attn_setup():
        import jax, jax.numpy as jnp
        import numpy as np
        INFTY_APPROX = 1e+30
        LAM = 10000.0

        def sinusoid_embs(length, width):
            pos = jnp.arange(length, dtype=jnp.float32)
            inv_lams = 1.0 / LAM ** (jnp.arange(0, width, 2, dtype=jnp.float32) / width)
            pre = pos[:, None] * inv_lams[None, :]
            cat = jnp.concatenate([jnp.sin(pre), jnp.cos(pre)], axis=-1)
            return jnp.flip(cat, axis=0)

        def rel_shift(x):
            b, t, _ = x.shape
            x = jnp.pad(x, ((0, 0), (0, 0), (1, 0)))
            x = x.reshape(b, t + 1, t)[:, 1:, :]
            return x
        B, T, D, K, V = (2, 512, 128, 128, 256)
        key = jax.random.key(seed)
        ks = jax.random.split(key, 10)
        s_d = 1.0 / np.sqrt(D)
        s_v = 1.0 / np.sqrt(V)
        return {'x': jax.random.normal(ks[0], (B, T, D), dtype=jnp.float32), 'g_ln': jnp.ones((D,), dtype=jnp.float32), 'W_q': s_d * jax.random.normal(ks[1], (D, K), dtype=jnp.float32), 'W_k': s_d * jax.random.normal(ks[2], (D, K), dtype=jnp.float32), 'W_v': s_d * jax.random.normal(ks[3], (D, V), dtype=jnp.float32), 'W_g': s_d * jax.random.normal(ks[4], (D, V), dtype=jnp.float32), 'W_r': s_d * jax.random.normal(ks[5], (D, K), dtype=jnp.float32), 'xl_u': 0.02 * jax.random.normal(ks[6], (K,), dtype=jnp.float32), 'xl_v': 0.02 * jax.random.normal(ks[7], (K,), dtype=jnp.float32), 'W_o': s_v * jax.random.normal(ks[8], (V, D), dtype=jnp.float32)}
    _L0_attn_in = _L0_attn_setup()

    def _L0_ffn_setup():
        import jax, jax.numpy as jnp
        import numpy as np
        DIM = 128
        DEPTH = 2
        HEADS = 8
        DIM_HEAD = 64
        WINDOW = 64
        INNER = HEADS * DIM_HEAD
        HID = int(DIM * 4 * 2 / 3)
        B, N = (2, 1024)
        QK_SCALE = 8.0

        def shift_token(t):
            t1, t2 = jnp.split(t, 2, axis=-1)
            t2 = jnp.pad(t2, ((0, 0), (1, 0), (0, 0)))[:, :-1]
            return jnp.concatenate([t1, t2], axis=-1)

        def l2norm(t):
            return t / jnp.clip(jnp.linalg.norm(t, axis=-1, keepdims=True), 1e-12)

        def rotate_half(x):
            x1, x2 = jnp.split(x, 2, axis=-1)
            return jnp.concatenate([-x2, x1], axis=-1)

        def rotary_xpos(q, k):
            n = q.shape[-2]
            half_idx = jnp.arange(0, DIM_HEAD, 2, dtype=jnp.float32)
            inv_freq = 1.0 / 10000.0 ** (half_idx / DIM_HEAD)
            t = jnp.arange(n, dtype=jnp.float32)
            freqs = t[:, None] * inv_freq[None, :]
            freqs = jnp.concatenate([freqs, freqs], axis=-1)
            base = (half_idx + 0.4 * DIM_HEAD) / (1.4 * DIM_HEAD)
            power = (t - n // 2) / float(WINDOW // 2)
            scale = base[None, :] ** power[:, None]
            scale = jnp.concatenate([scale, scale], axis=-1)
            cos, sin = (jnp.cos(freqs), jnp.sin(freqs))
            q = q * cos * scale + rotate_half(q) * sin * scale
            k = k * cos / scale + rotate_half(k) * sin / scale
            return (q, k)

        def local_attention(q, k, v):
            b, h, n, d = q.shape
            w = n // WINDOW
            bq = q.reshape(b, h, w, WINDOW, d) * QK_SCALE
            bk = k.reshape(b, h, w, WINDOW, d)
            bv = v.reshape(b, h, w, WINDOW, d)

            def look_around(t):
                p = jnp.pad(t, ((0, 0), (0, 0), (1, 0), (0, 0), (0, 0)))
                return jnp.concatenate([p[:, :, :w], p[:, :, 1:]], axis=3)
            bk, bv = (look_around(bk), look_around(bv))
            bt = jnp.arange(n).reshape(w, WINDOW)
            btp = jnp.pad(bt, ((1, 0), (0, 0)), constant_values=-1)
            btk = jnp.concatenate([btp[:w], btp[1:]], axis=1)
            sim = jnp.einsum('bhwid,bhwjd->bhwij', bq, bk)
            i = bt[:, :, None]
            j = btk[:, None, :]
            mask = (i < j) | (i > j + WINDOW) | (j == -1)
            sim = jnp.where(mask, -jnp.finfo(sim.dtype).max, sim)
            attn = jax.nn.softmax(sim, axis=-1)
            out = jnp.einsum('bhwij,bhwjd->bhwid', attn, bv)
            return out.reshape(b, h, n, d)

        def _layer(x, wqkv, qs, ksc, wo, lg, lb, w1, b1, w2, b2):
            b, n, _ = x.shape
            h = shift_token(x)
            qkv = h @ wqkv
            q, k, v = jnp.split(qkv, 3, axis=-1)
            to_heads = lambda t: t.reshape(b, n, HEADS, DIM_HEAD).transpose(0, 2, 1, 3)
            q, k, v = (to_heads(q), to_heads(k), to_heads(v))
            q = l2norm(q) * qs
            k = l2norm(k) * ksc
            q, k = rotary_xpos(q, k)
            o = local_attention(q, k, v)
            o = o.transpose(0, 2, 1, 3).reshape(b, n, INNER)
            x = x + o @ wo
            h = shift_token(x)
            mu = h.mean(-1, keepdims=True)
            var = h.var(-1, keepdims=True)
            h = (h - mu) / jnp.sqrt(var + 1e-05) * lg + lb
            h = h @ w1 + b1
            a, g = jnp.split(h, 2, axis=-1)
            h = a * jax.nn.gelu(g, approximate=False)
            x = x + h @ w2 + b2
            return x
        key = jax.random.key(seed)
        ks = jax.random.split(key, 6)
        return {'x': jax.random.normal(ks[0], (B, N, DIM), jnp.float32), 'wqkv': jax.random.normal(ks[1], (DEPTH, DIM, 3 * INNER), jnp.float32) * 0.02, 'q_scale': jnp.ones((DEPTH, DIM_HEAD), jnp.float32), 'k_scale': jnp.ones((DEPTH, DIM_HEAD), jnp.float32), 'wo': jax.random.normal(ks[2], (DEPTH, INNER, DIM), jnp.float32) * 0.02, 'ln_g': jnp.ones((DEPTH, DIM), jnp.float32), 'ln_b': jnp.zeros((DEPTH, DIM), jnp.float32), 'w1': jax.random.normal(ks[3], (DEPTH, DIM, 2 * HID), jnp.float32) * 0.02, 'b1': jnp.zeros((DEPTH, 2 * HID), jnp.float32), 'w2': jax.random.normal(ks[4], (DEPTH, HID, DIM), jnp.float32) * 0.02, 'b2': jnp.zeros((DEPTH, DIM), jnp.float32)}
    _L0_ffn_in = _L0_ffn_setup()
    _d = {'L0_attn_x': _L0_attn_in['x'], 'L0_attn_g_ln': _L0_attn_in['g_ln'], 'L0_attn_W_q': _L0_attn_in['W_q'], 'L0_attn_W_k': _L0_attn_in['W_k'], 'L0_attn_W_v': _L0_attn_in['W_v'], 'L0_attn_W_g': _L0_attn_in['W_g'], 'L0_attn_W_r': _L0_attn_in['W_r'], 'L0_attn_xl_u': _L0_attn_in['xl_u'], 'L0_attn_xl_v': _L0_attn_in['xl_v'], 'L0_attn_W_o': _L0_attn_in['W_o'], 'L0_ffn_wqkv': _L0_ffn_in['wqkv'], 'L0_ffn_q_scale': _L0_ffn_in['q_scale'], 'L0_ffn_k_scale': _L0_ffn_in['k_scale'], 'L0_ffn_wo': _L0_ffn_in['wo'], 'L0_ffn_ln_g': _L0_ffn_in['ln_g'], 'L0_ffn_ln_b': _L0_ffn_in['ln_b'], 'L0_ffn_w1': _L0_ffn_in['w1'], 'L0_ffn_b1': _L0_ffn_in['b1'], 'L0_ffn_w2': _L0_ffn_in['w2'], 'L0_ffn_b2': _L0_ffn_in['b2']}
    _x0 = _d['L0_attn_x']
    _d['L0_attn_x'] = jax.random.normal(jax.random.fold_in(jax.random.key(seed), 1), (4, 1024, 128), dtype=_x0.dtype)
    del _x0
    return _d

def reference(L0_attn_x, L0_attn_g_ln, L0_attn_W_q, L0_attn_W_k, L0_attn_W_v, L0_attn_W_g, L0_attn_W_r, L0_attn_xl_u, L0_attn_xl_v, L0_attn_W_o, L0_ffn_wqkv, L0_ffn_q_scale, L0_ffn_k_scale, L0_ffn_wo, L0_ffn_ln_g, L0_ffn_ln_b, L0_ffn_w1, L0_ffn_b1, L0_ffn_w2, L0_ffn_b2):

    def _L0_attn_ref(x, g_ln, W_q, W_k, W_v, W_g, W_r, xl_u, xl_v, W_o):
        import jax, jax.numpy as jnp
        import numpy as np
        INFTY_APPROX = 1e+30
        LAM = 10000.0

        def sinusoid_embs(length, width):
            pos = jnp.arange(length, dtype=jnp.float32)
            inv_lams = 1.0 / LAM ** (jnp.arange(0, width, 2, dtype=jnp.float32) / width)
            pre = pos[:, None] * inv_lams[None, :]
            cat = jnp.concatenate([jnp.sin(pre), jnp.cos(pre)], axis=-1)
            return jnp.flip(cat, axis=0)

        def rel_shift(x):
            b, t, _ = x.shape
            x = jnp.pad(x, ((0, 0), (0, 0), (1, 0)))
            x = x.reshape(b, t + 1, t)[:, 1:, :]
            return x
        B, T, D = x.shape
        K = W_q.shape[-1]
        tau = jnp.asarray(K, x.dtype) ** 0.5
        x_tilde = x * jax.lax.rsqrt(jnp.mean(jnp.square(x), axis=-1, keepdims=True) + 1e-06)
        x_tilde = x_tilde * g_ln
        q = x_tilde @ W_q / tau
        k = x_tilde @ W_k
        v = x_tilde @ W_v
        xl_r = sinusoid_embs(T, D) @ W_r
        scores_ac = jnp.einsum('bik,bjk->bij', q + xl_u, k)
        scores_bd = jnp.einsum('bik,jk->bij', q + xl_v, xl_r)
        scores_bd = rel_shift(scores_bd)
        scores = scores_ac + scores_bd
        keep = jnp.tril(jnp.ones((T, T), dtype=bool))
        scores = scores - jnp.asarray(INFTY_APPROX, x.dtype) * jnp.logical_not(keep)
        w = jax.nn.softmax(scores, axis=-1)
        wv = jnp.einsum('bij,bjv->biv', w, v)
        wv = wv * jax.nn.silu(x_tilde @ W_g)
        res = wv @ W_o
        return res

    def _L0_ffn_ref(x, wqkv, q_scale, k_scale, wo, ln_g, ln_b, w1, b1, w2, b2):
        import jax, jax.numpy as jnp
        import numpy as np
        DIM = 128
        DEPTH = 2
        HEADS = 8
        DIM_HEAD = 64
        WINDOW = 64
        INNER = HEADS * DIM_HEAD
        HID = int(DIM * 4 * 2 / 3)
        B, N = (2, 1024)
        QK_SCALE = 8.0

        def shift_token(t):
            t1, t2 = jnp.split(t, 2, axis=-1)
            t2 = jnp.pad(t2, ((0, 0), (1, 0), (0, 0)))[:, :-1]
            return jnp.concatenate([t1, t2], axis=-1)

        def l2norm(t):
            return t / jnp.clip(jnp.linalg.norm(t, axis=-1, keepdims=True), 1e-12)

        def rotate_half(x):
            x1, x2 = jnp.split(x, 2, axis=-1)
            return jnp.concatenate([-x2, x1], axis=-1)

        def rotary_xpos(q, k):
            n = q.shape[-2]
            half_idx = jnp.arange(0, DIM_HEAD, 2, dtype=jnp.float32)
            inv_freq = 1.0 / 10000.0 ** (half_idx / DIM_HEAD)
            t = jnp.arange(n, dtype=jnp.float32)
            freqs = t[:, None] * inv_freq[None, :]
            freqs = jnp.concatenate([freqs, freqs], axis=-1)
            base = (half_idx + 0.4 * DIM_HEAD) / (1.4 * DIM_HEAD)
            power = (t - n // 2) / float(WINDOW // 2)
            scale = base[None, :] ** power[:, None]
            scale = jnp.concatenate([scale, scale], axis=-1)
            cos, sin = (jnp.cos(freqs), jnp.sin(freqs))
            q = q * cos * scale + rotate_half(q) * sin * scale
            k = k * cos / scale + rotate_half(k) * sin / scale
            return (q, k)

        def local_attention(q, k, v):
            b, h, n, d = q.shape
            w = n // WINDOW
            bq = q.reshape(b, h, w, WINDOW, d) * QK_SCALE
            bk = k.reshape(b, h, w, WINDOW, d)
            bv = v.reshape(b, h, w, WINDOW, d)

            def look_around(t):
                p = jnp.pad(t, ((0, 0), (0, 0), (1, 0), (0, 0), (0, 0)))
                return jnp.concatenate([p[:, :, :w], p[:, :, 1:]], axis=3)
            bk, bv = (look_around(bk), look_around(bv))
            bt = jnp.arange(n).reshape(w, WINDOW)
            btp = jnp.pad(bt, ((1, 0), (0, 0)), constant_values=-1)
            btk = jnp.concatenate([btp[:w], btp[1:]], axis=1)
            sim = jnp.einsum('bhwid,bhwjd->bhwij', bq, bk)
            i = bt[:, :, None]
            j = btk[:, None, :]
            mask = (i < j) | (i > j + WINDOW) | (j == -1)
            sim = jnp.where(mask, -jnp.finfo(sim.dtype).max, sim)
            attn = jax.nn.softmax(sim, axis=-1)
            out = jnp.einsum('bhwij,bhwjd->bhwid', attn, bv)
            return out.reshape(b, h, n, d)

        def _layer(x, wqkv, qs, ksc, wo, lg, lb, w1, b1, w2, b2):
            b, n, _ = x.shape
            h = shift_token(x)
            qkv = h @ wqkv
            q, k, v = jnp.split(qkv, 3, axis=-1)
            to_heads = lambda t: t.reshape(b, n, HEADS, DIM_HEAD).transpose(0, 2, 1, 3)
            q, k, v = (to_heads(q), to_heads(k), to_heads(v))
            q = l2norm(q) * qs
            k = l2norm(k) * ksc
            q, k = rotary_xpos(q, k)
            o = local_attention(q, k, v)
            o = o.transpose(0, 2, 1, 3).reshape(b, n, INNER)
            x = x + o @ wo
            h = shift_token(x)
            mu = h.mean(-1, keepdims=True)
            var = h.var(-1, keepdims=True)
            h = (h - mu) / jnp.sqrt(var + 1e-05) * lg + lb
            h = h @ w1 + b1
            a, g = jnp.split(h, 2, axis=-1)
            h = a * jax.nn.gelu(g, approximate=False)
            x = x + h @ w2 + b2
            return x
        for l in range(DEPTH):
            x = _layer(x, wqkv[l], q_scale[l], k_scale[l], wo[l], ln_g[l], ln_b[l], w1[l], b1[l], w2[l], b2[l])
        return x
    x = L0_attn_x
    x = _layernorm(x + _L0_attn_ref(x, L0_attn_g_ln, L0_attn_W_q, L0_attn_W_k, L0_attn_W_v, L0_attn_W_g, L0_attn_W_r, L0_attn_xl_u, L0_attn_xl_v, L0_attn_W_o), axis=-1)
    x = _layernorm(x + _L0_ffn_ref(x, L0_ffn_wqkv, L0_ffn_q_scale, L0_ffn_k_scale, L0_ffn_wo, L0_ffn_ln_g, L0_ffn_ln_b, L0_ffn_w1, L0_ffn_b1, L0_ffn_w2, L0_ffn_b2), axis=-1)
    return x

_drawn_inputs = setup_inputs


def setup_inputs(seed=0):
    import zlib

    import numpy as np

    out = dict(_drawn_inputs(seed))
    spreads = {'L0_attn_g_ln': (1.0, 0.2),
     'L0_ffn_q_scale': (1.0, 0.6),
     'L0_ffn_k_scale': (1.0, 0.6),
     'L0_ffn_ln_g': (1.0, 0.6),
     'L0_ffn_ln_b': (0.0, 0.8),
     'L0_ffn_b1': (0.0, 0.8),
     'L0_ffn_b2': (0.0, 0.411)}
    factors = {'L0_attn_xl_v': 6.886,
     'L0_ffn_wqkv': 3.998,
     'L0_ffn_wo': 3.959,
     'L0_ffn_w1': 6.216,
     'L0_ffn_w2': 6.126}
    for name, (base, spread) in spreads.items():
        noise = np.random.default_rng([zlib.crc32(name.encode()), seed]).standard_normal(out[name].shape)
        drawn = base * np.exp(spread * noise) if base else spread * noise
        out[name] = jnp.asarray(drawn.astype(out[name].dtype))
    for name, factor in factors.items():
        out[name] = (out[name] * factor).astype(out[name].dtype)
    return out
```

```python
from contextlib import ExitStack

import numpy as np
import concourse.bass as bass
from concourse import mybir

F32 = mybir.dt.float32
BF16 = mybir.dt.bfloat16
ALU = mybir.AluOpType
ACT = mybir.ActivationFunctionType
AX = mybir.AxisListType

P = 128
B, T, D = 4, 1024, 128
NT = T // P
CH = 512
NC = T // CH
TC = CH // P
V = 256
VC = V // P
L = 2
H, DH = 8, 64
HH = DH // 2
INNER = H * DH
W = 64
HID = int(D * 4 * 2 / 3)
HCH = [(0, 128), (128, 128), (256, HID - 256)]
TAU = float(np.float32(D) ** np.float32(0.5))
MASKED = -1e30
QUADS = [(i, q) for i in range(NT) for q in range((i + 4) // 4)]


def constants():
    f = np.float32
    pos = np.arange(T, dtype=np.float64)
    w = 1.0 / 10000.0 ** (np.arange(0, D, 2) / D)
    ang = w[:, None] * pos[None, :]
    key = np.concatenate([np.cos(ang), np.sin(ang)], 0)
    qsin = np.concatenate([np.sin(ang), np.sin(ang)], 0)
    qcos = np.concatenate([np.cos(ang), np.cos(ang)], 0)
    rel = np.stack([key, qsin, qcos], 1).astype(f)
    half = np.arange(0, DH, 2) / 1.0
    inv = 1.0 / 10000.0 ** (half / DH)
    fr = pos[:, None] * inv[None, :]
    base = (half + 0.4 * DH) / (1.4 * DH)
    sc = base[None, :] ** ((pos - T // 2) / float(W // 2))[:, None]
    two = lambda a, b: np.concatenate([a, b], 1)
    cos, sin = np.cos(fr), np.sin(fr)
    tabs = [two(cos * sc, cos * sc) * 8.0, two(sin * sc, -sin * sc) * 8.0,
            two(cos / sc, cos / sc), two(sin / sc, -sin / sc)]
    rot = np.stack(tabs, 1).reshape(NT, P, 4, DH).transpose(1, 0, 2, 3).astype(f)
    ident = np.eye(P, dtype=f)
    centre = (np.eye(P) - 1.0 / P).astype(f)
    i, j = np.arange(P)[:, None], np.arange(P)[None, :]
    causal = np.where(j <= i, 0.0, MASKED).astype(f)
    wi, c = i % W, j % W
    own, before = c <= wi, c >= wi
    first = np.where(j < W, own, before)
    second = np.where(j < W, before, own)
    m = np.where(i < W, first, second)
    m0 = np.where((i < W) & (j >= W), False, m)
    masks = [np.where(a, 0.0, MASKED) for a in (m0, m)]
    masks = np.stack([np.tile(a, (1, 4)) for a in masks], 1).astype(f)
    return {"c_rel": rel, "c_rot": np.ascontiguousarray(rot), "c_ident": ident, "c_centre": centre,
            "c_causal": causal, "c_masks": masks}


def build(nc, a, out):
    ctx = ExitStack()
    with ctx:
        def sem(name):
            return ctx.enter_context(nc.semaphore(name))

        def sb(name, shape, dt=F32, stack=None):
            return (stack or ctx).enter_context(nc.sbuf_tensor(name, shape, dt))

        ps = ctx.enter_context(nc.psum_tensor("ps", [P, 8, CH], F32))

        XS = sb("XS", [P, (L + 1) * B, T + 1])
        ident = sb("ident", [P, P])
        identb = sb("identb", [P, P], BF16)
        centre = sb("centre", [P, P])
        mean1 = sb("mean1", [P, 1])
        mhalf = sb("mhalf", [P, 16])
        causalb = sb("causalb", [P, P], BF16)
        masksb = sb("masksb", [P, 2, CH], BF16)
        wqkv = sb("wqkv", [P, L, 3 * INNER])
        wo = sb("wo", [P, L, INNER // P, D])
        w1 = sb("w1", [P, L, 2 * HID])
        w2 = sb("w2", [P, L, 3, D])
        c1 = sb("c1", [P, L, 6])
        b2 = sb("b2", [P, L])
        tcos = sb("tcos", [P, L, NT, 2, DH])
        tsin = sb("tsin", [P, L, NT, 2, DH])

        sa = ExitStack()
        sa.__enter__()
        rel = sb("rel", [P, 3, T], stack=sa)
        KEYF, QSIN, QCOS = rel[:, 0, :], rel[:, 1, :], rel[:, 2, :]
        bmat = sb("bmat", [P, 3, P], stack=sa)
        cvec = sb("cvec", [P, 3], stack=sa)
        wv = sb("wv", [P, V], stack=sa)
        wg = sb("wg", [P, V], stack=sa)
        woa = sb("woa", [P, VC, D], stack=sa)

        ss = ExitStack()
        ss.__enter__()
        raw = sb("raw", [P, 3, P], stack=ss)
        wT = sb("wT", [P, 4, P], stack=ss)
        vecs = sb("vecs", [P, 3], stack=ss)
        rot = sb("rot", [P, NT, 4, DH], stack=ss)
        qks = sb("qks", [P, L, 2, DH], stack=ss)
        lnv = sb("lnv", [P, L, 2], stack=ss)
        b1c = sb("b1c", [P, L, 6], stack=ss)
        causalf = sb("causalf", [P, P], stack=ss)
        masksf = sb("masksf", [P, 2, CH], stack=ss)
        s_load, s_load2, s_fold, s_wt, s_wte, s_wp, s_dve, s_init = (
            sem(n) for n in ("weights_loaded", "tables_loaded", "weights_folded", "transposes_done",
                             "transposes_kept", "products_done", "setup_own", "setup_done"))
        col = lambda v: v.rearrange("(p o) -> p o", o=1)
        first_loads = [
            (raw[:, 0, :], a["L0_attn_W_q"]), (raw[:, 1, :], a["L0_attn_W_k"]), (raw[:, 2, :], a["L0_attn_W_r"]),
            (vecs[:, 0:1], col(a["L0_attn_g_ln"])), (vecs[:, 1:2], col(a["L0_attn_xl_u"])),
            (vecs[:, 2:3], col(a["L0_attn_xl_v"])), (ident[:], a["c_ident"]),
            (wv[:], a["L0_attn_W_v"]), (wg[:], a["L0_attn_W_g"]),
            (woa[:], a["L0_attn_W_o"].rearrange("(m p) n -> p m n", p=P)), (rel[:], a["c_rel"]),
            (centre[:], a["c_centre"]), (causalf[:], a["c_causal"]), (masksf[:], a["c_masks"]),
        ]
        later_loads = [(rot[:], a["c_rot"])]
        for l in range(L):
            later_loads += [
                (wqkv[:, l, :], a["L0_ffn_wqkv"][l]),
                (wo[:, l], a["L0_ffn_wo"][l].rearrange("(m p) n -> p m n", p=P)),
                (w1[:, l, :], a["L0_ffn_w1"][l]),
                (b2[:, l:l + 1], col(a["L0_ffn_b2"][l])),
                (lnv[:, l, 0:1], col(a["L0_ffn_ln_g"][l])), (lnv[:, l, 1:2], col(a["L0_ffn_ln_b"][l])),
                (qks[:, l, 0, :], a["L0_ffn_q_scale"][l].partition_broadcast(P)),
                (qks[:, l, 1, :], a["L0_ffn_k_scale"][l].partition_broadcast(P)),
            ]
            for c, (o, m) in enumerate(HCH):
                later_loads += [
                    (w2[0:m, l, c, :], a["L0_ffn_w2"][l][o:o + m, :]),
                    (b1c[0:m, l, c:c + 1], col(a["L0_ffn_b1"][l][o:o + m])),
                    (b1c[0:m, l, 3 + c:4 + c], col(a["L0_ffn_b1"][l][HID + o:HID + o + m])),
                ]

        with nc.Block() as block:
            @block.sync
            def _(sp):
                for dst, src in first_loads:
                    sp.dma_start(dst, src).then_inc(s_load, 16)

            @block.scalar
            def _(act):
                for dst, src in later_loads:
                    act.dma_start(dst, src).then_inc(s_load2, 16)

            @block.gpsimd
            def _(pool):
                nc.gpsimd.memset(XS[:, :, 0:1], 0.0).then_inc(s_init, 1)
                nc.gpsimd.memset(mhalf[:], -0.5).then_inc(s_init, 1)
                nc.gpsimd.memset(mean1[:], 1.0 / P).then_inc(s_init, 1)
                pool.wait_ge(s_init, 3)

            @block.vector
            def _(dve):
                own = [0]

                def link(ins):
                    own[0] += 1
                    ins.then_inc(s_dve, 1)
                    dve.wait_ge(s_dve, own[0])

                dve.wait_ge(s_load, 16 * len(first_loads))
                g = vecs[:, 0:1]
                nc.vector.tensor_scalar(raw[:, 0, :], raw[:, 0, :], g, 1.0 / TAU, ALU.mult, ALU.mult)
                link(nc.vector.tensor_scalar(raw[:, 1, :], raw[:, 1, :], g, None, ALU.mult))
                nc.vector.tensor_scalar(wv[:], wv[:], g, None, ALU.mult)
                nc.vector.tensor_scalar(wg[:], wg[:], g, None, ALU.mult)
                nc.vector.tensor_copy(identb[:], ident[:])
                nc.vector.tensor_copy(causalb[:], causalf[:])
                link(nc.vector.tensor_copy(masksb[:], masksf[:]))
                nc.vector.tensor_copy(raw[:, 2, 0:1], raw[:, 2, 0:1]).then_inc(s_fold, 1)
                dve.wait_ge(s_wt, 1)
                nc.vector.tensor_copy(wT[:, 0:3, :], ps[:, 0, 0:3 * P].rearrange("p (w n) -> p w n", w=3))
                h = P // 2
                nc.vector.tensor_copy(wT[:, 3, 0:h], ps[:, 0, 2 * P + h:3 * P])
                nc.vector.tensor_scalar(wT[:, 3, h:P], ps[:, 0, 2 * P:2 * P + h], -1.0, None,
                                        ALU.mult).then_inc(s_wte, 1)
                dve.wait_ge(s_load2, 16 * len(later_loads))
                for l in range(L):
                    for qk in range(2):
                        for tab, out_t in ((0, tcos), (1, tsin)):
                            nc.vector.tensor_tensor(
                                out_t[:, l, :, qk, :], rot[:, :, 2 * qk + tab, :],
                                qks[:, l, qk:qk + 1, :].to_broadcast([P, NT, DH]), ALU.mult)
                dve.wait_ge(s_wp, 1)
                nc.vector.tensor_copy(bmat[:], ps[:, 1, 0:3 * P].rearrange("p (w n) -> p w n", w=3))
                nc.vector.tensor_copy(cvec[:], ps[:, 2, 0:3])
                dve.wait_ge(s_wp, 2)
                for l in range(L):
                    for j in range(6):
                        m = HCH[j % 3][1]
                        nc.vector.tensor_tensor(c1[0:m, l, j:j + 1], ps[0:m, 3, 6 * l + j:6 * l + j + 1],
                                                b1c[0:m, l, j:j + 1], ALU.add)
                    link(nc.vector.tensor_scalar(w1[:, l, :], w1[:, l, :], lnv[:, l, 0:1], None, ALU.mult))

            @block.tensor
            def _(pe):
                pe.wait_ge(s_fold, 1)
                for w in range(3):
                    last = nc.tensor.transpose(ps[:, 0, w * P:(w + 1) * P], raw[:, w, :], ident[:])
                last.then_inc(s_wt, 1)
                pe.wait_ge(s_wte, 1)
                for w in range(3):
                    nc.tensor.matmul(ps[:, 1, w * P:(w + 1) * P], wT[:, 0, :], wT[:, 1 + w, :], start=True, stop=True)
                for w in range(3):
                    last = nc.tensor.matmul(ps[:, 2, w:w + 1], wT[:, 1 + w, :], vecs[:, (1 if w == 0 else 2):(2 if w == 0 else 3)],
                                            start=True, stop=True)
                last.then_inc(s_wp, 1)
                pe.wait_ge(s_load2, 16 * len(later_loads))
                for l in range(L):
                    for j in range(6):
                        o, m = HCH[j % 3]
                        o += HID * (j // 3)
                        last = nc.tensor.matmul(ps[0:m, 3, 6 * l + j:6 * l + j + 1], w1[:, l, o:o + m],
                                                lnv[:, l, 1:2], start=True, stop=True)
                last.then_inc(s_wp, 1)
        ss.close()

        xin = sb("xin", [P, NT, D], stack=sa)
        xn = sb("xn", [P, NT, D], stack=sa)
        xsq = sb("xsq", [P, NT, D], stack=sa)
        xms = sb("xms", [P, 2, NT], stack=sa)
        xrs = sb("xrs", [P, NT], stack=sa)
        XR = sb("XR", [P, T], stack=sa)
        XT = sb("XT", [P, T], stack=sa)
        QA = sb("QA", [P, T], stack=sa)
        QB = sb("QB", [P, T], stack=sa)
        m1 = sb("m1", [P, T], stack=sa)
        m2 = sb("m2", [P, T], stack=sa)
        prob = sb("prob", [P, 2, T], stack=sa)
        nmax = sb("nmax", [P, 2], stack=sa)
        psumr = sb("psumr", [P, 2], stack=sa)
        pinv = sb("pinv", [P, 2], stack=sa)
        probT = sb("probT", [P, 2, NT, P], stack=sa)
        UT = sb("UT", [P, NC, CH], stack=sa)
        gex = sb("gex", [P, CH], stack=sa)
        gsb = sb("gsb", [P, CH], stack=sa)
        gated = sb("gated", [P, VC, CH], stack=sa)
        yT = sb("yT", [P, CH], stack=sa)
        yc = sb("yc", [P, CH], stack=sa)
        ysq = sb("ysq", [P, CH], stack=sa)
        yvar = sb("yvar", [P, TC], stack=sa)
        yrs = sb("yrs", [P, TC], stack=sa)

        (x_in, xsq_d, ms_r, rx_r, xn_r, raw_t, xn_t, xr_r, xt_r, qa_mm, p1_mm, p2_mm, qa_r, m_r, qb_r, s_mm,
         max_r, exp_r, inv_r, p_r, pt_mm, pt_ev, pv_mm, u_ev, g_mm, gex_r, gate_own, gs_r, wv_mm, gt_r, res_mm, y_r,
         cen_mm, yc_r, st_mm, var_r, rstd_r, bc_mm, x_r) = (sem(n) for n in (
             "x_loaded", "x_own", "meansq_ready", "x_scale_ready", "xn_ready", "x_transposed", "xn_transposed",
             "XR_ready", "XT_ready", "qa_done", "p1_done", "p2_done", "QA_ready", "m1m2_ready", "QB_ready",
             "scores_done", "max_ready", "exp_ready", "pinv_ready", "probs_ready", "pT_done", "probT_ready",
             "pv_done", "UT_ready", "gate_done", "gate_exp_ready", "gate_own", "gate_ready", "wv_done",
             "gated_ready", "res_done", "y_ready", "centred_done", "yc_ready", "var_done", "var_ready",
             "rstd_ready", "rstd_spread", "X_ready"))
        SLOT = {4: (0, 1), 5: (2, 3), 6: (4, 5), 7: (6, 7)}

        x_dram = a["L0_attn_x"].rearrange("b (t p) d -> p b t d", p=P)

        def quads_upto(i):
            return sum(1 for (ii, _) in QUADS if ii <= i)

        with nc.Block() as block:
            @block.sync
            def _(sp):
                with sp.Fori(0, B) as b:
                    sp.wait_ge(raw_t, b)
                    sp.wait_ge(xn_r, b)
                    sp.dma_start(xin[:].unsqueeze(1), x_dram[:, bass.ds(b, 1)]).then_inc(x_in, 16)

            @block.gpsimd
            def _(pool):
                def rstd(c, b):
                    pool.wait_ge(var_r, b * NC + (c + 1))
                    nc.gpsimd.tensor_tensor(yrs[:], yvar[:], mhalf[:, 0:TC], ALU.pow).then_inc(rstd_r, 1)

                with pool.Fori(0, B) as b:
                    pool.wait_ge(ms_r, b + 1)
                    nc.gpsimd.tensor_tensor(xrs[:], xms[:, 1, :], mhalf[:, 0:NT], ALU.pow).then_inc(rx_r, 1)
                    pool.wait_ge(m_r, b * 2 + 2)
                    nc.gpsimd.tensor_tensor(QB[:], m1[:], m2[:], ALU.add).then_inc(qb_r, 1)
                    for c in range(NC):
                        rstd(c, b)

            @block.scalar
            def _(act):
                def tail(c, k, b):
                    n = b * NC + c
                    if k in (0, 2):
                        m = k // 2
                        act.wait_ge(g_mm, b * 4 + (2 * c + m + 1))
                        nc.scalar.activation(gex[:], ps[:, 7, :], ACT.Exp, scale=-1.0).then_inc(gex_r, 1)
                    if k == 5:
                        act.wait_ge(cen_mm, n + 1)
                        nc.scalar.activation(yc[:], ps[:, 7, :], ACT.Copy).then_inc(yc_r, 1)
                        nc.scalar.activation(ysq[:], ps[:, 7, :], ACT.Square).then_inc(yc_r, 1)

                def exp(i, b):
                    act.wait_ge(max_r, b * NT + (i + 1))
                    n = P * (i + 1)
                    s = ps[:, 2 * (i % 2):2 * (i % 2) + 2, :].rearrange("p a n -> p (a n)")
                    nc.scalar.activation(prob[:, i % 2, 0:n], s[:, 0:n], ACT.Exp, bias=nmax[:, i % 2:i % 2 + 1],
                                         accum_out=psumr[:, i % 2:i % 2 + 1]).then_inc(exp_r, 1)

                def keep_probT(i, b):
                    for k, (ii, q) in enumerate(QUADS):
                        if ii == i:
                            m = min(4, i + 1 - 4 * q)
                            act.wait_ge(pt_mm, b * len(QUADS) + (k + 1))
                            nc.scalar.activation(
                                probT[:, i % 2, 4 * q:4 * q + m, :],
                                ps[:, 4 + k % 2, 0:m * P].rearrange("p (m n) -> p m n", m=m),
                                ACT.Copy).then_inc(pt_ev, 1)

                with act.Fori(0, B) as b:
                    act.wait_ge(raw_t, b + 1)
                    nc.scalar.activation(XR[:], ps[:, 4:6, :].rearrange("p a n -> p (a n)"), ACT.Copy).then_inc(xr_r, 1)
                    act.wait_ge(xn_t, b + 1)
                    nc.scalar.activation(XT[:], ps[:, 6:8, :].rearrange("p a n -> p (a n)"), ACT.Copy).then_inc(xt_r, 1)
                    act.wait_ge(qa_mm, b + 1)
                    nc.scalar.activation(QA[:], ps[:, 4:6, :].rearrange("p a n -> p (a n)"), ACT.Identity,
                                         bias=cvec[:, 0:1]).then_inc(qa_r, 1)
                    exp(0, b)
                    for i in range(NT):
                        if i + 1 < NT:
                            exp(i + 1, b)
                        keep_probT(i, b)
                        for k in SLOT.get(i, ()):
                            tail(0, k, b)
                        if i % TC == TC - 1:
                            act.wait_ge(pv_mm, b * NT + (i + 1))
                            nc.scalar.activation(UT[:, i // TC, :], ps[:, 6, :], ACT.Copy).then_inc(u_ev, 1)
                    for k in range(8):
                        tail(1, k, b)

            @block.vector
            def _(dve):
                def tail(c, k, b):
                    n = b * NC + c
                    if k in (0, 2):
                        m = k // 2
                        g = b * 4 + (2 * c + m)
                        dve.wait_ge(gex_r, g + 1)
                        nc.vector.tensor_scalar(gsb[:], gex[:], 1.0, None, ALU.add).then_inc(gate_own, 1)
                        dve.wait_ge(gate_own, g * 2 + 1)
                        nc.vector.reciprocal(gsb[:], gsb[:]).then_inc(gate_own, 1)
                        dve.wait_ge(gate_own, g * 2 + 2)
                        nc.vector.tensor_tensor(gsb[:], ps[:, 7, :], gsb[:], ALU.mult).then_inc(gs_r, 1)
                    if k in (1, 3):
                        m = k // 2
                        g = b * 4 + (2 * c + m)
                        dve.wait_ge(wv_mm, g + 1)
                        dve.wait_ge(gs_r, g + 1)
                        nc.vector.tensor_tensor(gated[:, m, :], ps[:, 7, :], gsb[:], ALU.mult).then_inc(gt_r, 1)
                    if k == 4:
                        dve.wait_ge(res_mm, n + 1)
                        dve.wait_ge(xr_r, b + 1)
                        nc.vector.tensor_tensor(yT[:], ps[:, 7, :], XR[:, c * CH:(c + 1) * CH], ALU.add).then_inc(y_r, 1)
                    if k == 6:
                        dve.wait_ge(st_mm, n + 1)
                        nc.vector.tensor_scalar(yvar[:], ps[:, 7, 0:TC], 1e-5, None, ALU.add).then_inc(var_r, 1)
                    if k == 7:
                        dve.wait_ge(bc_mm, n + 1)
                        nc.vector.tensor_tensor(XS[:, bass.ds(b, 1), 1 + c * CH:1 + (c + 1) * CH], ps[:, 7:8, :],
                                                yc[:].unsqueeze(1), ALU.mult).then_inc(x_r, 1)

                def rowmax(i, b):
                    dve.wait_ge(s_mm, b * NT + (i + 1))
                    n = P * (i + 1)
                    s = ps[:, 2 * (i % 2):2 * (i % 2) + 2, :].rearrange("p a n -> p (a n)")
                    nc.vector.tensor_reduce(nmax[:, i % 2:i % 2 + 1], s[:, 0:n], AX.X, ALU.max, negate=True).then_inc(max_r, 1)

                def normalise(i, b):
                    dve.wait_ge(exp_r, b * NT + (i + 1))
                    r = pinv[:, i % 2:i % 2 + 1]
                    nc.vector.reciprocal(r, psumr[:, i % 2:i % 2 + 1]).then_inc(inv_r, 1)
                    dve.wait_ge(inv_r, b * NT + (i + 1))
                    p = prob[:, i % 2, 0:P * (i + 1)]
                    nc.vector.tensor_scalar(p, p, r, None, ALU.mult).then_inc(p_r, 1)

                with dve.Fori(0, B) as b:
                    dve.wait_ge(x_in, b * 16 + 16)
                    nc.vector.tensor_tensor(xsq[:], xin[:], xin[:], ALU.mult).then_inc(xsq_d, 1)
                    dve.wait_ge(xsq_d, b * 2 + 1)
                    nc.vector.tensor_reduce(xms[:, 0, :], xsq[:], AX.X, ALU.add).then_inc(xsq_d, 1)
                    dve.wait_ge(xsq_d, b * 2 + 2)
                    nc.vector.tensor_scalar(xms[:, 1, :], xms[:, 0, :], 1.0 / D, 1e-6, ALU.mult, ALU.add).then_inc(ms_r, 1)
                    dve.wait_ge(rx_r, b + 1)
                    dve.wait_ge(pv_mm, b * NT)
                    nc.vector.tensor_tensor(xn[:], xin[:], xrs[:].unsqueeze(2).to_broadcast([P, NT, D]),
                                            ALU.mult).then_inc(xn_r, 1)
                    dve.wait_ge(p1_mm, b + 1)
                    nc.vector.scalar_tensor_tensor(m1[:], ps[:, 6:8, :].rearrange("p a n -> p (a n)"), cvec[:, 1:2],
                                                   QSIN, ALU.add, ALU.mult).then_inc(m_r, 1)
                    dve.wait_ge(p2_mm, b + 1)
                    nc.vector.scalar_tensor_tensor(m2[:], ps[:, 0:2, :].rearrange("p a n -> p (a n)"), cvec[:, 2:3],
                                                   QCOS, ALU.add, ALU.mult).then_inc(m_r, 1)
                    rowmax(0, b)
                    for i in range(NT):
                        if i + 1 < NT:
                            rowmax(i + 1, b)
                        normalise(i, b)
                        for k in SLOT.get(i, ()):
                            tail(0, k, b)
                    for k in range(8):
                        tail(1, k, b)

            @block.tensor
            def _(pe):
                def tail(c, k, b):
                    n = b * NC + c
                    cs = slice(c * CH, (c + 1) * CH)
                    if k in (0, 2):
                        m = k // 2
                        if m == 0:
                            pe.wait_ge(x_r, n)
                        else:
                            pe.wait_ge(gt_r, b * 4 + (2 * c + 1))
                        nc.tensor.matmul(ps[:, 7, :], wg[:, m * P:(m + 1) * P], XT[:, cs], start=True,
                                         stop=True).then_inc(g_mm, 1)
                    if k in (1, 3):
                        m = k // 2
                        pe.wait_ge(gs_r, b * 4 + (2 * c + m + 1))
                        pe.wait_ge(u_ev, n + 1)
                        nc.tensor.matmul(ps[:, 7, :], wv[:, m * P:(m + 1) * P], UT[:, c, :], start=True,
                                         stop=True).then_inc(wv_mm, 1)
                    if k == 4:
                        pe.wait_ge(gt_r, b * 4 + (2 * c + 2))
                        for m in range(VC):
                            last = nc.tensor.matmul(ps[:, 7, :], woa[:, m, :], gated[:, m, :], start=(m == 0), stop=(m == VC - 1))
                        last.then_inc(res_mm, 1)
                    if k == 5:
                        pe.wait_ge(y_r, n + 1)
                        nc.tensor.matmul(ps[:, 7, :], centre[:], yT[:], start=True, stop=True).then_inc(cen_mm, 1)
                    if k == 6:
                        pe.wait_ge(yc_r, n * 2 + 2)
                        for s in range(TC):
                            last = nc.tensor.matmul(ps[:, 7, s:s + 1], ysq[:, s * P:(s + 1) * P], mean1[:], start=True, stop=True)
                        last.then_inc(st_mm, 1)
                    if k == 7:
                        pe.wait_ge(rstd_r, n + 1)
                        for s in range(TC):
                            last = nc.tensor.matmul(ps[:, 7, s * P:(s + 1) * P], yrs[:, s:s + 1].to_broadcast([P, P]),
                                                    ident[:], start=True, stop=True)
                        last.then_inc(bc_mm, 1)

                def scores(i, b):
                    if i >= 1:
                        pe.wait_ge(exp_r, b * NT + (i - 1))
                    qs = slice(i * P, (i + 1) * P)
                    for c in range((i + TC) // TC):
                        n = min(CH, P * (i + 1) - c * CH)
                        o = ps[:, 2 * (i % 2) + c, 0:n]
                        nc.tensor.matmul(o, QA[:, qs], XT[:, c * CH:c * CH + n], start=True, stop=False)
                        diag = c == i // TC
                        last = nc.tensor.matmul(o, QB[:, qs], KEYF[:, c * CH:c * CH + n], start=False, stop=not diag)
                        if diag:
                            last = nc.tensor.matmul(o[:, n - P:n], identb[:], causalb[:], start=False, stop=True)
                    last.then_inc(s_mm, 1)

                def transpose_probs(i, b):
                    pe.wait_ge(p_r, b * NT + (i + 1))
                    for k, (ii, q) in enumerate(QUADS):
                        if ii == i:
                            if k >= 2:
                                pe.wait_ge(pt_ev, b * len(QUADS) + (k - 1))
                            for m in range(min(4, i + 1 - 4 * q)):
                                j = 4 * q + m
                                last = nc.tensor.transpose(ps[:, 4 + k % 2, m * P:(m + 1) * P],
                                                           prob[:, i % 2, j * P:(j + 1) * P], ident[:])
                            last.then_inc(pt_mm, 1)

                def mix(i, b):
                    pe.wait_ge(pt_ev, b * len(QUADS) + quads_upto(i))
                    if i == TC:
                        pe.wait_ge(u_ev, b * NC + 1)
                    for j in range(i + 1):
                        last = nc.tensor.matmul(ps[:, 6, (i % TC) * P:(i % TC + 1) * P], xn[:, j, :],
                                                probT[:, i % 2, j, :], start=(j == 0), stop=(j == i))
                    last.then_inc(pv_mm, 1)

                with pe.Fori(0, B) as b:
                    pe.wait_ge(x_in, b * 16 + 16)
                    pe.wait_ge(pt_ev, b * len(QUADS))
                    for t in range(NT):
                        last = nc.tensor.transpose(ps[:, 4 + t // TC, (t % TC) * P:(t % TC + 1) * P], xin[:, t, :], ident[:])
                    last.then_inc(raw_t, 1)
                    pe.wait_ge(xn_r, b + 1)
                    pe.wait_ge(u_ev, b * NC)
                    pe.wait_ge(x_r, b * NC)
                    for t in range(NT):
                        last = nc.tensor.transpose(ps[:, 6 + t // TC, (t % TC) * P:(t % TC + 1) * P], xn[:, t, :], ident[:])
                    last.then_inc(xn_t, 1)
                    pe.wait_ge(xr_r, b + 1)
                    pe.wait_ge(xt_r, b + 1)
                    for w, (bank, done) in enumerate(((4, qa_mm), (6, p1_mm), (0, p2_mm))):
                        if w == 2:
                            pe.wait_ge(exp_r, b * NT)
                        for c in range(NC):
                            last = nc.tensor.matmul(ps[:, bank + c, :], bmat[:, w, :], XT[:, c * CH:(c + 1) * CH],
                                                    start=True, stop=True)
                        last.then_inc(done, 1)
                    pe.wait_ge(qa_r, b + 1)
                    pe.wait_ge(qb_r, b + 1)
                    scores(0, b)
                    for i in range(NT):
                        if i + 1 < NT:
                            scores(i + 1, b)
                        transpose_probs(i, b)
                        slot = SLOT.get(i, ())
                        for k in slot[:1]:
                            tail(0, k, b)
                        mix(i, b)
                        for k in slot[1:]:
                            tail(0, k, b)
                    for k in range(8):
                        tail(1, k, b)
        sa.close()

        sf = ExitStack()
        sf.__enter__()
        ffn(nc, ctx, sem, lambda name, shape, dt=F32: sb(name, shape, dt, sf), ps, XS, ident, identb, centre, mean1, mhalf, masksb, wqkv, wo, w1, w2, c1, b2,
            tcos, tsin, x_r)
        sf.close()
        finish(nc, ctx, sem, sb, ps, XS, ident, mhalf, out)


def ffn(nc, ctx, sem, sb, ps, XS, ident, identb, centre, mean1, mhalf, masksb, wqkv, wo, w1, w2, c1, b2,
        tcos, tsin, x_r):
    X1 = sb("X1", [P, B, T + 1])
    hT = sb("hT", [P, 2, CH])
    sq = sb("sq", [P, 2, CH])
    ss16 = sb("ss16", [P, 2, 16])
    rn16 = sb("rn16", [P, 2, 16])
    work = sb("work", [P, 6, CH])
    rc = work[:, 0:2, :]
    rs = work[:, 2:4, :]
    qkr = work[:, 4:6, :]
    qkn = sb("qkn", [P, 2, 2, CH])
    VB = sb("VB", [P, 4, H, DH + 1])
    VA = sb("VA", [P, 4, H, DH + 1])
    qT = sb("qT", [P, H // 2, P])
    kT = sb("kT", [P, 2, H // 2, 3, W])
    prb = sb("prb", [P, 2, H, P])
    mx = sb("mx", [P, 2, H])
    pT = sb("pT", [P, H, P])
    oinv = sb("oinv", [P, H])
    on = sb("on", [P, H, DH])
    oT = sb("oT", [P, INNER // P, P])
    h2 = sb("h2", [P, 2, CH])
    hc = sb("hc", [P, 2, CH])
    hsq = sb("hsq", [P, CH])
    hvar = sb("hvar", [P, TC])
    hrs = sb("hrs", [P, TC])
    hn = sb("hn", [P, 2, CH])
    gel = sb("gel", [P, 3, CH])
    hid = work[:].rearrange("p (a k) n -> p a k n", a=2)

    (ini, h_r, qk_mm, v_mm, sq_r, v_r, ssr, ss_own, rn_r, rc_r, rs_r, add_r, qkn_r, tq_mm, tk_mm, qT_r, kT_r, s_mm,
     mx_r, sub_r, e_r, pt_mm, pt_r, pv_mm, oi_r, on_r, ot_mm, ot_r, wo_mm, x1_r) = (sem(n) for n in (
         "ffn_buffers_set", "hT_ready", "qk_done", "v_done", "squares_ready", "V_ready", "sumsq_ready", "sumsq_own",
         "rnorm_ready", "cos_part_ready", "sin_part_ready", "rotated_ready", "qk_ready", "qT_done",
         "kT_done", "qT_ready", "kT_ready", "win_scores_done", "win_max_ready", "win_shift_ready", "win_exp_ready",
         "win_pT_done", "win_pT_ready", "win_pv_done", "win_inv_ready", "win_out_ready", "oT_done", "oT_ready",
         "wo_done", "X1_ready"))
    (h2_r, ce_mm, hc_r, sv_mm, hv_r, hr_r, hb_mm, hn_r, w1_mm, ge_r, hid_r, w2_mm) = (sem(n) for n in (
        "h2_ready", "h2_centred", "hc_ready", "hvar_done", "hvar_ready", "hrstd_ready", "hrstd_spread", "hn_ready",
        "w1_done", "gelu_ready", "hidden_ready", "w2_done"))
    BQ, BV, BT, BS, BP = 0, 2, 3, 5, 7

    def tiles(t):
        return t // NT, t % NT

    def loops(eng, step, lead):
        for t in range(-lead, 0):
            step(0, t, NT)
        with eng.Fori(0, B - 1) as b:
            for t in range(NT):
                step(b, t, 2 * NT)
        for t in range(NT):
            step(B - 1, t, NT)

    for l in range(L):
        with nc.Block() as block:
            n0 = l * B * NT

            def cnt(b, t, per=1, k=0):
                return b * (NT * per) + ((n0 + t) * per + k)

            @block.gpsimd
            def _(pool):
                if l == 0:
                    nc.gpsimd.memset(VA[:, :, :, 0:DH], 0.0).then_inc(ini, 1)
                    nc.gpsimd.memset(VA[:, :, :, DH:DH + 1], 1.0).then_inc(ini, 1)
                    nc.gpsimd.memset(VB[:, :, :, DH:DH + 1], 1.0).then_inc(ini, 1)
                    nc.gpsimd.memset(kT[:], 0.0).then_inc(ini, 1)
                    nc.gpsimd.memset(X1[:, :, 0:1], 0.0).then_inc(ini, 1)
                    pool.wait_ge(ini, 5)

                def step(b, t, end):
                    j = t + 3
                    if j < end:
                        r = j % 2
                        pool.wait_ge(ssr, cnt(b, j, 1, 1))
                        nc.gpsimd.tensor_tensor(rn16[:, r, :], ss16[:, r, :], mhalf[:], ALU.pow).then_inc(rn_r, 1)
                        pool.wait_ge(rc_r, cnt(b, j, 1, 1))
                        pool.wait_ge(rs_r, cnt(b, j, 2, 2))
                        pool.wait_ge(qkn_r, cnt(b, j))
                        nc.gpsimd.tensor_tensor(qkr, rc, rs, ALU.add).then_inc(add_r, 1)

                loops(pool, step, 3)

            @block.scalar
            def _(act):
                if l == 0:
                    act.wait_ge(ini, 5)

                def shift(b, t):
                    db, tt = tiles(t)
                    c = tt // TC
                    g = b * NC + (l * B * NC + db * NC + c)
                    act.wait_ge(x_r, g + 1)
                    if c == 1 or db or not isinstance(b, int):
                        act.wait_ge(qk_mm, cnt(b, t - TC))
                        act.wait_ge(v_mm, cnt(b, t - TC))
                    src = b + (l * B + db)
                    lo, up = (0, D // 2), (D // 2, D)
                    nc.scalar.activation(hT[lo[0]:lo[1], c:c + 1, :],
                                         XS[lo[0]:lo[1], bass.ds(src, 1), 1 + c * CH:1 + (c + 1) * CH], ACT.Copy).then_inc(h_r, 1)
                    nc.scalar.activation(hT[up[0]:up[1], c:c + 1, :],
                                         XS[up[0]:up[1], bass.ds(src, 1), c * CH:(c + 1) * CH], ACT.Copy).then_inc(h_r, 1)

                def step(b, t, end):
                    if t == -3:
                        shift(b, 0)
                    j = t + 4
                    if j % TC == 0 and j < end and j > 0:
                        shift(b, j)
                    j = t + 3
                    if j < end:
                        act.wait_ge(qk_mm, cnt(b, j, 1, 1))
                        act.wait_ge(ssr, cnt(b, j))
                        nc.scalar.activation(sq[:], ps[:, BQ:BQ + 2, :], ACT.Square).then_inc(sq_r, 1)
                        act.wait_ge(v_mm, cnt(b, j, 1, 1))
                        if l or not isinstance(b, int) or b or j > 3:
                            act.wait_ge(pv_mm, cnt(b, j - 2, 2))
                        v = ps[:, BV, :].rearrange("p (h d) -> p h d", h=H)
                        nc.scalar.activation(VB[:, j % 4, :, 0:DH], v, ACT.Copy).then_inc(v_r, 1)
                        nc.scalar.activation(VA[0:W, j % 4, :, 0:DH], v[0:W], ACT.Copy).then_inc(v_r, 1)
                        nc.scalar.activation(VA[W:P, (j + 1) % 4, :, 0:DH], v[W:P], ACT.Copy).then_inc(v_r, 1)
                    j = t + 2
                    if 0 <= j < end:
                        act.wait_ge(tq_mm, cnt(b, j, 1, 1))
                        nc.scalar.activation(qT[:], ps[:, BT, :].rearrange("p (h n) -> p h n", n=P), ACT.Copy).then_inc(qT_r, 1)
                    j = t + 1
                    if 0 <= j < end:
                        for f in range(2):
                            act.wait_ge(pt_mm, cnt(b, j, 2, f + 1))
                            nc.scalar.activation(pT[:, 4 * f:4 * f + 4, :], ps[:, BP, :].rearrange("p (h n) -> p h n", n=P),
                                                 ACT.Copy).then_inc(pt_r, 1)
                    for f in range(2):
                        if f == 1 and t >= 0:
                            act.wait_ge(ot_mm, cnt(b, t, 1, 1))
                            nc.scalar.activation(oT[:], ps[:, BP, :].rearrange("p (m n) -> p m n", n=P), ACT.Copy).then_inc(ot_r, 1)
                        j = t + 2
                        if 0 <= j < end:
                            act.wait_ge(sub_r, cnt(b, j, 2, f + 1))
                            p = prb[:, j % 2, 4 * f:4 * f + 4, :]
                            nc.scalar.activation(p, p, ACT.Exp).then_inc(e_r, 1)

                loops(act, step, 3)

            @block.vector
            def _(dve):
                if l == 0:
                    dve.wait_ge(ini, 5)

                def step(b, t, end):
                    j = t + 3
                    if j < end:
                        r, tt = j % 2, j % NT
                        qk = ps[:, BQ:BQ + 2, :].rearrange("p a (h d) -> p a h d", h=H)
                        dve.wait_ge(sq_r, cnt(b, j, 1, 1))
                        nc.vector.tensor_reduce(ss16[:, r, :], sq[:].rearrange("p a (h d) -> p (a h) d", h=H),
                                                AX.X, ALU.add).then_inc(ss_own, 1)
                        dve.wait_ge(add_r, cnt(b, j))
                        nc.vector.tensor_tensor(rc.rearrange("p a (h d) -> p a h d", h=H), qk,
                                                tcos[:, l, tt].unsqueeze(2).to_broadcast([P, 2, H, DH]),
                                                ALU.mult).then_inc(rc_r, 1)
                        ro = rs.rearrange("p a (h d) -> p a h d", h=H)
                        for f in range(2):
                            i0, o0 = f * HH, (1 - f) * HH
                            nc.vector.tensor_tensor(
                                ro[:, :, :, o0:o0 + HH], qk[:, :, :, i0:i0 + HH],
                                tsin[:, l, tt, :, i0:i0 + HH].unsqueeze(2).to_broadcast([P, 2, H, HH]),
                                ALU.mult).then_inc(rs_r, 1)
                        dve.wait_ge(ss_own, cnt(b, j, 1, 1))
                        nc.vector.tensor_scalar(ss16[:, r, :], ss16[:, r, :], 1e-24, None, ALU.max).then_inc(ssr, 1)
                    j = t + 2
                    if 0 <= j < end:
                        dve.wait_ge(tk_mm, cnt(b, j, 1, 1))
                        kp = ps[:, BT + 1, :].rearrange("p (h s n) -> p h s n", s=2, n=W)
                        nc.vector.tensor_copy(kT[:, j % 2, :, 0:3:2, :], kp).then_inc(kT_r, 1)
                        nc.vector.tensor_copy(kT[:, (j + 1) % 2, :, 1:2, :], kp[:, :, 1:2, :]).then_inc(kT_r, 1)
                        for f in range(2):
                            dve.wait_ge(s_mm, cnt(b, j, 2, f + 1))
                            s = ps[:, BS + f, :].rearrange("p (h n) -> p h n", n=P)
                            m = mx[:, f, 0:4]
                            nc.vector.tensor_reduce(m, s, AX.X, ALU.max).then_inc(mx_r, 1)
                            dve.wait_ge(mx_r, cnt(b, j, 2, f + 1))
                            nc.vector.tensor_tensor(prb[:, j % 2, 4 * f:4 * f + 4, :], s,
                                                    m.unsqueeze(2).to_broadcast([P, 4, P]), ALU.subtract).then_inc(sub_r, 1)
                    j = t + 3
                    if j < end:
                        dve.wait_ge(add_r, cnt(b, j, 1, 1))
                        dve.wait_ge(rn_r, cnt(b, j, 1, 1))
                        nc.vector.tensor_tensor(qkn[:, j % 2].rearrange("p a (h d) -> p (a h) d", h=H),
                                                qkr.rearrange("p a (h d) -> p (a h) d", h=H),
                                                rn16[:, j % 2, :].unsqueeze(2).to_broadcast([P, 16, DH]),
                                                ALU.mult).then_inc(qkn_r, 1)
                    j = t + 1
                    if 0 <= j < end:
                        for f in range(2):
                            dve.wait_ge(pv_mm, cnt(b, j, 2, f + 1))
                            o = ps[:, BT + f, 0:4 * (DH + 1)].rearrange("p (h d) -> p h d", h=4)
                            r = oinv[:, 4 * f:4 * f + 4]
                            nc.vector.reciprocal(r.unsqueeze(2), o[:, :, DH:DH + 1]).then_inc(oi_r, 1)
                            dve.wait_ge(oi_r, cnt(b, j, 2, f + 1))
                            nc.vector.tensor_tensor(on[:, f:H:2, :], o[:, :, 0:DH],
                                                    r.unsqueeze(2).to_broadcast([P, 4, DH]), ALU.mult).then_inc(on_r, 1)
                    if t >= 0:
                        dve.wait_ge(wo_mm, cnt(b, t, 1, 1))
                        nc.vector.tensor_tensor(X1[:, bass.ds(b, 1), 1 + t * P:1 + (t + 1) * P],
                                                ps[:, BV:BV + 1, 0:P],
                                                XS[:, bass.ds(b + l * B, 1), 1 + t * P:1 + (t + 1) * P],
                                                ALU.add).then_inc(x1_r, 1)

                loops(dve, step, 3)

            @block.tensor
            def _(pe):
                if l == 0:
                    pe.wait_ge(ini, 5)

                def step(b, t, end):
                    j = t + 3
                    if j < end:
                        c, s = (j % NT) // TC, j % TC
                        h = hT[:, c, s * P:(s + 1) * P]
                        db, tt = tiles(j)
                        pe.wait_ge(h_r, b * (2 * NC) + (2 * (l * B * NC + db * NC + c) + 2))
                        pe.wait_ge(rc_r, cnt(b, j))
                        pe.wait_ge(rs_r, cnt(b, j, 2))
                        pe.wait_ge(sq_r, cnt(b, j))
                        for m in range(2):
                            last = nc.tensor.matmul(ps[:, BQ + m, :], h, wqkv[:, l, m * INNER:(m + 1) * INNER],
                                                    start=True, stop=True)
                        last.then_inc(qk_mm, 1)
                        if t > 0 or not isinstance(b, int) or b or l:
                            pe.wait_ge(x1_r, cnt(b, max(t, 0)))
                        pe.wait_ge(v_r, cnt(b, j, 3))
                        nc.tensor.matmul(ps[:, BV, :], h, wqkv[:, l, 2 * INNER:], start=True, stop=True).then_inc(v_mm, 1)
                    j = t + 2
                    if 0 <= j < end:
                        pe.wait_ge(qkn_r, cnt(b, j, 1, 1))
                        for qk, done in ((0, tq_mm), (1, tk_mm)):
                            pe.wait_ge(on_r, cnt(b, j - 1, 2, qk - 1) if (j > 1 or l or not isinstance(b, int) or b) else 0)
                            for hp in range(H // 2):
                                last = nc.tensor.transpose(ps[:, BT + qk, hp * P:(hp + 1) * P],
                                                           qkn[:, j % 2, qk, hp * P:(hp + 1) * P], ident[:])
                            last.then_inc(done, 1)
                    for f in range(2):
                        j = t + 1
                        if 0 <= j < end:
                            pe.wait_ge(e_r, cnt(b, j, 2, f + 1))
                            pe.wait_ge(pt_r, cnt(b, j, 2, f))
                            pe.wait_ge(ot_r, cnt(b, t) if (t > 0 or l or not isinstance(b, int) or b) else 0)
                            for h in range(4):
                                last = nc.tensor.transpose(ps[:, BP, h * P:(h + 1) * P], prb[:, j % 2, 4 * f + h, :], ident[:])
                            last.then_inc(pt_mm, 1)
                        j = t + 2
                        if 0 <= j < end:
                            if f == 0:
                                pe.wait_ge(qT_r, cnt(b, j, 1, 1))
                                pe.wait_ge(kT_r, cnt(b, j, 2, 2))
                            pe.wait_ge(sub_r, cnt(b, j - 1, 2, f + 1) if (j > 0 or l or not isinstance(b, int) or b) else 0)
                            nc.tensor.matmul(ps[:, BS + f, :], identb[:], masksb[:, 0 if j % NT == 0 else 1, :],
                                             start=True, stop=False, skip_group_check=True)
                            for h in range(4):
                                hp, r = h, DH * f
                                for w in range(2):
                                    keys = kT[r:r + DH, j % 2, hp, 0:2, :] if w == 0 else kT[r:r + DH, j % 2, hp, 0:3:2, :]
                                    last = nc.tensor.matmul(ps[w * W:(w + 1) * W, BS + f, h * P:(h + 1) * P],
                                                            qT[r:r + DH, hp, w * W:(w + 1) * W], keys,
                                                            start=False, stop=(h == 3), skip_group_check=True)
                            last.then_inc(s_mm, 1)
                    if t >= 0:
                        pe.wait_ge(on_r, cnt(b, t, 2, 2))
                        pe.wait_ge(pt_r, cnt(b, min(t + 2, end), 2))
                        for m in range(INNER // P):
                            last = nc.tensor.transpose(ps[:, BP, m * P:(m + 1) * P], on[:, 2 * m:2 * m + 2, :].rearrange("p h d -> p (h d)"), ident[:])
                        last.then_inc(ot_mm, 1)
                    j = t + 1
                    if 0 <= j < end:
                        pe.wait_ge(v_r, cnt(b, j, 3, 3))
                        for f in range(2):
                            pe.wait_ge(pt_r, cnt(b, j, 2, f + 1))
                            if f == 0:
                                pe.wait_ge(qT_r, cnt(b, min(j + 2, end)))
                            else:
                                pe.wait_ge(kT_r, cnt(b, min(j + 2, end), 2))
                            for h in range(4):
                                for w, val in ((0, VA), (1, VB)):
                                    last = nc.tensor.matmul(ps[w * W:(w + 1) * W, BT + f, h * (DH + 1):(h + 1) * (DH + 1)],
                                                            pT[:, 4 * f + h, w * W:(w + 1) * W], val[:, j % 4, 2 * h + f, :],
                                                            start=True, stop=True)
                            last.then_inc(pv_mm, 1)
                    if t >= 0:
                        pe.wait_ge(ot_r, cnt(b, t, 1, 1))
                        pe.wait_ge(v_r, cnt(b, min(t + 4, end), 3))
                        pe.wait_ge(x1_r, cnt(b, t))
                        for m in range(INNER // P):
                            last = nc.tensor.matmul(ps[:, BV, 0:P], wo[:, l, m, :], oT[:, m, :],
                                                    start=(m == 0), stop=(m == INNER // P - 1))
                        last.then_inc(wo_mm, 1)

                loops(pe, step, 3)

        with nc.Block() as block:
            g0 = l * B * NC
            BC, BW2 = 6, 7

            def at(b, c, per=1, k=0):
                return b * (NC * per) + ((g0 + c) * per + k)

            def rounds(eng, step, lead):
                for c in range(-lead, 0):
                    step(0, c, NC)
                with eng.Fori(0, B - 1) as b:
                    for c in range(NC):
                        step(b, c, 2 * NC)
                for c in range(NC):
                    step(B - 1, c, NC)

            @block.gpsimd
            def _(pool):
                def step(b, c, end):
                    j = c + 2
                    if j < end:
                        pool.wait_ge(hv_r, at(b, j, 1, 1))
                        nc.gpsimd.tensor_tensor(hrs[:], hvar[:], mhalf[:, 0:TC], ALU.pow).then_inc(hr_r, 1)

                rounds(pool, step, 2)

            @block.scalar
            def _(act):
                def step(b, c, end):
                    j = c + 2
                    if j < end:
                        r = j % NC
                        x = bass.ds(b + j // NC, 1)
                        act.wait_ge(x1_r, b * NT + (l * B * NT + (j + 1) * TC))
                        act.wait_ge(ce_mm, at(b, j - 1) if (j > 1 or l or not isinstance(b, int) or b) else 0)
                        nc.scalar.activation(h2[0:D // 2, r:r + 1, :], X1[0:D // 2, x, 1 + r * CH:1 + (r + 1) * CH],
                                             ACT.Copy).then_inc(h2_r, 1)
                        nc.scalar.activation(h2[D // 2:D, r:r + 1, :], X1[D // 2:D, x, r * CH:(r + 1) * CH],
                                             ACT.Copy).then_inc(h2_r, 1)
                        act.wait_ge(ce_mm, at(b, j, 1, 1))
                        act.wait_ge(hn_r, at(b, j - 1) if (j > 1 or l or not isinstance(b, int) or b) else 0)
                        nc.scalar.activation(hc[:, j % 2, :], ps[:, BC, :], ACT.Copy).then_inc(hc_r, 1)
                        nc.scalar.activation(hsq[:], ps[:, BC, :], ACT.Square).then_inc(hc_r, 1)
                    j = c + 1
                    if 0 <= j < end:
                        for k, (o, m) in enumerate(HCH):
                            act.wait_ge(w1_mm, at(b, j, 3, k + 1))
                            act.wait_ge(hid_r, at(b, j, 3, k - 2) if (j > 0 or k > 2 or l or not isinstance(b, int) or b) else 0)
                            nc.scalar.activation(gel[0:m, k, :], ps[0:m, 2 * k + 1, :], ACT.Gelu,
                                                 bias=c1[0:m, l, 3 + k:4 + k]).then_inc(ge_r, 1)

                rounds(act, step, 2)

            @block.vector
            def _(dve):
                def step(b, c, end):
                    for k, (o, m) in enumerate(HCH):
                        j = c + 2
                        if j < end and k == 1:
                            dve.wait_ge(sv_mm, at(b, j, 1, 1))
                            nc.vector.tensor_scalar(hvar[:], ps[:, BW2, 0:TC], 1e-5, None, ALU.add).then_inc(hv_r, 1)
                        if c >= 0 and k == 1:
                            dve.wait_ge(w2_mm, at(b, c, 1, 1))
                            nc.vector.scalar_tensor_tensor(
                                XS[:, bass.ds(b + (l + 1) * B, 1), 1 + c * CH:1 + (c + 1) * CH], ps[:, BW2:BW2 + 1, :],
                                b2[:, l:l + 1], X1[:, bass.ds(b, 1), 1 + c * CH:1 + (c + 1) * CH],
                                ALU.add, ALU.add).then_inc(x_r, 1)
                        if j < end and k == 2:
                            dve.wait_ge(hb_mm, at(b, j, 1, 1))
                            dve.wait_ge(hc_r, at(b, j, 2, 1))
                            nc.vector.tensor_tensor(hn[:, j % 2, :], ps[:, BC, :], hc[:, j % 2, :], ALU.mult).then_inc(hn_r, 1)
                        j = c + 1
                        if 0 <= j < end:
                            dve.wait_ge(ge_r, at(b, j, 3, k + 1))
                            nc.vector.scalar_tensor_tensor(hid[0:m, j % 2, k, :], ps[0:m, 2 * k, :], c1[0:m, l, k:k + 1],
                                                           gel[0:m, k, :], ALU.add, ALU.mult).then_inc(hid_r, 1)

                rounds(dve, step, 2)

            @block.tensor
            def _(pe):
                def step(b, c, end):
                    j = c + 2
                    if j < end:
                        pe.wait_ge(h2_r, at(b, j, 2, 2))
                        pe.wait_ge(hn_r, at(b, j))
                        nc.tensor.matmul(ps[:, BC, :], centre[:], h2[:, j % NC, :], start=True, stop=True).then_inc(ce_mm, 1)
                    for k, (o, m) in enumerate(HCH):
                        j = c + 2
                        if j < end and k == 1:
                            pe.wait_ge(hc_r, at(b, j, 2, 2))
                            pe.wait_ge(x_r, at(b, c) + B * NC if (c > 0 or l or not isinstance(b, int) or b) else 0)
                            for s in range(TC):
                                last = nc.tensor.matmul(ps[:, BW2, s:s + 1], hsq[:, s * P:(s + 1) * P], mean1[:],
                                                        start=True, stop=True)
                            last.then_inc(sv_mm, 1)
                        if c >= 0 and k == 1:
                            pe.wait_ge(hid_r, at(b, c, 3, 3))
                            pe.wait_ge(hv_r, at(b, min(c + 3, end)))
                            for kk, (oo, mm) in enumerate(HCH):
                                last = nc.tensor.matmul(ps[:, BW2, :], w2[0:mm, l, kk, :], hid[0:mm, c % 2, kk, :],
                                                        start=(kk == 0), stop=(kk == 2))
                            last.then_inc(w2_mm, 1)
                        if j < end and k == 2:
                            pe.wait_ge(hr_r, at(b, j, 1, 1))
                            for s in range(TC):
                                last = nc.tensor.matmul(ps[:, BC, s * P:(s + 1) * P], hrs[:, s:s + 1].to_broadcast([P, P]),
                                                        ident[:], start=True, stop=True)
                            last.then_inc(hb_mm, 1)
                        j = c + 1
                        if 0 <= j < end:
                            pe.wait_ge(hn_r, at(b, j, 1, 1))
                            pe.wait_ge(hid_r, at(b, j, 3, k - 2) if (j > 0 or k > 2 or l or not isinstance(b, int) or b) else 0)
                            for half in range(2):
                                last = nc.tensor.matmul(ps[0:m, 2 * k + half, :], w1[:, l, half * HID + o:half * HID + o + m],
                                                        hn[:, j % 2, :], start=True, stop=True)
                            last.then_inc(w1_mm, 1)

                rounds(pe, step, 2)


def finish(nc, ctx, sem, sb, ps, XS, ident, mhalf, out):
    ys = sb("ys", [P, 2, CH])
    mu = sb("mu", [P, 2, TC])
    zc = sb("zc", [P, 2, TC, D])
    zs = sb("zs", [P, 2, TC, D])
    zv = sb("zv", [P, 2, TC])
    zr = sb("zr", [P, 2, TC])
    zo = sb("zo", [P, 2, TC, D])
    (s_y, s_t, s_m, s_m2, s_c, s_q, s_v, s_v2, s_r, s_o, s_out) = (sem(n) for n in (
        "sum_ready", "sum_transposed", "total_ready", "mean_ready", "centred_ready", "zsquares_ready", "zsum_ready",
        "zvar_ready", "zrstd_ready", "result_ready", "result_stored"))
    out_v = out.rearrange("b (t p) d -> p b t d", p=P)
    with nc.Block() as block:
        @block.sync
        def _(sp):
            with sp.Fori(0, B) as b:
                for c in range(NC):
                    sp.wait_ge(s_o, b * NC + (c + 1))
                    sp.dma_start(out_v[:, bass.ds(b, 1), c * TC:(c + 1) * TC, :], zo[:, c:c + 1]).then_inc(s_out, 16)
            sp.wait_ge(s_out, 16 * B * NC)

        @block.gpsimd
        def _(pool):
            with pool.Fori(0, B) as b:
                for c in range(NC):
                    pool.wait_ge(s_t, b * NC + c)
                    nc.gpsimd.tensor_tensor(ys[:, c:c + 1, :], XS[:, bass.ds(b, 1), 1 + c * CH:1 + (c + 1) * CH],
                                            XS[:, bass.ds(b + L * B, 1), 1 + c * CH:1 + (c + 1) * CH], ALU.add).then_inc(s_y, 1)
                    pool.wait_ge(s_v2, b * NC + (c + 1))
                    nc.gpsimd.tensor_tensor(zr[:, c, :], zv[:, c, :], mhalf[:, 0:TC], ALU.pow).then_inc(s_r, 1)

        @block.tensor
        def _(pe):
            with pe.Fori(0, B) as b:
                for c in range(NC):
                    pe.wait_ge(s_y, b * NC + (c + 1))
                    pe.wait_ge(s_c, b * NC + c)
                    for s in range(TC):
                        last = nc.tensor.transpose(ps[:, c, s * P:(s + 1) * P], ys[:, c, s * P:(s + 1) * P], ident[:])
                    last.then_inc(s_t, 1)

        @block.scalar
        def _(act):
            with act.Fori(0, B) as b:
                for c in range(NC):
                    act.wait_ge(s_c, b * NC + (c + 1))
                    nc.scalar.activation(zs[:, c], zc[:, c], ACT.Square).then_inc(s_q, 1)

        @block.vector
        def _(dve):
            with dve.Fori(0, B) as b:
                for c in range(NC):
                    n = b * NC + (c + 1)
                    z = ps[:, c, :].rearrange("p (t d) -> p t d", d=D)
                    dve.wait_ge(s_t, n)
                    nc.vector.tensor_reduce(mu[:, c, :], z, AX.X, ALU.add).then_inc(s_m, 1)
                    dve.wait_ge(s_m, n)
                    nc.vector.tensor_scalar(mu[:, c, :], mu[:, c, :], 1.0 / D, None, ALU.mult).then_inc(s_m2, 1)
                    dve.wait_ge(s_m2, n)
                    nc.vector.tensor_tensor(zc[:, c], z, mu[:, c, :].unsqueeze(2).to_broadcast([P, TC, D]),
                                            ALU.subtract).then_inc(s_c, 1)
                    dve.wait_ge(s_q, n)
                    nc.vector.tensor_reduce(zv[:, c, :], zs[:, c], AX.X, ALU.add).then_inc(s_v, 1)
                    dve.wait_ge(s_v, n)
                    nc.vector.tensor_scalar(zv[:, c, :], zv[:, c, :], 1.0 / D, 1e-5, ALU.mult, ALU.add).then_inc(s_v2, 1)
                    dve.wait_ge(s_r, n)
                    dve.wait_ge(s_out, b * (16 * NC))
                    nc.vector.tensor_tensor(zo[:, c], zc[:, c], zr[:, c, :].unsqueeze(2).to_broadcast([P, TC, D]),
                                            ALU.mult).then_inc(s_o, 1)


def kernel(**inputs):
    import numpy as _np
    import concourse.bacc as _bacc
    from concourse import mybir as _mybir
    from concourse.bass_utils import run_bass_kernel_spmd as _run

    nc = _bacc.Bacc("TRN2", target_bir_lowering=False, num_devices=1)
    arrays, aps = {}, {}
    for name, value in {**inputs, **constants()}.items():
        arr = _np.ascontiguousarray(value)
        arrays[f"in_{name}"] = arr
        aps[name] = nc.dram_tensor(f"in_{name}", arr.shape, _mybir.dt.from_np(arr.dtype), kind="ExternalInput").ap()
    out = nc.dram_tensor("out", (B, T, D), _mybir.dt.float32, kind="ExternalOutput").ap()
    build(nc, aps, out)
    r = _run(nc, [arrays], core_ids=[0])
    return r.results[0]["out"]
```

```python
from contextlib import ExitStack

import numpy as np
import concourse.bass as bass
from concourse import mybir

F32 = mybir.dt.float32
F32R = mybir.dt.float32r
BF16 = mybir.dt.bfloat16
ALU = mybir.AluOpType
ACT = mybir.ActivationFunctionType
AX = mybir.AxisListType

P = 128
B, T, D = 4, 1024, 128
NT = T // P
CH = 512
NC = T // CH
TC = CH // P
V = 256
VC = V // P
L = 2
H, DH = 8, 64
HH = DH // 2
INNER = H * DH
W = 64
HID = int(D * 4 * 2 / 3)
HCH = [(0, 128), (128, 128), (256, HID - 256)]
FIRST = 1
TAU = float(np.float32(D) ** np.float32(0.5))
MASKED = -1e30
QUADS = [(i, q) for i in range(NT) for q in range((i + 4) // 4)]

LOOP_SEMAPHORES = (
    "x_squares", "meansq_ready", "x_scale_ready", "xn_ready", "x_transposed", "xn_transposed", "XR_ready",
    "XT_ready", "qa_done", "p1_done", "p2_done", "QA_ready", "m1m2_ready", "QB_ready", "scores_done",
    "max_ready", "exp_ready", "pinv_ready", "probs_ready", "pT_done", "probT_ready", "pv_done", "UT_ready",
    "gate_done", "gate_tanh_ready", "gate_ready", "wv_done", "gated_ready", "res_done", "y_ready",
    "centred_done", "yc_ready", "var_done", "var_ready", "rstd_ready", "rstd_spread", "X_ready", "hT_ready",
    "qk_done", "v_done", "squares_ready", "V_ready", "sumsq_ready", "sumsq_own", "rnorm_ready",
    "shifted_ready", "shifted_main_ready", "cos_part_ready", "sin_part_ready", "rotated_ready", "qk_ready", "qT_done", "kT_done", "qT_ready",
    "kT_ready", "win_scores_done", "win_max_ready", "win_shift_ready", "win_exp_ready", "win_pT_done",
    "win_pT_ready", "win_pv_done", "win_inv_ready", "win_out_ready", "oT_done", "oT_ready", "wo_done",
    "X1_ready", "h2_ready", "h2_centred", "hc_ready", "hvar_done", "hvar_ready", "hrstd_ready",
    "hrstd_spread", "hn_ready", "w1_done", "gelu_ready", "hidden_ready", "w2_done", "sum_ready",
    "sum_transposed", "total_ready", "mean_ready", "centred_ready", "zsquares_ready", "zsum_ready",
    "zvar_ready", "zrstd_ready", "result_ready",
)


def constants():
    f = np.float32
    pos = np.arange(T, dtype=np.float64)
    w = 1.0 / 10000.0 ** (np.arange(0, D, 2) / D)
    ang = w[:, None] * pos[None, :]
    key = np.concatenate([np.cos(ang), np.sin(ang)], 0)
    qsin = np.concatenate([np.sin(ang), np.sin(ang)], 0)
    qcos = np.concatenate([np.cos(ang), np.cos(ang)], 0)
    rel = np.stack([key, qsin, qcos], 1).astype(f)
    half = np.arange(0, DH, 2) / 1.0
    inv = 1.0 / 10000.0 ** (half / DH)
    fr = pos[:, None] * inv[None, :]
    base = (half + 0.4 * DH) / (1.4 * DH)
    sc = base[None, :] ** ((pos - T // 2) / float(W // 2))[:, None]
    two = lambda a, b: np.concatenate([a, b], 1)
    cos, sin = np.cos(fr), np.sin(fr)
    tabs = [two(cos * sc, cos * sc) * 8.0, two(sin * sc, -sin * sc) * 8.0,
            two(cos / sc, cos / sc), two(sin / sc, -sin / sc)]
    rot = np.stack(tabs, 1).reshape(NT, P, 4, DH).transpose(1, 0, 2, 3).astype(f)
    ident = np.eye(P, dtype=f)
    centre = (np.eye(P) - 1.0 / P).astype(f)
    i, j = np.arange(P)[:, None], np.arange(P)[None, :]
    causal = np.where(j <= i, 0.0, MASKED).astype(f)
    wi, c = i % W, j % W
    own, before = c <= wi, c >= wi
    first = np.where(j < W, own, before)
    second = np.where(j < W, before, own)
    m = np.where(i < W, first, second)
    m0 = np.where((i < W) & (j >= W), False, m)
    masks = [np.where(a, 0.0, MASKED) for a in (m0, m)]
    masks = np.stack([np.tile(a, (1, 4)) for a in masks], 1).astype(f)
    return {"c_rel": rel, "c_rot": np.ascontiguousarray(rot), "c_ident": ident, "c_centre": centre,
            "c_causal": causal, "c_masks": masks}


def build(nc, a, out):
    ctx = ExitStack()
    with ctx:
        def sem(name):
            return ctx.enter_context(nc.semaphore(name))

        loop_semaphores = {name: sem(name) for name in LOOP_SEMAPHORES}
        counted = loop_semaphores.get

        def sb(name, shape, dt=F32, stack=None):
            return (stack or ctx).enter_context(nc.sbuf_tensor(name, shape, dt))

        ps = ctx.enter_context(nc.psum_tensor("ps", [P, 8, CH], F32))

        XS = sb("XS", [P, 2 * B, T + 1])
        ident = sb("ident", [P, P])
        identb = sb("identb", [P, P], BF16)
        centre = sb("centre", [P, P])
        mean1 = sb("mean1", [P, 1])
        mhalf = sb("mhalf", [P, 16])
        causalb = sb("causalb", [P, P], BF16)
        masksb = sb("masksb", [P, 2, CH], BF16)
        wqkv_main = sb("wqkv_main", [P, L, 3 * INNER], F32R)
        wqkv_rest = sb("wqkv_rest", [P, L, 3 * INNER], F32R)
        wo = sb("wo", [P, L, INNER // P, D])
        w1 = sb("w1", [P, L, 2 * HID])
        w2 = sb("w2", [P, L, 3, D])
        c1 = sb("c1", [P, L, 6])
        b2 = sb("b2", [P, L])
        tcos = sb("tcos", [P, L, NT, 2, DH])
        tsin = sb("tsin", [P, L, NT, 2, DH])

        sa = ExitStack()
        sa.__enter__()
        wqkv = sb("wqkv", [P, L, 3 * INNER], stack=sa)
        rel = sb("rel", [P, 3, T], stack=sa)
        KEYF, QSIN, QCOS = rel[:, 0, :], rel[:, 1, :], rel[:, 2, :]
        bmat = sb("bmat", [P, 3, P], stack=sa)
        cvec = sb("cvec", [P, 3], stack=sa)
        wv = sb("wv", [P, V], stack=sa)
        wg = sb("wg", [P, V], stack=sa)
        woa = sb("woa", [P, VC, D], stack=sa)

        ss = ExitStack()
        ss.__enter__()
        raw = sb("raw", [P, 3, P], stack=ss)
        wT = sb("wT", [P, 4, P], stack=ss)
        vecs = sb("vecs", [P, 3], stack=ss)
        rot = sb("rot", [P, NT, 4, DH], stack=ss)
        qks = sb("qks", [P, L, 2, DH], stack=ss)
        lnv = sb("lnv", [P, L, 2], stack=ss)
        b1c = sb("b1c", [P, L, 6], stack=ss)
        causalf = sb("causalf", [P, P], stack=ss)
        masksf = sb("masksf", [P, 2, CH], stack=ss)
        s_load, s_load2, s_fold, s_wt, s_wte, s_wp, s_dve, s_init = (
            sem(n) for n in ("weights_loaded", "tables_loaded", "weights_folded", "transposes_done",
                             "transposes_kept", "products_done", "setup_own", "setup_done"))
        col = lambda v: v.rearrange("(p o) -> p o", o=1)
        first_loads = [
            (raw[:, 0, :], a["L0_attn_W_q"]), (raw[:, 1, :], a["L0_attn_W_k"]), (raw[:, 2, :], a["L0_attn_W_r"]),
            (vecs[:, 0:1], col(a["L0_attn_g_ln"])), (vecs[:, 1:2], col(a["L0_attn_xl_u"])),
            (vecs[:, 2:3], col(a["L0_attn_xl_v"])), (ident[:], a["c_ident"]),
            (wv[:], a["L0_attn_W_v"]), (wg[:], a["L0_attn_W_g"]),
            (woa[:], a["L0_attn_W_o"].rearrange("(m p) n -> p m n", p=P)), (rel[:], a["c_rel"]),
            (centre[:], a["c_centre"]), (causalf[:], a["c_causal"]), (masksf[:], a["c_masks"]),
        ]
        later_loads = [(rot[:], a["c_rot"])]
        for l in range(L):
            later_loads += [
                (wqkv[:, l, :], a["L0_ffn_wqkv"][l]),
                (wo[:, l], a["L0_ffn_wo"][l].rearrange("(m p) n -> p m n", p=P)),
                (w1[:, l, :], a["L0_ffn_w1"][l]),
                (b2[:, l:l + 1], col(a["L0_ffn_b2"][l])),
                (lnv[:, l, 0:1], col(a["L0_ffn_ln_g"][l])), (lnv[:, l, 1:2], col(a["L0_ffn_ln_b"][l])),
                (qks[:, l, 0, :], a["L0_ffn_q_scale"][l].partition_broadcast(P)),
                (qks[:, l, 1, :], a["L0_ffn_k_scale"][l].partition_broadcast(P)),
            ]
            for c, (o, m) in enumerate(HCH):
                later_loads += [
                    (w2[0:m, l, c, :], a["L0_ffn_w2"][l][o:o + m, :]),
                    (b1c[0:m, l, c:c + 1], col(a["L0_ffn_b1"][l][o:o + m])),
                    (b1c[0:m, l, 3 + c:4 + c], col(a["L0_ffn_b1"][l][HID + o:HID + o + m])),
                ]

        with nc.Block() as block:
            @block.sync
            def _(sp):
                for dst, src in first_loads:
                    sp.dma_start(dst, src).then_inc(s_load, 16)
                for s in loop_semaphores.values():
                    sp.sem_inc(s, FIRST)

            @block.scalar
            def _(act):
                for dst, src in later_loads:
                    act.dma_start(dst, src).then_inc(s_load2, 16)

            @block.gpsimd
            def _(pool):
                nc.gpsimd.memset(XS[:, :, 0:1], 0.0).then_inc(s_init, 1)
                nc.gpsimd.memset(mhalf[:], -0.5).then_inc(s_init, 1)
                nc.gpsimd.memset(mean1[:], 1.0 / P).then_inc(s_init, 1)
                pool.wait_ge(s_init, 3)

            @block.vector
            def _(dve):
                own = [0]

                def link(ins):
                    own[0] += 1
                    ins.then_inc(s_dve, 1)
                    dve.wait_ge(s_dve, own[0])

                dve.wait_ge(s_load, 16 * len(first_loads))
                g = vecs[:, 0:1]
                nc.vector.tensor_scalar(raw[:, 0, :], raw[:, 0, :], g, 1.0 / TAU, ALU.mult, ALU.mult)
                link(nc.vector.tensor_scalar(raw[:, 1, :], raw[:, 1, :], g, None, ALU.mult))
                nc.vector.tensor_scalar(wv[:], wv[:], g, None, ALU.mult)
                nc.vector.tensor_scalar(wg[:], wg[:], g, None, ALU.mult)
                nc.vector.tensor_copy(identb[:], ident[:])
                nc.vector.tensor_copy(causalb[:], causalf[:])
                link(nc.vector.tensor_copy(masksb[:], masksf[:]))
                nc.vector.tensor_copy(raw[:, 2, 0:1], raw[:, 2, 0:1]).then_inc(s_fold, 1)
                dve.wait_ge(s_wt, 1)
                nc.vector.tensor_copy(wT[:, 0:3, :], ps[:, 0, 0:3 * P].rearrange("p (w n) -> p w n", w=3))
                h = P // 2
                nc.vector.tensor_copy(wT[:, 3, 0:h], ps[:, 0, 2 * P + h:3 * P])
                nc.vector.tensor_scalar(wT[:, 3, h:P], ps[:, 0, 2 * P:2 * P + h], -1.0, None,
                                        ALU.mult).then_inc(s_wte, 1)
                dve.wait_ge(s_load2, 16 * len(later_loads))
                for l in range(L):
                    for qk in range(2):
                        for tab, out_t in ((0, tcos), (1, tsin)):
                            nc.vector.tensor_tensor(
                                out_t[:, l, :, qk, :], rot[:, :, 2 * qk + tab, :],
                                qks[:, l, qk:qk + 1, :].to_broadcast([P, NT, DH]), ALU.mult)
                dve.wait_ge(s_wp, 1)
                nc.vector.tensor_copy(bmat[:], ps[:, 1, 0:3 * P].rearrange("p (w n) -> p w n", w=3))
                nc.vector.tensor_copy(cvec[:], ps[:, 2, 0:3])
                dve.wait_ge(s_wp, 2)
                for l in range(L):
                    for j in range(6):
                        m = HCH[j % 3][1]
                        nc.vector.tensor_tensor(c1[0:m, l, j:j + 1], ps[0:m, 3, 6 * l + j:6 * l + j + 1],
                                                b1c[0:m, l, j:j + 1], ALU.add)
                    link(nc.vector.tensor_scalar(w1[:, l, :], w1[:, l, :], lnv[:, l, 0:1], None, ALU.mult))

            @block.tensor
            def _(pe):
                pe.wait_ge(s_fold, 1)
                for w in range(3):
                    last = nc.tensor.transpose(ps[:, 0, w * P:(w + 1) * P], raw[:, w, :], ident[:])
                last.then_inc(s_wt, 1)
                pe.wait_ge(s_wte, 1)
                for w in range(3):
                    nc.tensor.matmul(ps[:, 1, w * P:(w + 1) * P], wT[:, 0, :], wT[:, 1 + w, :], start=True, stop=True)
                for w in range(3):
                    last = nc.tensor.matmul(ps[:, 2, w:w + 1], wT[:, 1 + w, :], vecs[:, (1 if w == 0 else 2):(2 if w == 0 else 3)],
                                            start=True, stop=True)
                last.then_inc(s_wp, 1)
                pe.wait_ge(s_load2, 16 * len(later_loads))
                for l in range(L):
                    for j in range(6):
                        o, m = HCH[j % 3]
                        o += HID * (j // 3)
                        last = nc.tensor.matmul(ps[0:m, 3, 6 * l + j:6 * l + j + 1], w1[:, l, o:o + m],
                                                lnv[:, l, 1:2], start=True, stop=True)
                last.then_inc(s_wp, 1)
        ss.close()

        xin = sb("xin", [P, NT, D], stack=sa)
        xn = sb("xn", [P, NT, D], stack=sa)
        xsq = sb("xsq", [P, NT, D], stack=sa)
        xms = sb("xms", [P, 2, NT], stack=sa)
        xrs = sb("xrs", [P, NT], stack=sa)
        XR = sb("XR", [P, T], stack=sa)
        XT = sb("XT", [P, T], stack=sa)
        QA = sb("QA", [P, T], stack=sa)
        QB = sb("QB", [P, T], stack=sa)
        m1 = sb("m1", [P, T], stack=sa)
        m2 = sb("m2", [P, T], stack=sa)
        prob = sb("prob", [P, 2, T], stack=sa)
        nmax = sb("nmax", [P, 2], stack=sa)
        psumr = sb("psumr", [P, 2], stack=sa)
        pinv = sb("pinv", [P, 2], stack=sa)
        probT = sb("probT", [P, 2, NT, P], stack=sa)
        UT = sb("UT", [P, NC, CH], stack=sa)
        gth = sb("gth", [P, VC, CH], stack=sa)
        gsb = sb("gsb", [P, VC, CH], stack=sa)
        gated = sb("gated", [P, VC, CH], stack=sa)
        yT = sb("yT", [P, CH], stack=sa)
        yc = sb("yc", [P, CH], stack=sa)
        ysq = sb("ysq", [P, CH], stack=sa)
        yvar = sb("yvar", [P, TC], stack=sa)
        yrs = sb("yrs", [P, TC], stack=sa)

        (xsq_d, ms_r, rx_r, xn_r, raw_t, xn_t, xr_r, xt_r, qa_mm, p1_mm, p2_mm, qa_r, m_r, qb_r, s_mm,
         max_r, exp_r, inv_r, p_r, pt_mm, pt_ev, pv_mm, u_ev, g_mm, gth_r, gs_r, wv_mm, gt_r, res_mm, y_r,
         cen_mm, yc_r, st_mm, var_r, rstd_r, bc_mm, x_r) = (counted(n) for n in (
             "x_squares", "meansq_ready", "x_scale_ready", "xn_ready", "x_transposed", "xn_transposed",
             "XR_ready", "XT_ready", "qa_done", "p1_done", "p2_done", "QA_ready", "m1m2_ready", "QB_ready",
             "scores_done", "max_ready", "exp_ready", "pinv_ready", "probs_ready", "pT_done", "probT_ready",
             "pv_done", "UT_ready", "gate_done", "gate_tanh_ready", "gate_ready", "wv_done",
             "gated_ready", "res_done", "y_ready", "centred_done", "yc_ready", "var_done", "var_ready",
             "rstd_ready", "rstd_spread", "X_ready"))
        x_in = sem("x_loaded")
        w_split = sem("weights_split")
        SLOT = {4: (0, 1), 5: (2, 3), 6: (4, 5), 7: (6, 7)}
        NQ = len(QUADS)

        def both(bank):
            return ps[:, bank:bank + 2, :].rearrange("p a n -> p (a n)")

        def tail_bank(c, k):
            return 6 if c == 1 and k in (2, 3) else 7

        x_dram = a["L0_attn_x"].rearrange("b (t p) d -> p b t d", p=P)

        def quads_upto(i):
            return sum(1 for (ii, _) in QUADS if ii <= i)

        with nc.Block() as block:
            @block.sync
            def _(sp):
                with sp.Fori(0, B) as b:
                    sp.wait_ge(raw_t, FIRST + b)
                    sp.wait_ge(xn_r, FIRST + b)
                    sp.dma_start(xin[:].unsqueeze(1), x_dram[:, bass.ds(b, 1)]).then_inc(x_in, 16)

            @block.gpsimd
            def _(pool):
                def token_scale(b):
                    pool.wait_ge(ms_r, FIRST + 1 + b)
                    nc.gpsimd.tensor_tensor(xrs[:], xms[:, 1, :], mhalf[:, 0:NT], ALU.pow).then_inc(rx_r, 1)

                def position_queries(b):
                    pool.wait_ge(m_r, FIRST + 2 + b * 2)
                    nc.gpsimd.tensor_tensor(QB[:], m1[:], m2[:], ALU.add).then_inc(qb_r, 1)

                def rstd(c, b):
                    pool.wait_ge(var_r, FIRST + 1 + c + b * NC)
                    nc.gpsimd.tensor_tensor(yrs[:], yvar[:], mhalf[:, 0:TC], ALU.pow).then_inc(rstd_r, 1)

                def batch(b, more):
                    if more:
                        token_scale(b + 1)
                    rstd(0, b)
                    if more:
                        position_queries(b + 1)
                    rstd(1, b)

                def split_weights():
                    for l in range(L):
                        nc.gpsimd.tensor_copy(wqkv_main[:, l, :], wqkv[:, l, :]).then_inc(w_split, 1)
                    for l in range(L):
                        pool.wait_ge(w_split, 1 + l)
                        nc.gpsimd.tensor_tensor(wqkv_rest[:, l, :], wqkv[:, l, :], wqkv_main[:, l, :].bitcast(F32),
                                                ALU.subtract)

                token_scale(0)
                position_queries(0)
                split_weights()
                with pool.Fori(0, B - 1) as b:
                    batch(b, True)
                batch(B - 1, False)

            @block.scalar
            def _(act):
                def tail(c, k, b):
                    n = FIRST + c + b * NC
                    bank = ps[:, tail_bank(c, k), :]
                    if k in (0, 2):
                        m = k // 2
                        act.wait_ge(g_mm, FIRST + (2 * c + m + 1) + b * 4)
                        nc.scalar.activation(gth[:, m, :], bank, ACT.Tanh, scale=0.5).then_inc(gth_r, 1)
                    if k == 5:
                        act.wait_ge(cen_mm, n + 1)
                        nc.scalar.activation(yc[:], bank, ACT.Copy).then_inc(yc_r, 1)
                        nc.scalar.activation(ysq[:], bank, ACT.Square).then_inc(yc_r, 1)

                def exp(i, b):
                    act.wait_ge(max_r, FIRST + (i + 1) + b * NT)
                    n = P * (i + 1)
                    nc.scalar.activation(prob[:, i % 2, 0:n], both(2 * (i % 2))[:, 0:n], ACT.Exp, bias=nmax[:, i % 2:i % 2 + 1],
                                         accum_out=psumr[:, i % 2:i % 2 + 1]).then_inc(exp_r, 1)

                def keep_probT(i, b):
                    for k, (ii, q) in enumerate(QUADS):
                        if ii == i:
                            m = min(4, i + 1 - 4 * q)
                            act.wait_ge(pt_mm, FIRST + (k + 1) + b * NQ)
                            nc.scalar.activation(
                                probT[:, i % 2, 4 * q:4 * q + m, :],
                                ps[:, 4 + k % 2, 0:m * P].rearrange("p (m n) -> p m n", m=m),
                                ACT.Copy).then_inc(pt_ev, 1)

                def keep_mixed(c, b):
                    act.wait_ge(pv_mm, FIRST + (c + 1) * TC + b * NT)
                    nc.scalar.activation(UT[:, c, :], ps[:, 6, :], ACT.Copy).then_inc(u_ev, 1)

                def keep_xT(b):
                    act.wait_ge(xn_t, FIRST + 1 + b)
                    nc.scalar.activation(XT[:], both(0), ACT.Copy).then_inc(xt_r, 1)

                def content_queries(b):
                    act.wait_ge(qa_mm, FIRST + 1 + b)
                    nc.scalar.activation(QA[:], both(2), ACT.Identity, bias=cvec[:, 0:1]).then_inc(qa_r, 1)

                def keep_raw(b):
                    act.wait_ge(raw_t, FIRST + 1 + b)
                    act.wait_ge(y_r, FIRST + b * NC)
                    nc.scalar.activation(XR[:], both(2), ACT.Copy).then_inc(xr_r, 1)

                def batch(b, more):
                    for i in range(NT):
                        if i + 1 < NT:
                            exp(i + 1, b)
                        keep_probT(i, b)
                        for k in SLOT.get(i, ()):
                            tail(0, k, b)
                        if i == TC:
                            keep_mixed(0, b)
                    tail(1, 0, b)
                    keep_mixed(1, b)
                    tail(1, 2, b)
                    if more:
                        keep_xT(b + 1)
                        content_queries(b + 1)
                    tail(1, 5, b)
                    if more:
                        keep_raw(b + 1)
                        exp(0, b + 1)

                keep_xT(0)
                content_queries(0)
                keep_raw(0)
                exp(0, 0)
                with act.Fori(0, B - 1) as b:
                    batch(b, True)
                batch(B - 1, False)

            @block.vector
            def _(dve):
                def tail(c, k, b):
                    n = FIRST + c + b * NC
                    bank = ps[:, tail_bank(c, k), :]
                    m = k // 2
                    g = FIRST + (2 * c + m) + b * 4
                    if k in (0, 2):
                        dve.wait_ge(gth_r, g + 1)
                        nc.vector.scalar_tensor_tensor(gsb[:, m, :], gth[:, m, :], 1.0, bank, ALU.add, ALU.mult).then_inc(gs_r, 1)
                    if k in (1, 3):
                        dve.wait_ge(wv_mm, g + 1)
                        dve.wait_ge(gs_r, g + 1)
                        nc.vector.scalar_tensor_tensor(gated[:, m, :], bank, 0.5, gsb[:, m, :], ALU.mult, ALU.mult).then_inc(gt_r, 1)
                    if k == 4:
                        dve.wait_ge(res_mm, n + 1)
                        dve.wait_ge(xr_r, FIRST + 1 + b)
                        nc.vector.tensor_tensor(yT[:], bank, XR[:, c * CH:(c + 1) * CH], ALU.add).then_inc(y_r, 1)
                    if k == 6:
                        dve.wait_ge(st_mm, n + 1)
                        nc.vector.tensor_scalar(yvar[:], bank[:, 0:TC], 1e-5, None, ALU.add).then_inc(var_r, 1)
                    if k == 7:
                        dve.wait_ge(bc_mm, n + 1)
                        nc.vector.tensor_tensor(XS[:, bass.ds(b, 1), 1 + c * CH:1 + (c + 1) * CH], bank.unsqueeze(1),
                                                yc[:].unsqueeze(1), ALU.mult).then_inc(x_r, 1)

                def rowmax(i, b):
                    dve.wait_ge(s_mm, FIRST + (i + 1) + b * NT)
                    nc.vector.tensor_reduce(nmax[:, i % 2:i % 2 + 1], both(2 * (i % 2))[:, 0:P * (i + 1)], AX.X, ALU.max,
                                            negate=True).then_inc(max_r, 1)

                def normalise(i, b):
                    dve.wait_ge(exp_r, FIRST + (i + 1) + b * NT)
                    r = pinv[:, i % 2:i % 2 + 1]
                    nc.vector.reciprocal(r, psumr[:, i % 2:i % 2 + 1]).then_inc(inv_r, 1)
                    dve.wait_ge(inv_r, FIRST + (i + 1) + b * NT)
                    p = prob[:, i % 2, 0:P * (i + 1)]
                    nc.vector.tensor_scalar(p, p, r, None, ALU.mult).then_inc(p_r, 1)

                def mean_square(b):
                    dve.wait_ge(x_in, 16 + b * 16)
                    nc.vector.tensor_tensor(xsq[:], xin[:], xin[:], ALU.mult).then_inc(xsq_d, 1)
                    dve.wait_ge(xsq_d, FIRST + 1 + b * 2)
                    nc.vector.tensor_reduce(xms[:, 0, :], xsq[:], AX.X, ALU.add).then_inc(xsq_d, 1)
                    dve.wait_ge(xsq_d, FIRST + 2 + b * 2)
                    nc.vector.tensor_scalar(xms[:, 1, :], xms[:, 0, :], 1.0 / D, 1e-6, ALU.mult, ALU.add).then_inc(ms_r, 1)

                def scale_tokens(b):
                    dve.wait_ge(rx_r, FIRST + 1 + b)
                    dve.wait_ge(pv_mm, FIRST + b * NT)
                    nc.vector.tensor_tensor(xn[:], xin[:], xrs[:].unsqueeze(2).to_broadcast([P, NT, D]),
                                            ALU.mult).then_inc(xn_r, 1)

                def rotate(w, b):
                    dve.wait_ge((p1_mm, p2_mm)[w], FIRST + 1 + b)
                    nc.vector.scalar_tensor_tensor((m1, m2)[w][:], both((4, 0)[w]), cvec[:, 1 + w:2 + w], (QSIN, QCOS)[w],
                                                   ALU.add, ALU.mult).then_inc(m_r, 1)

                def batch(b, more):
                    for i in range(NT):
                        normalise(i, b)
                        if i + 1 < NT:
                            rowmax(i + 1, b)
                        for k in SLOT.get(i, ()):
                            tail(0, k, b)
                        if i == 3 and more:
                            mean_square(b + 1)
                    tail(1, 0, b)
                    if more:
                        scale_tokens(b + 1)
                    for k in (2, 1, 3, 4):
                        tail(1, k, b)
                    if more:
                        rotate(0, b + 1)
                        rotate(1, b + 1)
                    tail(1, 6, b)
                    if more:
                        rowmax(0, b + 1)
                    tail(1, 7, b)

                mean_square(0)
                scale_tokens(0)
                rotate(0, 0)
                rotate(1, 0)
                rowmax(0, 0)
                with dve.Fori(0, B - 1) as b:
                    batch(b, True)
                batch(B - 1, False)

            @block.tensor
            def _(pe):
                def tail(c, k, b):
                    n = FIRST + c + b * NC
                    cs = slice(c * CH, (c + 1) * CH)
                    bank = ps[:, tail_bank(c, k), :]
                    m = k // 2
                    if k in (0, 2):
                        if m == 0:
                            pe.wait_ge(x_r, n)
                        elif c == 0:
                            pe.wait_ge(gt_r, FIRST + 1 + b * 4)
                        else:
                            pe.wait_ge(u_ev, FIRST + NC + b * NC)
                        nc.tensor.matmul(bank, wg[:, m * P:(m + 1) * P], XT[:, cs], start=True, stop=True).then_inc(g_mm, 1)
                    if k in (1, 3):
                        pe.wait_ge(gs_r, FIRST + (2 * c + m + 1) + b * 4)
                        pe.wait_ge(u_ev, n + 1)
                        nc.tensor.matmul(bank, wv[:, m * P:(m + 1) * P], UT[:, c, :], start=True, stop=True).then_inc(wv_mm, 1)
                    if k == 4:
                        pe.wait_ge(gt_r, FIRST + (2 * c + 2) + b * 4)
                        for m in range(VC):
                            last = nc.tensor.matmul(bank, woa[:, m, :], gated[:, m, :], start=(m == 0), stop=(m == VC - 1))
                        last.then_inc(res_mm, 1)
                    if k == 5:
                        pe.wait_ge(y_r, n + 1)
                        nc.tensor.matmul(bank, centre[:], yT[:], start=True, stop=True).then_inc(cen_mm, 1)
                    if k == 6:
                        pe.wait_ge(yc_r, FIRST + 2 * c + 2 + b * (2 * NC))
                        for s in range(TC):
                            last = nc.tensor.matmul(bank[:, s:s + 1], ysq[:, s * P:(s + 1) * P], mean1[:], start=True, stop=True)
                        last.then_inc(st_mm, 1)
                    if k == 7:
                        pe.wait_ge(rstd_r, n + 1)
                        for s in range(TC):
                            last = nc.tensor.transpose(bank[:, s * P:(s + 1) * P], yrs[:, s:s + 1].to_broadcast([P, P]), ident[:])
                        last.then_inc(bc_mm, 1)

                def scores(i, b):
                    if i >= 1:
                        pe.wait_ge(exp_r, FIRST + (i - 1) + b * NT)
                    if i == 1:
                        pe.wait_ge(xr_r, FIRST + 1 + b)
                    qs = slice(i * P, (i + 1) * P)
                    for c in range((i + TC) // TC):
                        n = min(CH, P * (i + 1) - c * CH)
                        o = ps[:, 2 * (i % 2) + c, 0:n]
                        nc.tensor.matmul(o, QA[:, qs], XT[:, c * CH:c * CH + n], start=True, stop=False)
                        diag = c == i // TC
                        last = nc.tensor.matmul(o, QB[:, qs], KEYF[:, c * CH:c * CH + n], start=False, stop=not diag)
                        if diag:
                            last = nc.tensor.matmul(o[:, n - P:n], identb[:], causalb[:], start=False, stop=True)
                    last.then_inc(s_mm, 1)

                def transpose_probs(i, b):
                    pe.wait_ge(p_r, FIRST + (i + 1) + b * NT)
                    for k, (ii, q) in enumerate(QUADS):
                        if ii == i:
                            if k >= 2:
                                pe.wait_ge(pt_ev, FIRST + (k - 1) + b * NQ)
                            for m in range(min(4, i + 1 - 4 * q)):
                                j = 4 * q + m
                                last = nc.tensor.transpose(ps[:, 4 + k % 2, m * P:(m + 1) * P],
                                                           prob[:, i % 2, j * P:(j + 1) * P], ident[:])
                            last.then_inc(pt_mm, 1)

                def mix(i, b):
                    pe.wait_ge(pt_ev, FIRST + quads_upto(i) + b * NQ)
                    if i in (0, TC):
                        pe.wait_ge(u_ev, FIRST + i // TC + b * NC)
                    for j in range(i + 1):
                        last = nc.tensor.matmul(ps[:, 6, (i % TC) * P:(i % TC + 1) * P], xn[:, j, :],
                                                probT[:, i % 2, j, :], start=(j == 0), stop=(j == i))
                    last.then_inc(pv_mm, 1)

                def transpose_tokens(src, bank, ready, done, b):
                    pe.wait_ge(*ready)
                    for t in range(NT):
                        last = nc.tensor.transpose(ps[:, bank + t // TC, (t % TC) * P:(t % TC + 1) * P], src[:, t, :], ident[:])
                    last.then_inc(done, 1)

                def queries(w, bank, done, b):
                    for c in range(NC):
                        last = nc.tensor.matmul(ps[:, bank + c, :], bmat[:, w, :], XT[:, c * CH:(c + 1) * CH],
                                                start=True, stop=True)
                    last.then_inc(done, 1)

                def head(k, b):
                    if k == 0:
                        pe.wait_ge(exp_r, FIRST + b * NT)
                        transpose_tokens(xn, 0, (xn_r, FIRST + 1 + b), xn_t, b)
                    if k == 1:
                        pe.wait_ge(xt_r, FIRST + 1 + b)
                        queries(0, 2, qa_mm, b)
                    if k == 2:
                        pe.wait_ge(pt_ev, FIRST + b * NQ)
                        queries(1, 4, p1_mm, b)
                    if k == 3:
                        queries(2, 0, p2_mm, b)
                    if k == 4:
                        pe.wait_ge(qa_r, FIRST + 1 + b)
                        transpose_tokens(xin, 2, (x_in, 16 + b * 16), raw_t, b)
                    if k == 5:
                        pe.wait_ge(qb_r, FIRST + 1 + b)
                        scores(0, b)

                def batch(b, more):
                    for i in range(NT):
                        if i + 1 < NT:
                            scores(i + 1, b)
                        if i == 0:
                            pe.wait_ge(m_r, FIRST + 1 + b * 2)
                        transpose_probs(i, b)
                        slot = SLOT.get(i, ())
                        for k in slot[:1]:
                            tail(0, k, b)
                        if i >= 1:
                            mix(i - 1, b)
                        for k in slot[1:]:
                            tail(0, k, b)
                    tail(1, 0, b)
                    mix(NT - 1, b)
                    tail(1, 2, b)
                    for heads, k in (((0,), 1), ((), 3), ((1,), 4), ((2,), 5), ((3,), 6), ((4, 5), 7)):
                        for h in heads:
                            if more:
                                head(h, b + 1)
                        tail(1, k, b)

                for k in range(6):
                    head(k, 0)
                with pe.Fori(0, B - 1) as b:
                    batch(b, True)
                batch(B - 1, False)
        sa.close()

        sf = ExitStack()
        sf.__enter__()
        ffn(nc, sem, counted, lambda name, shape, dt=F32: sb(name, shape, dt, sf), ps, XS, ident, identb, centre, mean1, mhalf, masksb, wqkv_main, wqkv_rest, wo, w1, w2, c1, b2,
            tcos, tsin, x_r)
        sf.close()
        finish(nc, sem, counted, sb, ps, XS, ident, mhalf, out)


def ffn(nc, sem, counted, sb, ps, XS, ident, identb, centre, mean1, mhalf, masksb, wqkv_main, wqkv_rest, wo, w1, w2, c1, b2,
        tcos, tsin, x_r):
    X1 = sb("X1", [P, B, T + 1])
    hT = sb("hT", [P, CH])
    hT_main = sb("hT_main", [P, 2, CH], F32R)
    hT_rest = sb("hT_rest", [P, 2, CH], F32R)
    sq = sb("sq", [P, 2, CH])
    ss16 = sb("ss16", [P, 2, 16])
    rn16 = sb("rn16", [P, 2, 16])
    work = sb("work", [P, 6, CH])
    rc = work[:, 0:2, :]
    rs = work[:, 2:4, :]
    qkr = work[:, 4:6, :]
    qkn = sb("qkn", [P, 2, 2, CH])
    VB = sb("VB", [P, 4, H, DH + 1])
    VA = sb("VA", [P, 4, H, DH + 1])
    qT = sb("qT", [P, H, P])
    kT = sb("kT", [P, 2, H // 2, 3, W])
    prb = sb("prb", [P, 2, H, P])
    mx = sb("mx", [P, 2, H])
    pT = sb("pT", [P, H, P])
    oinv = sb("oinv", [P, H])
    on = sb("on", [P, H, DH])
    oT = sb("oT", [P, INNER // P, P])
    h2 = sb("h2", [P, 2, CH])
    hc = sb("hc", [P, 2, CH])
    hsq = sb("hsq", [P, CH])
    hvar = sb("hvar", [P, TC])
    hrs = sb("hrs", [P, TC])
    hn = sb("hn", [P, 2, CH])
    gel = sb("gel", [P, 3, CH])
    hid = work[:].rearrange("p (a k) n -> p a k n", a=2)

    ini = sem("ffn_buffers_set")
    (hs_r, hm_r, h_r, qk_mm, v_mm, sq_r, v_r, ssr, ss_own, rn_r, rc_r, rs_r, add_r, qkn_r, tq_mm, tk_mm, qT_r, kT_r, s_mm,
     mx_r, sub_r, e_r, pt_mm, pt_r, pv_mm, oi_r, on_r, ot_mm, ot_r, wo_mm, x1_r) = (counted(n) for n in (
         "shifted_ready", "shifted_main_ready", "hT_ready", "qk_done", "v_done", "squares_ready", "V_ready", "sumsq_ready", "sumsq_own",
         "rnorm_ready", "cos_part_ready", "sin_part_ready", "rotated_ready", "qk_ready", "qT_done",
         "kT_done", "qT_ready", "kT_ready", "win_scores_done", "win_max_ready", "win_shift_ready", "win_exp_ready",
         "win_pT_done", "win_pT_ready", "win_pv_done", "win_inv_ready", "win_out_ready", "oT_done", "oT_ready",
         "wo_done", "X1_ready"))
    (h2_r, ce_mm, hc_r, sv_mm, hv_r, hr_r, hb_mm, hn_r, w1_mm, ge_r, hid_r, w2_mm) = (counted(n) for n in (
        "h2_ready", "h2_centred", "hc_ready", "hvar_done", "hvar_ready", "hrstd_ready", "hrstd_spread", "hn_ready",
        "w1_done", "gelu_ready", "hidden_ready", "w2_done"))
    BQ, BV, BT, BS, BP = 0, 2, 3, 5, 7

    def due(v):
        return not isinstance(v, int) or v > FIRST

    def tiles(t):
        return t // NT, t % NT

    def loops(eng, step, lead):
        for t in range(-lead, 0):
            step(0, t, NT)
        with eng.Fori(0, B - 1) as b:
            for t in range(NT):
                step(b, t, 2 * NT)
        for t in range(NT):
            step(B - 1, t, NT)

    for l in range(L):
        with nc.Block() as block:
            n0 = l * B * NT

            def cnt(b, t, per=1, k=0):
                return b * (NT * per) + (FIRST + (n0 + t) * per + k)

            def chunk(b, t, per=1, k=0):
                return b * (NC * per) + (FIRST + (l * B * NC + t // TC) * per + k)

            @block.gpsimd
            def _(pool):
                if l == 0:
                    nc.gpsimd.memset(VA[:, :, :, 0:DH], 0.0).then_inc(ini, 1)
                    nc.gpsimd.memset(VA[:, :, :, DH:DH + 1], 1.0).then_inc(ini, 1)
                    nc.gpsimd.memset(VB[:, :, :, DH:DH + 1], 1.0).then_inc(ini, 1)
                    nc.gpsimd.memset(kT[:], 0.0).then_inc(ini, 1)
                    nc.gpsimd.memset(qT[:], 0.0).then_inc(ini, 1)
                    nc.gpsimd.memset(X1[:, :, 0:1], 0.0).then_inc(ini, 1)
                    pool.wait_ge(ini, 6)

                def split(b, t):
                    c = t // TC % NC
                    pool.wait_ge(hm_r, chunk(b, t, 1, 1))
                    nc.gpsimd.tensor_tensor(hT_rest[:, c, :], hT[:], hT_main[:, c, :].bitcast(F32),
                                            ALU.subtract).then_inc(h_r, 1)

                def step(b, t, end):
                    if t == -4:
                        split(b, 0)
                    j = t + 5
                    if j % TC == 0 and j < end:
                        split(b, j)
                    j = t + 4
                    if j < end:
                        pool.wait_ge(rc_r, cnt(b, j, 1, 1))
                        pool.wait_ge(rs_r, cnt(b, j, 2, 2))
                        if due(cnt(b, j)):
                            pool.wait_ge(qkn_r, cnt(b, j))
                        nc.gpsimd.tensor_tensor(qkr, rc, rs, ALU.add).then_inc(add_r, 1)
                        pool.wait_ge(ssr, cnt(b, j, 1, 1))
                        nc.gpsimd.tensor_tensor(rn16[:, j % 2, :], ss16[:, j % 2, :], mhalf[:], ALU.pow).then_inc(rn_r, 1)

                loops(pool, step, 4)

            @block.scalar
            def _(act):
                if l == 0:
                    act.wait_ge(ini, 6)

                def shift(b, t):
                    db, tt = tiles(t)
                    c = tt // TC
                    g = b * NC + (FIRST + l * B * NC + db * NC + c)
                    act.wait_ge(x_r, g + 1)
                    if due(cnt(b, t - TC)):
                        act.wait_ge(qk_mm, cnt(b, t - TC))
                        act.wait_ge(v_mm, cnt(b, t - TC))
                    if due(chunk(b, t)):
                        act.wait_ge(h_r, chunk(b, t))
                    src = b + (l * B + db)
                    lo, up = (0, D // 2), (D // 2, D)
                    nc.scalar.activation(hT[lo[0]:lo[1]].unsqueeze(1),
                                         XS[lo[0]:lo[1], bass.ds(src, 1), 1 + c * CH:1 + (c + 1) * CH], ACT.Copy).then_inc(hs_r, 1)
                    nc.scalar.activation(hT[up[0]:up[1]].unsqueeze(1),
                                         XS[up[0]:up[1], bass.ds(src, 1), c * CH:(c + 1) * CH], ACT.Copy).then_inc(hs_r, 1)
                    act.wait_ge(hs_r, chunk(b, t, 2, 2))
                    nc.scalar.activation(hT_main[:, c, :], hT[:], ACT.Copy).then_inc(hm_r, 1)

                def keep_pT(b, j, f):
                    act.wait_ge(pt_mm, cnt(b, j, 2, f + 1))
                    nc.scalar.activation(pT[:, 4 * f:4 * f + 4, :], ps[:, BP, :].rearrange("p (h n) -> p h n", n=P),
                                         ACT.Copy).then_inc(pt_r, 1)

                def step(b, t, end):
                    if t == -4:
                        shift(b, 0)
                    j = t + 5
                    if j % TC == 0 and j < end:
                        shift(b, j)
                    j = t + 2
                    if 0 <= j < end:
                        act.wait_ge(tq_mm, cnt(b, j, 1, 1))
                        qp = ps[:, BT, :].rearrange("p (h n) -> p h n", n=P)
                        for f in range(2):
                            r = slice(DH * f, DH * f + DH)
                            nc.scalar.activation(qT[r, f:H:2, :], qp[r], ACT.Copy).then_inc(qT_r, 1)
                        act.wait_ge(tk_mm, cnt(b, j, 1, 1))
                        kp = ps[:, BT + 1, :].rearrange("p (h s n) -> p h s n", s=2, n=W)
                        nc.scalar.activation(kT[:, j % 2, :, 0:3:2, :], kp, ACT.Copy).then_inc(kT_r, 1)
                        nc.scalar.activation(kT[:, (j + 1) % 2, :, 1:2, :], kp[:, :, 1:2, :], ACT.Copy).then_inc(kT_r, 1)
                    j = t + 1
                    if 0 <= j < end:
                        keep_pT(b, j, 0)
                    j = t + 3
                    if 0 <= j < end:
                        act.wait_ge(v_mm, cnt(b, j, 1, 1))
                        if due(cnt(b, j - 2, 2)):
                            act.wait_ge(pv_mm, cnt(b, j - 2, 2))
                        v = ps[:, BV, :].rearrange("p (h d) -> p h d", h=H)
                        nc.scalar.activation(VB[:, j % 4, :, 0:DH], v, ACT.Copy).then_inc(v_r, 1)
                        nc.scalar.activation(VA[0:W, j % 4, :, 0:DH], v[0:W], ACT.Copy).then_inc(v_r, 1)
                        nc.scalar.activation(VA[W:P, (j + 1) % 4, :, 0:DH], v[W:P], ACT.Copy).then_inc(v_r, 1)
                    j = t + 4
                    if j < end:
                        act.wait_ge(rc_r, cnt(b, j, 1, 1))
                        act.wait_ge(rs_r, cnt(b, j, 2, 2))
                        if due(cnt(b, j)):
                            act.wait_ge(ssr, cnt(b, j))
                        nc.scalar.activation(sq[:], ps[:, BQ:BQ + 2, :], ACT.Square).then_inc(sq_r, 1)
                    j = t + 1
                    if 0 <= j < end:
                        keep_pT(b, j, 1)
                    for f in range(2):
                        if f == 1 and t >= 0:
                            act.wait_ge(ot_mm, cnt(b, t, 1, 1))
                            nc.scalar.activation(oT[:], ps[:, BP, :].rearrange("p (m n) -> p m n", n=P), ACT.Copy).then_inc(ot_r, 1)
                        j = t + 2
                        if 0 <= j < end:
                            act.wait_ge(sub_r, cnt(b, j, 2, f + 1))
                            p = prb[:, j % 2, 4 * f:4 * f + 4, :]
                            nc.scalar.activation(p, p, ACT.Exp).then_inc(e_r, 1)

                loops(act, step, 4)

            @block.vector
            def _(dve):
                if l == 0:
                    dve.wait_ge(ini, 6)

                def largest_off(b, j, f):
                    dve.wait_ge(s_mm, cnt(b, j, 2, f + 1))
                    s = ps[:, BS + f, :].rearrange("p (h n) -> p h n", n=P)
                    m = mx[:, f, 0:4]
                    nc.vector.tensor_reduce(m, s, AX.X, ALU.max).then_inc(mx_r, 1)
                    dve.wait_ge(mx_r, cnt(b, j, 2, f + 1))
                    nc.vector.tensor_tensor(prb[:, j % 2, 4 * f:4 * f + 4, :], s,
                                            m.unsqueeze(2).to_broadcast([P, 4, P]), ALU.subtract).then_inc(sub_r, 1)

                def step(b, t, end):
                    j = t + 3
                    if 0 <= j < end:
                        dve.wait_ge(add_r, cnt(b, j, 1, 1))
                        dve.wait_ge(rn_r, cnt(b, j, 1, 1))
                        nc.vector.tensor_tensor(qkn[:, j % 2].rearrange("p a (h d) -> p (a h) d", h=H),
                                                qkr.rearrange("p a (h d) -> p (a h) d", h=H),
                                                rn16[:, j % 2, :].unsqueeze(2).to_broadcast([P, 16, DH]),
                                                ALU.mult).then_inc(qkn_r, 1)
                    j = t + 4
                    if j < end:
                        tt = j % NT
                        qk = ps[:, BQ:BQ + 2, :].rearrange("p a (h d) -> p a h d", h=H)
                        dve.wait_ge(qk_mm, cnt(b, j, 1, 1))
                        if due(cnt(b, j)):
                            dve.wait_ge(add_r, cnt(b, j))
                        nc.vector.tensor_tensor(rc.rearrange("p a (h d) -> p a h d", h=H), qk,
                                                tcos[:, l, tt].unsqueeze(2).to_broadcast([P, 2, H, DH]),
                                                ALU.mult).then_inc(rc_r, 1)
                        ro = rs.rearrange("p a (h d) -> p a h d", h=H)
                        for f in range(2):
                            i0, o0 = f * HH, (1 - f) * HH
                            nc.vector.tensor_tensor(
                                ro[:, :, :, o0:o0 + HH], qk[:, :, :, i0:i0 + HH],
                                tsin[:, l, tt, :, i0:i0 + HH].unsqueeze(2).to_broadcast([P, 2, H, HH]),
                                ALU.mult).then_inc(rs_r, 1)
                    j = t + 2
                    if 0 <= j < end:
                        largest_off(b, j, 0)
                    j = t + 4
                    if j < end:
                        r = ss16[:, j % 2, :]
                        dve.wait_ge(sq_r, cnt(b, j, 1, 1))
                        nc.vector.tensor_reduce(r, sq[:].rearrange("p a (h d) -> p (a h) d", h=H), AX.X, ALU.add).then_inc(ss_own, 1)
                        dve.wait_ge(ss_own, cnt(b, j, 1, 1))
                        nc.vector.tensor_scalar(r, r, 1e-24, None, ALU.max).then_inc(ssr, 1)
                    j = t + 2
                    if 0 <= j < end:
                        largest_off(b, j, 1)
                    j = t + 1
                    if 0 <= j < end:
                        for f in range(2):
                            dve.wait_ge(pv_mm, cnt(b, j, 2, f + 1))
                            o = ps[:, BT + f, 0:4 * (DH + 1)].rearrange("p (h d) -> p h d", h=4)
                            r = oinv[:, 4 * f:4 * f + 4]
                            nc.vector.reciprocal(r.unsqueeze(2), o[:, :, DH:DH + 1]).then_inc(oi_r, 1)
                            dve.wait_ge(oi_r, cnt(b, j, 2, f + 1))
                            nc.vector.tensor_tensor(on[:, f:H:2, :], o[:, :, 0:DH],
                                                    r.unsqueeze(2).to_broadcast([P, 4, DH]), ALU.mult).then_inc(on_r, 1)
                    if t >= 0:
                        dve.wait_ge(wo_mm, cnt(b, t, 1, 1))
                        nc.vector.tensor_tensor(X1[:, bass.ds(b, 1), 1 + t * P:1 + (t + 1) * P],
                                                ps[:, BV:BV + 1, 0:P],
                                                XS[:, bass.ds(b + l * B, 1), 1 + t * P:1 + (t + 1) * P],
                                                ALU.add).then_inc(x1_r, 1)

                loops(dve, step, 4)

            @block.tensor
            def _(pe):
                if l == 0:
                    pe.wait_ge(ini, 6)

                def project(j, bank, m):
                    at_h = (j % NT) // TC, slice(j % TC * P, (j % TC + 1) * P)
                    main, rest = hT_main[:, at_h[0], at_h[1]], hT_rest[:, at_h[0], at_h[1]]
                    w = slice(m * INNER, (m + 1) * INNER)
                    nc.tensor.matmul(ps[:, bank, :], rest, wqkv_main[:, l, w], start=True, stop=False)
                    nc.tensor.matmul(ps[:, bank, :], main, wqkv_rest[:, l, w], start=False, stop=False)
                    return nc.tensor.matmul(ps[:, bank, :], main, wqkv_main[:, l, w], start=False, stop=True)

                def step(b, t, end):
                    j = t + 2
                    if 0 <= j < end:
                        pe.wait_ge(qkn_r, cnt(b, j, 1, 1))
                        for qk, done in ((0, tq_mm), (1, tk_mm)):
                            if due(cnt(b, j - 1, 2, qk - 1)):
                                pe.wait_ge(on_r, cnt(b, j - 1, 2, qk - 1))
                            for hp in range(H // 2):
                                last = nc.tensor.transpose(ps[:, BT + qk, hp * P:(hp + 1) * P],
                                                           qkn[:, j % 2, qk, hp * P:(hp + 1) * P], ident[:])
                            last.then_inc(done, 1)
                    j = t + 4
                    if j < end:
                        pe.wait_ge(h_r, chunk(b, j, 1, 1))
                        if due(cnt(b, j)):
                            pe.wait_ge(rc_r, cnt(b, j))
                        if due(cnt(b, j, 2)):
                            pe.wait_ge(rs_r, cnt(b, j, 2))
                        if due(cnt(b, j)):
                            pe.wait_ge(sq_r, cnt(b, j))
                        for m in range(2):
                            last = project(j, BQ + m, m)
                        last.then_inc(qk_mm, 1)
                    for f in range(2):
                        j = t + 1
                        if 0 <= j < end:
                            pe.wait_ge(e_r, cnt(b, j, 2, f + 1))
                            if due(cnt(b, j, 2, f)):
                                pe.wait_ge(pt_r, cnt(b, j, 2, f))
                            if due(cnt(b, t)):
                                pe.wait_ge(ot_r, cnt(b, t))
                            for h in range(4):
                                last = nc.tensor.transpose(ps[:, BP, h * P:(h + 1) * P], prb[:, j % 2, 4 * f + h, :], ident[:])
                            last.then_inc(pt_mm, 1)
                        j = t + 3
                        if f == 0 and 0 <= j < end:
                            if due(cnt(b, max(t, 0))):
                                pe.wait_ge(x1_r, cnt(b, max(t, 0)))
                            if due(cnt(b, j, 3)):
                                pe.wait_ge(v_r, cnt(b, j, 3))
                            project(j, BV, 2).then_inc(v_mm, 1)
                        j = t + 2
                        if 0 <= j < end:
                            if f == 0:
                                pe.wait_ge(qT_r, cnt(b, j, 2, 2))
                                pe.wait_ge(kT_r, cnt(b, j, 2, 2))
                            if due(cnt(b, j - 1, 2, f + 1)):
                                pe.wait_ge(sub_r, cnt(b, j - 1, 2, f + 1))
                            nc.tensor.matmul(ps[:, BS + f, :], identb[:], masksb[:, 0 if j % NT == 0 else 1, :],
                                             start=True, stop=False, skip_group_check=True)
                            for h in range(4):
                                for w in range(2):
                                    keys = kT[:, j % 2, h, 0:2, :] if w == 0 else kT[:, j % 2, h, 0:3:2, :]
                                    last = nc.tensor.matmul(ps[w * W:(w + 1) * W, BS + f, h * P:(h + 1) * P],
                                                            qT[:, 2 * h + f, w * W:(w + 1) * W], keys,
                                                            start=False, stop=(h == 3), skip_group_check=True)
                            last.then_inc(s_mm, 1)
                    if t >= 0:
                        pe.wait_ge(on_r, cnt(b, t, 2, 2))
                        if due(cnt(b, min(t + 2, end), 2)):
                            pe.wait_ge(pt_r, cnt(b, min(t + 2, end), 2))
                        for m in range(INNER // P):
                            last = nc.tensor.transpose(ps[:, BP, m * P:(m + 1) * P], on[:, 2 * m:2 * m + 2, :].rearrange("p h d -> p (h d)"), ident[:])
                        last.then_inc(ot_mm, 1)
                    j = t + 1
                    if 0 <= j < end:
                        pe.wait_ge(v_r, cnt(b, j, 3, 3))
                        for f in range(2):
                            pe.wait_ge(pt_r, cnt(b, j, 2, f + 1))
                            if f == 0:
                                if due(cnt(b, min(j + 2, end), 2)):
                                    pe.wait_ge(qT_r, cnt(b, min(j + 2, end), 2))
                            else:
                                if due(cnt(b, min(j + 2, end), 2)):
                                    pe.wait_ge(kT_r, cnt(b, min(j + 2, end), 2))
                            for h in range(4):
                                for w, val in ((0, VA), (1, VB)):
                                    last = nc.tensor.matmul(ps[w * W:(w + 1) * W, BT + f, h * (DH + 1):(h + 1) * (DH + 1)],
                                                            pT[:, 4 * f + h, w * W:(w + 1) * W], val[:, j % 4, 2 * h + f, :],
                                                            start=True, stop=True)
                            last.then_inc(pv_mm, 1)
                    if t >= 0:
                        pe.wait_ge(ot_r, cnt(b, t, 1, 1))
                        if due(cnt(b, min(t + 4, end), 3)):
                            pe.wait_ge(v_r, cnt(b, min(t + 4, end), 3))
                        if due(cnt(b, t)):
                            pe.wait_ge(x1_r, cnt(b, t))
                        for m in range(INNER // P):
                            last = nc.tensor.matmul(ps[:, BV, 0:P], wo[:, l, m, :], oT[:, m, :],
                                                    start=(m == 0), stop=(m == INNER // P - 1))
                        last.then_inc(wo_mm, 1)

                loops(pe, step, 4)

        with nc.Block() as block:
            g0 = l * B * NC
            BC, BW2 = 6, 7

            def at(b, c, per=1, k=0):
                return b * (NC * per) + (FIRST + (g0 + c) * per + k)

            def rounds(eng, step, lead):
                for c in range(-lead, 0):
                    step(0, c, NC)
                with eng.Fori(0, B - 1) as b:
                    for c in range(NC):
                        step(b, c, 2 * NC)
                for c in range(NC):
                    step(B - 1, c, NC)

            @block.gpsimd
            def _(pool):
                def step(b, c, end):
                    j = c + 2
                    if j < end:
                        pool.wait_ge(hv_r, at(b, j, 1, 1))
                        nc.gpsimd.tensor_tensor(hrs[:], hvar[:], mhalf[:, 0:TC], ALU.pow).then_inc(hr_r, 1)

                rounds(pool, step, 2)

            @block.scalar
            def _(act):
                def step(b, c, end):
                    j = c + 2
                    if j < end:
                        r = j % NC
                        x = bass.ds(b + j // NC, 1)
                        act.wait_ge(x1_r, b * NT + (FIRST + l * B * NT + (j + 1) * TC))
                        if due(at(b, j - 1)):
                            act.wait_ge(ce_mm, at(b, j - 1))
                        nc.scalar.activation(h2[0:D // 2, r:r + 1, :], X1[0:D // 2, x, 1 + r * CH:1 + (r + 1) * CH],
                                             ACT.Copy).then_inc(h2_r, 1)
                        nc.scalar.activation(h2[D // 2:D, r:r + 1, :], X1[D // 2:D, x, r * CH:(r + 1) * CH],
                                             ACT.Copy).then_inc(h2_r, 1)
                        act.wait_ge(ce_mm, at(b, j, 1, 1))
                        if due(at(b, j - 1)):
                            act.wait_ge(hn_r, at(b, j - 1))
                        nc.scalar.activation(hc[:, j % 2, :], ps[:, BC, :], ACT.Copy).then_inc(hc_r, 1)
                        nc.scalar.activation(hsq[:], ps[:, BC, :], ACT.Square).then_inc(hc_r, 1)
                    j = c + 1
                    if 0 <= j < end:
                        for k, (o, m) in enumerate(HCH):
                            act.wait_ge(w1_mm, at(b, j, 3, k + 1))
                            if due(at(b, j, 3, k - 2)):
                                act.wait_ge(hid_r, at(b, j, 3, k - 2))
                            nc.scalar.activation(gel[0:m, k, :], ps[0:m, 2 * k + 1, :], ACT.Gelu,
                                                 bias=c1[0:m, l, 3 + k:4 + k]).then_inc(ge_r, 1)

                rounds(act, step, 2)

            @block.vector
            def _(dve):
                def step(b, c, end):
                    for k, (o, m) in enumerate(HCH):
                        j = c + 2
                        if j < end and k == 1:
                            dve.wait_ge(sv_mm, at(b, j, 1, 1))
                            nc.vector.tensor_scalar(hvar[:], ps[:, BW2, 0:TC], 1e-5, None, ALU.add).then_inc(hv_r, 1)
                        if c >= 0 and k == 1:
                            dve.wait_ge(w2_mm, at(b, c, 1, 1))
                            nc.vector.scalar_tensor_tensor(
                                XS[:, bass.ds(b + B, 1), 1 + c * CH:1 + (c + 1) * CH], ps[:, BW2:BW2 + 1, :],
                                b2[:, l:l + 1], X1[:, bass.ds(b, 1), 1 + c * CH:1 + (c + 1) * CH],
                                ALU.add, ALU.add).then_inc(x_r, 1)
                        if j < end and k == 2:
                            dve.wait_ge(hb_mm, at(b, j, 1, 1))
                            dve.wait_ge(hc_r, at(b, j, 2, 1))
                            nc.vector.tensor_tensor(hn[:, j % 2, :], ps[:, BC, :], hc[:, j % 2, :], ALU.mult).then_inc(hn_r, 1)
                        j = c + 1
                        if 0 <= j < end:
                            dve.wait_ge(ge_r, at(b, j, 3, k + 1))
                            nc.vector.scalar_tensor_tensor(hid[0:m, j % 2, k, :], ps[0:m, 2 * k, :], c1[0:m, l, k:k + 1],
                                                           gel[0:m, k, :], ALU.add, ALU.mult).then_inc(hid_r, 1)

                rounds(dve, step, 2)

            @block.tensor
            def _(pe):
                def step(b, c, end):
                    j = c + 2
                    if j < end:
                        pe.wait_ge(h2_r, at(b, j, 2, 2))
                        if due(at(b, j)):
                            pe.wait_ge(hn_r, at(b, j))
                        nc.tensor.matmul(ps[:, BC, :], centre[:], h2[:, j % NC, :], start=True, stop=True).then_inc(ce_mm, 1)
                    for k, (o, m) in enumerate(HCH):
                        j = c + 2
                        if j < end and k == 1:
                            pe.wait_ge(hc_r, at(b, j, 2, 2))
                            if due(at(b, c) + B * NC):
                                pe.wait_ge(x_r, at(b, c) + B * NC)
                            for s in range(TC):
                                last = nc.tensor.matmul(ps[:, BW2, s:s + 1], hsq[:, s * P:(s + 1) * P], mean1[:],
                                                        start=True, stop=True)
                            last.then_inc(sv_mm, 1)
                        if c >= 0 and k == 1:
                            pe.wait_ge(hid_r, at(b, c, 3, 3))
                            if due(at(b, min(c + 3, end))):
                                pe.wait_ge(hv_r, at(b, min(c + 3, end)))
                            for kk, (oo, mm) in enumerate(HCH):
                                last = nc.tensor.matmul(ps[:, BW2, :], w2[0:mm, l, kk, :], hid[0:mm, c % 2, kk, :],
                                                        start=(kk == 0), stop=(kk == 2))
                            last.then_inc(w2_mm, 1)
                        if j < end and k == 2:
                            pe.wait_ge(hr_r, at(b, j, 1, 1))
                            for s in range(TC):
                                last = nc.tensor.transpose(ps[:, BC, s * P:(s + 1) * P], hrs[:, s:s + 1].to_broadcast([P, P]), ident[:])
                            last.then_inc(hb_mm, 1)
                        j = c + 1
                        if 0 <= j < end:
                            pe.wait_ge(hn_r, at(b, j, 1, 1))
                            if due(at(b, j, 3, k - 2)):
                                pe.wait_ge(hid_r, at(b, j, 3, k - 2))
                            for half in range(2):
                                last = nc.tensor.matmul(ps[0:m, 2 * k + half, :], w1[:, l, half * HID + o:half * HID + o + m],
                                                        hn[:, j % 2, :], start=True, stop=True)
                            last.then_inc(w1_mm, 1)

                rounds(pe, step, 2)


def finish(nc, sem, counted, sb, ps, XS, ident, mhalf, out):
    NG = B * NC
    ys = sb("ys", [P, 2, CH])
    mu = sb("mu", [P, NG, TC])
    zc = sb("zc", [P, NG, TC, D])
    zs = sb("zs", [P, 2, TC, D])
    zv = sb("zv", [P, NG, TC])
    zr = sb("zr", [P, NG, TC])
    zo = sb("zo", [P, 2, TC, D])
    (s_y, s_t, s_m, s_m2, s_c, s_q, s_v, s_v2, s_r, s_o) = (counted(n) for n in (
        "sum_ready", "sum_transposed", "total_ready", "mean_ready", "centred_ready", "zsquares_ready", "zsum_ready",
        "zvar_ready", "zrstd_ready", "result_ready"))
    s_out = [sem(f"result_stored_{c}") for c in range(NC)]
    out_v = out.rearrange("b (t p) d -> p b t d", p=P)
    F2 = FIRST + 1
    with nc.Block() as block:
        @block.sync
        def _(sp):
            with sp.Fori(0, B) as b:
                for c in range(NC):
                    sp.wait_ge(s_o, F2 + c + b * NC)
                    sp.dma_start(out_v[:, bass.ds(b, 1), c * TC:(c + 1) * TC, :], zo[:, c:c + 1]).then_inc(s_out[c], 16)
            for c in range(NC):
                sp.wait_ge(s_out[c], 16 * B)

        @block.gpsimd
        def _(pool):
            def add(g):
                b, c = g // NC, g % NC
                if g >= 2:
                    pool.wait_ge(s_t, FIRST + g - 1)
                nc.gpsimd.tensor_tensor(ys[:, c:c + 1, :], XS[:, b:b + 1, 1 + c * CH:1 + (c + 1) * CH],
                                        XS[:, B + b:B + b + 1, 1 + c * CH:1 + (c + 1) * CH], ALU.add).then_inc(s_y, 1)

            def root(g, n):
                pool.wait_ge(s_v2, FIRST + g + n)
                nc.gpsimd.tensor_tensor(zr[:, g:g + n, :], zv[:, g:g + n, :],
                                        mhalf[:, 0:n * TC].rearrange("p (g t) -> p g t", g=n), ALU.pow).then_inc(s_r, 1)

            for g in range(NG):
                add(g)
                if g % 2 == 1 and g >= 3:
                    root(g - 3, 2)
            root(NG - 2, 2)

        @block.tensor
        def _(pe):
            for g in range(NG):
                c = g % 2
                pe.wait_ge(s_y, F2 + g)
                if g >= 2:
                    pe.wait_ge(s_c, FIRST + g - 1)
                for s in range(TC):
                    last = nc.tensor.transpose(ps[:, c, s * P:(s + 1) * P], ys[:, c, s * P:(s + 1) * P], ident[:])
                last.then_inc(s_t, 1)

        @block.scalar
        def _(act):
            for g in range(NG):
                act.wait_ge(s_c, F2 + g)
                if g >= 2:
                    act.wait_ge(s_v, FIRST + g - 1)
                nc.scalar.activation(zs[:, g % 2], zc[:, g], ACT.Square).then_inc(s_q, 1)

        @block.vector
        def _(dve):
            def centre_rows(g):
                z = ps[:, g % 2, :].rearrange("p (t d) -> p t d", d=D)
                dve.wait_ge(s_t, F2 + g)
                nc.vector.tensor_reduce(mu[:, g, :], z, AX.X, ALU.add).then_inc(s_m, 1)
                dve.wait_ge(s_m, F2 + g)
                nc.vector.tensor_scalar(mu[:, g, :], mu[:, g, :], 1.0 / D, None, ALU.mult).then_inc(s_m2, 1)
                dve.wait_ge(s_m2, F2 + g)
                nc.vector.tensor_tensor(zc[:, g], z, mu[:, g, :].unsqueeze(2).to_broadcast([P, TC, D]),
                                        ALU.subtract).then_inc(s_c, 1)

            def variance(g):
                dve.wait_ge(s_q, F2 + g)
                nc.vector.tensor_reduce(zv[:, g, :], zs[:, g % 2], AX.X, ALU.add).then_inc(s_v, 1)
                dve.wait_ge(s_v, F2 + g)
                nc.vector.tensor_scalar(zv[:, g, :], zv[:, g, :], 1.0 / D, 1e-5, ALU.mult, ALU.add).then_inc(s_v2, 1)

            def scale(g):
                dve.wait_ge(s_r, F2 + g // 2)
                if g >= 2:
                    dve.wait_ge(s_out[g % 2], 16 * (g // 2))
                nc.vector.tensor_tensor(zo[:, g % 2], zc[:, g], zr[:, g, :].unsqueeze(2).to_broadcast([P, TC, D]),
                                        ALU.mult).then_inc(s_o, 1)

            for g in range(NG + 4):
                if g < NG:
                    centre_rows(g)
                if 1 <= g <= NG:
                    variance(g - 1)
                if g >= 4:
                    scale(g - 4)


def kernel(**inputs):
    import numpy as _np
    import concourse.bacc as _bacc
    from concourse import mybir as _mybir
    from concourse.bass_utils import run_bass_kernel_spmd as _run

    nc = _bacc.Bacc("TRN2", target_bir_lowering=False, num_devices=1)
    arrays, aps = {}, {}
    for name, value in {**inputs, **constants()}.items():
        arr = _np.ascontiguousarray(value)
        arrays[f"in_{name}"] = arr
        aps[name] = nc.dram_tensor(f"in_{name}", arr.shape, _mybir.dt.from_np(arr.dtype), kind="ExternalInput").ap()
    out = nc.dram_tensor("out", (B, T, D), _mybir.dt.float32, kind="ExternalOutput").ap()
    build(nc, aps, out)
    r = _run(nc, [arrays], core_ids=[0])
    return r.results[0]["out"]
```

```python
from contextlib import ExitStack

import numpy as np
import concourse.bass as bass
from concourse import mybir

F32 = mybir.dt.float32
F32R = mybir.dt.float32r
BF16 = mybir.dt.bfloat16
ALU = mybir.AluOpType
ACT = mybir.ActivationFunctionType
AX = mybir.AxisListType

P = 128
B, T, D = 4, 1024, 128
NT = T // P
CH = 512
NC = T // CH
TC = CH // P
V = 256
VC = V // P
L = 2
H, DH = 8, 64
HH = DH // 2
INNER = H * DH
W = 64
HID = int(D * 4 * 2 / 3)
HCH = [(0, 128), (128, 128), (256, HID - 256)]
FIRST = 1
TAU = float(np.float32(D) ** np.float32(0.5))
MASKED = -1e30
QUADS = [(i, q) for i in range(NT) for q in range((i + 4) // 4)]

LOOP_SEMAPHORES = (
    "x_squares", "meansq_ready", "x_scale_ready", "xn_ready", "x_transposed", "xn_transposed", "XR_ready",
    "XT_ready", "qa_done", "p1_done", "p2_done", "QA_ready", "m1m2_ready", "QB_ready", "scores_done",
    "max_ready", "exp_ready", "pinv_ready", "probs_ready", "pT_done", "probT_ready", "pv_done", "UT_ready",
    "gate_done", "gate_tanh_ready", "gate_ready", "wv_done", "gated_ready", "res_done", "y_ready",
    "centred_done", "yc_ready", "var_done", "var_ready", "rstd_ready", "rstd_spread", "X_ready", "hT_ready",
    "qk_done", "v_done", "squares_ready", "V_ready", "sumsq_ready", "sumsq_own", "rnorm_ready",
    "shifted_ready", "shifted_main_ready", "cos_part_ready", "sin_part_ready", "rotated_ready", "qk_ready", "qT_done", "kT_done", "qT_ready",
    "kT_ready", "win_scores_done", "win_max_ready", "win_shift_ready", "win_exp_ready", "win_pT_done",
    "win_pT_ready", "win_pv_done", "win_inv_ready", "win_out_ready", "oT_done", "oT_ready", "wo_done",
    "X1_ready", "h2_ready", "h2_centred", "hc_ready", "hvar_done", "hvar_ready", "hrstd_ready",
    "hrstd_spread", "hn_ready", "hn_main_ready", "hn_rest_ready", "w1_done", "gelu_ready", "hidden_ready", "hidden_main_ready",
    "hidden_rest_ready", "w2_done", "sum_ready",
    "sum_transposed", "total_ready", "mean_ready", "centred_ready", "zsquares_ready", "zsum_ready",
    "zvar_ready", "zrstd_ready", "result_ready",
)


def constants():
    f = np.float32
    pos = np.arange(T, dtype=np.float64)
    w = 1.0 / 10000.0 ** (np.arange(0, D, 2) / D)
    ang = w[:, None] * pos[None, :]
    key = np.concatenate([np.cos(ang), np.sin(ang)], 0)
    qsin = np.concatenate([np.sin(ang), np.sin(ang)], 0)
    qcos = np.concatenate([np.cos(ang), np.cos(ang)], 0)
    rel = np.stack([key, qsin, qcos], 1).astype(f)
    half = np.arange(0, DH, 2) / 1.0
    inv = 1.0 / 10000.0 ** (half / DH)
    fr = pos[:, None] * inv[None, :]
    base = (half + 0.4 * DH) / (1.4 * DH)
    sc = base[None, :] ** ((pos - T // 2) / float(W // 2))[:, None]
    two = lambda a, b: np.concatenate([a, b], 1)
    cos, sin = np.cos(fr), np.sin(fr)
    tabs = [two(cos * sc, cos * sc) * 8.0, two(sin * sc, -sin * sc) * 8.0,
            two(cos / sc, cos / sc), two(sin / sc, -sin / sc)]
    rot = np.stack(tabs, 1).reshape(NT, P, 4, DH).transpose(1, 0, 2, 3).astype(f)
    ident = np.eye(P, dtype=f)
    centre = (np.eye(P) - 1.0 / P).astype(f)
    i, j = np.arange(P)[:, None], np.arange(P)[None, :]
    causal = np.where(j <= i, 0.0, MASKED).astype(f)
    wi, c = i % W, j % W
    own, before = c <= wi, c >= wi
    first = np.where(j < W, own, before)
    second = np.where(j < W, before, own)
    m = np.where(i < W, first, second)
    m0 = np.where((i < W) & (j >= W), False, m)
    masks = [np.where(a, 0.0, MASKED) for a in (m0, m)]
    masks = np.stack([np.tile(a, (1, 4)) for a in masks], 1).astype(f)
    return {"c_rel": rel, "c_rot": np.ascontiguousarray(rot), "c_ident": ident, "c_centre": centre,
            "c_causal": causal, "c_masks": masks}


def build(nc, a, out):
    ctx = ExitStack()
    with ctx:
        def sem(name):
            return ctx.enter_context(nc.semaphore(name))

        loop_semaphores = {name: sem(name) for name in LOOP_SEMAPHORES}
        counted = loop_semaphores.get

        def sb(name, shape, dt=F32, stack=None):
            return (stack or ctx).enter_context(nc.sbuf_tensor(name, shape, dt))

        ps = ctx.enter_context(nc.psum_tensor("ps", [P, 8, CH], F32))

        XS = sb("XS", [P, 2 * B, T + 1])
        ident = sb("ident", [P, P])
        identb = sb("identb", [P, P], BF16)
        centre = sb("centre", [P, P])
        mean1 = sb("mean1", [P, 1])
        mhalf = sb("mhalf", [P, 16])
        causalb = sb("causalb", [P, P], BF16)
        masksb = sb("masksb", [P, 2, CH], BF16)
        wqkv_main = sb("wqkv_main", [P, L, 3 * INNER], F32R)
        wqkv_rest = sb("wqkv_rest", [P, L, 3 * INNER], F32R)
        wo = sb("wo", [P, L, INNER // P, D])
        w1_main = sb("w1_main", [P, L, 2 * HID], F32R)
        w1_rest = sb("w1_rest", [P, L, 2 * HID], F32R)
        w2_main = sb("w2_main", [P, L, 3, D], F32R)
        w2_rest = sb("w2_rest", [P, L, 3, D], F32R)
        c1 = sb("c1", [P, L, 6])
        b2 = sb("b2", [P, L])
        tcos = sb("tcos", [P, L, NT, 2, DH])
        tsin = sb("tsin", [P, L, NT, 2, DH])

        sa = ExitStack()
        sa.__enter__()
        wqkv = sb("wqkv", [P, 3 * INNER], stack=sa)
        w1 = sb("w1", [P, L, 2 * HID], stack=sa)
        w2 = sb("w2", [P, L, 3, D], stack=sa)
        rel = sb("rel", [P, 3, T], stack=sa)
        KEYF, QSIN, QCOS = rel[:, 0, :], rel[:, 1, :], rel[:, 2, :]
        bmat = sb("bmat", [P, 3, P], stack=sa)
        cvec = sb("cvec", [P, 3], stack=sa)
        wv = sb("wv", [P, V], stack=sa)
        wg = sb("wg", [P, V], stack=sa)
        woa = sb("woa", [P, VC, D], stack=sa)

        raw = sb("raw", [P, 3, P], stack=sa)
        wT = sb("wT", [P, 4, P], stack=sa)
        vecs = sb("vecs", [P, 3], stack=sa)
        rot = sb("rot", [P, NT, 4, DH], stack=sa)
        qks = sb("qks", [P, L, 2, DH], stack=sa)
        lnv = sb("lnv", [P, L, 2], stack=sa)
        b1c = sb("b1c", [P, L, 6], stack=sa)
        causalf = sb("causalf", [P, P], stack=sa)
        xin = sb("xin", [P, NT, D], stack=sa)
        xn = sb("xn", [P, NT, D], stack=sa)
        xms = sb("xms", [P, 2, NT], stack=sa)
        xrs = sb("xrs", [P, NT], stack=sa)
        XR = sb("XR", [P, T], stack=sa)
        XT = sb("XT", [P, T], stack=sa)
        QA = sb("QA", [P, T], stack=sa)
        QB = sb("QB", [P, T], stack=sa)
        m1 = QB
        m2 = sb("m2", [P, T], stack=sa)
        xsq = m2[:].rearrange("p (t d) -> p t d", d=D)
        prob = sb("prob", [P, 2, T], stack=sa)
        nmax = sb("nmax", [P, 2], stack=sa)
        psumr = sb("psumr", [P, 2], stack=sa)
        pinv = sb("pinv", [P, 2], stack=sa)
        probT = sb("probT", [P, 2, NT, P], stack=sa)
        UT = sb("UT", [P, NC, CH], stack=sa)
        gth = sb("gth", [P, VC, CH], stack=sa)
        gsb = sb("gsb", [P, VC, CH], stack=sa)
        gated = sb("gated", [P, VC, CH], stack=sa)
        yT = sb("yT", [P, CH], stack=sa)
        yc = sb("yc", [P, CH], stack=sa)
        ysq = sb("ysq", [P, CH], stack=sa)
        yvar = sb("yvar", [P, TC], stack=sa)
        yrs = sb("yrs", [P, TC], stack=sa)
        masksf = gth

        (s_maps, s_load, s_load2, s_rest, s_fold, s_masks, s_wt, s_wte, s_wp, s_bm, s_c1, s_w1, w_split, q_split,
         x_in, s_dve, s_init) = (
            sem(n) for n in ("maps_loaded", "weights_loaded", "second_branch_loaded", "second_wqkv_loaded", "maps_folded",
                             "masks_ready", "transposes_done", "transposes_kept", "products_done", "maps_ready",
                             "bias_products_done", "hidden_bias_ready", "weights_split", "first_wqkv_split", "x_loaded",
                             "setup_own", "setup_done"))
        x_dram = a["L0_attn_x"].rearrange("b (t p) d -> p b t d", p=P)
        col = lambda v: v.rearrange("(p o) -> p o", o=1)
        map_loads = [
            (raw[:, 0, :], a["L0_attn_W_q"]), (vecs[:, 0:1], col(a["L0_attn_g_ln"])), (raw[:, 1, :], a["L0_attn_W_k"]),
            (raw[:, 2, :], a["L0_attn_W_r"]), (ident[:], a["c_ident"]), (vecs[:, 1:2], col(a["L0_attn_xl_u"])),
            (vecs[:, 2:3], col(a["L0_attn_xl_v"])),
        ]
        first_loads = [
            (causalf[:], a["c_causal"]), (rel[:], a["c_rel"]),
            (wv[:], a["L0_attn_W_v"]), (wg[:], a["L0_attn_W_g"]),
            (woa[:], a["L0_attn_W_o"].rearrange("(m p) n -> p m n", p=P)),
            (centre[:], a["c_centre"]), (masksf[:], a["c_masks"]),
        ]
        later_loads = [(rot[:], a["c_rot"]), (wqkv[:], a["L0_ffn_wqkv"][0])]
        for l in range(L):
            later_loads += [
                (wo[:, l], a["L0_ffn_wo"][l].rearrange("(m p) n -> p m n", p=P)),
                (w1[:, l, :], a["L0_ffn_w1"][l]),
                (b2[:, l:l + 1], col(a["L0_ffn_b2"][l])),
                (lnv[:, l, 0:1], col(a["L0_ffn_ln_g"][l])), (lnv[:, l, 1:2], col(a["L0_ffn_ln_b"][l])),
                (qks[:, l, 0, :], a["L0_ffn_q_scale"][l].partition_broadcast(P)),
                (qks[:, l, 1, :], a["L0_ffn_k_scale"][l].partition_broadcast(P)),
            ]
            for c, (o, m) in enumerate(HCH):
                later_loads += [
                    (w2[0:m, l, c, :], a["L0_ffn_w2"][l][o:o + m, :]),
                    (b1c[0:m, l, c:c + 1], col(a["L0_ffn_b1"][l][o:o + m])),
                    (b1c[0:m, l, 3 + c:4 + c], col(a["L0_ffn_b1"][l][HID + o:HID + o + m])),
                ]

        with nc.Block() as block:
            @block.sync
            def _(sp):
                for dst, src in map_loads:
                    sp.dma_start(dst, src).then_inc(s_maps, 16)
                for s in loop_semaphores.values():
                    sp.sem_inc(s, FIRST)

            @block.scalar
            def _(act):
                act.dma_start(xin[:].unsqueeze(1), x_dram[:, 0:1]).then_inc(x_in, 16)
                for dst, src in first_loads:
                    act.dma_start(dst, src).then_inc(s_load, 16)

            @block.gpsimd
            def _(pool):
                nc.gpsimd.memset(XS[:, :, 0:1], 0.0).then_inc(s_init, 1)
                nc.gpsimd.memset(mhalf[:], -0.5).then_inc(s_init, 1)
                nc.gpsimd.memset(mean1[:], 1.0 / P).then_inc(s_init, 1)
                pool.wait_ge(s_init, 3)

        (xsq_d, ms_r, rx_r, xn_r, raw_t, xn_t, xr_r, xt_r, qa_mm, p1_mm, p2_mm, qa_r, m_r, qb_r, s_mm,
         max_r, exp_r, inv_r, p_r, pt_mm, pt_ev, pv_mm, u_ev, g_mm, gth_r, gs_r, wv_mm, gt_r, res_mm, y_r,
         cen_mm, yc_r, st_mm, var_r, rstd_r, bc_mm, x_r) = (counted(n) for n in (
             "x_squares", "meansq_ready", "x_scale_ready", "xn_ready", "x_transposed", "xn_transposed",
             "XR_ready", "XT_ready", "qa_done", "p1_done", "p2_done", "QA_ready", "m1m2_ready", "QB_ready",
             "scores_done", "max_ready", "exp_ready", "pinv_ready", "probs_ready", "pT_done", "probT_ready",
             "pv_done", "UT_ready", "gate_done", "gate_tanh_ready", "gate_ready", "wv_done",
             "gated_ready", "res_done", "y_ready", "centred_done", "yc_ready", "var_done", "var_ready",
             "rstd_ready", "rstd_spread", "X_ready"))
        SLOT = {4: (0, 1), 5: (2, 3), 6: (4, 5), 7: (6, 7)}
        NQ = len(QUADS)

        def both(bank):
            return ps[:, bank:bank + 2, :].rearrange("p a n -> p (a n)")

        def tail_bank(c, k):
            return 6 if c == 1 and k in (2, 3) else 7

        def quads_upto(i):
            return sum(1 for (ii, _) in QUADS if ii <= i)

        with nc.Block() as block:
            @block.sync
            def _(sp):
                for dst, src in later_loads:
                    sp.dma_start(dst, src).then_inc(s_load2, 16)

                def load_tokens(b):
                    sp.wait_ge(raw_t, FIRST + b)
                    sp.wait_ge(xn_r, FIRST + b)
                    sp.dma_start(xin[:].unsqueeze(1), x_dram[:, bass.ds(b, 1)]).then_inc(x_in, 16)

                load_tokens(1)
                sp.wait_ge(q_split, 1)
                sp.dma_start(wqkv[:], a["L0_ffn_wqkv"][1]).then_inc(s_rest, 16)
                with sp.Fori(2, B) as b:
                    load_tokens(b)

            @block.gpsimd
            def _(pool):
                def token_scale(b):
                    pool.wait_ge(ms_r, FIRST + 1 + b)
                    nc.gpsimd.tensor_tensor(xrs[:], xms[:, 1, :], mhalf[:, 0:NT], ALU.pow).then_inc(rx_r, 1)

                def position_queries(b):
                    pool.wait_ge(m_r, FIRST + 2 + b * 2)
                    nc.gpsimd.tensor_tensor(QB[:], m1[:], m2[:], ALU.add).then_inc(qb_r, 1)

                def rstd(c, b):
                    pool.wait_ge(var_r, FIRST + 1 + c + b * NC)
                    nc.gpsimd.tensor_tensor(yrs[:], yvar[:], mhalf[:, 0:TC], ALU.pow).then_inc(rstd_r, 1)

                def batch(b, more):
                    if more:
                        token_scale(b + 1)
                    rstd(0, b)
                    if more:
                        position_queries(b + 1)
                    rstd(1, b)

                def prepare(l):
                    for qk in range(2):
                        for tab, out_t in ((0, tcos), (1, tsin)):
                            nc.gpsimd.tensor_tensor(out_t[:, l, :, qk, :], rot[:, :, 2 * qk + tab, :],
                                                    qks[:, l, qk:qk + 1, :].to_broadcast([P, NT, DH]), ALU.mult)
                    nc.gpsimd.tensor_tensor(w1[:, l, :], w1[:, l, :], lnv[:, l, 0:1].to_broadcast([P, 2 * HID]),
                                            ALU.mult).then_inc(s_w1, 1)
                    pool.wait_ge(s_w1, l + 1)
                    parts = [(wqkv[:], wqkv_main[:, l, :], wqkv_rest[:, l, :]), (w1[:, l, :], w1_main[:, l, :], w1_rest[:, l, :]),
                             (w2[:, l, 0:2, :], w2_main[:, l, 0:2, :], w2_rest[:, l, 0:2, :])]
                    for n, (whole, main, rest) in enumerate(parts):
                        nc.gpsimd.tensor_copy(main, whole).then_inc(w_split, 1)
                        pool.wait_ge(w_split, len(parts) * l + n + 1)
                        nc.gpsimd.tensor_tensor(rest, whole, main.bitcast(F32), ALU.subtract).then_inc(q_split, 1)

                token_scale(0)
                position_queries(0)
                pool.wait_ge(s_load2, 16 * len(later_loads))
                pool.wait_ge(s_c1, 1)
                prepare(0)
                with pool.Fori(0, B - 1) as b:
                    batch(b, True)
                pool.wait_ge(s_rest, 16)
                prepare(1)
                batch(B - 1, False)

            @block.scalar
            def _(act):
                def tail(c, k, b):
                    n = FIRST + c + b * NC
                    bank = ps[:, tail_bank(c, k), :]
                    if k in (0, 2):
                        m = k // 2
                        act.wait_ge(g_mm, FIRST + (2 * c + m + 1) + b * 4)
                        nc.scalar.activation(gth[:, m, :], bank, ACT.Tanh, scale=0.5).then_inc(gth_r, 1)
                    if k == 5:
                        act.wait_ge(cen_mm, n + 1)
                        nc.scalar.activation(yc[:], bank, ACT.Copy).then_inc(yc_r, 1)
                        nc.scalar.activation(ysq[:], bank, ACT.Square).then_inc(yc_r, 1)

                def exp(i, b):
                    act.wait_ge(max_r, FIRST + (i + 1) + b * NT)
                    n = P * (i + 1)
                    nc.scalar.activation(prob[:, i % 2, 0:n], both(2 * (i % 2))[:, 0:n], ACT.Exp, bias=nmax[:, i % 2:i % 2 + 1],
                                         accum_out=psumr[:, i % 2:i % 2 + 1]).then_inc(exp_r, 1)

                def keep_probT(i, b):
                    for k, (ii, q) in enumerate(QUADS):
                        if ii == i:
                            m = min(4, i + 1 - 4 * q)
                            act.wait_ge(pt_mm, FIRST + (k + 1) + b * NQ)
                            nc.scalar.activation(
                                probT[:, i % 2, 4 * q:4 * q + m, :],
                                ps[:, 4 + k % 2, 0:m * P].rearrange("p (m n) -> p m n", m=m),
                                ACT.Copy).then_inc(pt_ev, 1)

                def keep_mixed(c, b):
                    act.wait_ge(pv_mm, FIRST + (c + 1) * TC + b * NT)
                    nc.scalar.activation(UT[:, c, :], ps[:, 6, :], ACT.Copy).then_inc(u_ev, 1)

                def keep_xT(b):
                    act.wait_ge(xn_t, FIRST + 1 + b)
                    nc.scalar.activation(XT[:], both(0), ACT.Copy).then_inc(xt_r, 1)

                def content_queries(b):
                    act.wait_ge(qa_mm, FIRST + 1 + b)
                    nc.scalar.activation(QA[:], both(2), ACT.Identity, bias=cvec[:, 0:1]).then_inc(qa_r, 1)

                def keep_raw(b):
                    act.wait_ge(raw_t, FIRST + 1 + b)
                    act.wait_ge(y_r, FIRST + b * NC)
                    nc.scalar.activation(XR[:], both(2), ACT.Copy).then_inc(xr_r, 1)

                def batch(b, more):
                    for i in range(NT):
                        if i + 1 < NT:
                            exp(i + 1, b)
                        keep_probT(i, b)
                        for k in SLOT.get(i, ()):
                            tail(0, k, b)
                        if i == TC:
                            keep_mixed(0, b)
                    tail(1, 0, b)
                    keep_mixed(1, b)
                    tail(1, 2, b)
                    if more:
                        keep_xT(b + 1)
                        content_queries(b + 1)
                    tail(1, 5, b)
                    if more:
                        keep_raw(b + 1)
                        exp(0, b + 1)

                keep_xT(0)
                act.wait_ge(s_bm, 2)
                content_queries(0)
                keep_raw(0)
                exp(0, 0)
                with act.Fori(0, B - 1) as b:
                    batch(b, True)
                batch(B - 1, False)

            @block.vector
            def _(dve):
                def tail(c, k, b):
                    n = FIRST + c + b * NC
                    bank = ps[:, tail_bank(c, k), :]
                    m = k // 2
                    g = FIRST + (2 * c + m) + b * 4
                    if k in (0, 2):
                        dve.wait_ge(gth_r, g + 1)
                        nc.vector.scalar_tensor_tensor(gsb[:, m, :], gth[:, m, :], 1.0, bank, ALU.add, ALU.mult).then_inc(gs_r, 1)
                    if k in (1, 3):
                        dve.wait_ge(wv_mm, g + 1)
                        dve.wait_ge(gs_r, g + 1)
                        nc.vector.scalar_tensor_tensor(gated[:, m, :], bank, 0.5, gsb[:, m, :], ALU.mult, ALU.mult).then_inc(gt_r, 1)
                    if k == 4:
                        dve.wait_ge(res_mm, n + 1)
                        dve.wait_ge(xr_r, FIRST + 1 + b)
                        nc.vector.tensor_tensor(yT[:], bank, XR[:, c * CH:(c + 1) * CH], ALU.add).then_inc(y_r, 1)
                    if k == 6:
                        dve.wait_ge(st_mm, n + 1)
                        nc.vector.tensor_scalar(yvar[:], bank[:, 0:TC], 1e-5, None, ALU.add).then_inc(var_r, 1)
                    if k == 7:
                        dve.wait_ge(bc_mm, n + 1)
                        nc.vector.tensor_tensor(XS[:, bass.ds(b, 1), 1 + c * CH:1 + (c + 1) * CH], bank.unsqueeze(1),
                                                yc[:].unsqueeze(1), ALU.mult).then_inc(x_r, 1)

                def rowmax(i, b):
                    dve.wait_ge(s_mm, FIRST + (i + 1) + b * NT)
                    nc.vector.tensor_reduce(nmax[:, i % 2:i % 2 + 1], both(2 * (i % 2))[:, 0:P * (i + 1)], AX.X, ALU.max,
                                            negate=True).then_inc(max_r, 1)

                def normalise(i, b):
                    dve.wait_ge(exp_r, FIRST + (i + 1) + b * NT)
                    r = pinv[:, i % 2:i % 2 + 1]
                    nc.vector.reciprocal(r, psumr[:, i % 2:i % 2 + 1]).then_inc(inv_r, 1)
                    dve.wait_ge(inv_r, FIRST + (i + 1) + b * NT)
                    p = prob[:, i % 2, 0:P * (i + 1)]
                    nc.vector.tensor_scalar(p, p, r, None, ALU.mult).then_inc(p_r, 1)

                def mean_square(b):
                    dve.wait_ge(x_in, 16 + b * 16)
                    nc.vector.tensor_tensor(xsq[:], xin[:], xin[:], ALU.mult).then_inc(xsq_d, 1)
                    dve.wait_ge(xsq_d, FIRST + 1 + b * 2)
                    nc.vector.tensor_reduce(xms[:, 0, :], xsq[:], AX.X, ALU.add).then_inc(xsq_d, 1)
                    dve.wait_ge(xsq_d, FIRST + 2 + b * 2)
                    nc.vector.tensor_scalar(xms[:, 1, :], xms[:, 0, :], 1.0 / D, 1e-6, ALU.mult, ALU.add).then_inc(ms_r, 1)

                def scale_tokens(b):
                    dve.wait_ge(rx_r, FIRST + 1 + b)
                    dve.wait_ge(pv_mm, FIRST + b * NT)
                    nc.vector.tensor_tensor(xn[:], xin[:], xrs[:].unsqueeze(2).to_broadcast([P, NT, D]),
                                            ALU.mult).then_inc(xn_r, 1)

                def rotate(w, b):
                    dve.wait_ge((p1_mm, p2_mm)[w], FIRST + 1 + b)
                    nc.vector.scalar_tensor_tensor((m1, m2)[w][:], both((4, 0)[w]), cvec[:, 1 + w:2 + w], (QSIN, QCOS)[w],
                                                   ALU.add, ALU.mult).then_inc(m_r, 1)

                def batch(b, more):
                    for i in range(NT):
                        normalise(i, b)
                        if i + 1 < NT:
                            rowmax(i + 1, b)
                        for k in SLOT.get(i, ()):
                            tail(0, k, b)
                        if i == 3 and more:
                            mean_square(b + 1)
                    tail(1, 0, b)
                    if more:
                        scale_tokens(b + 1)
                    for k in (2, 1, 3, 4):
                        tail(1, k, b)
                    if more:
                        rotate(0, b + 1)
                        rotate(1, b + 1)
                    tail(1, 6, b)
                    if more:
                        rowmax(0, b + 1)
                    tail(1, 7, b)

                dve.wait_ge(s_maps, 16 * len(map_loads))
                g = vecs[:, 0:1]
                nc.vector.tensor_scalar(raw[:, 0, :], raw[:, 0, :], g, 1.0 / TAU, ALU.mult, ALU.mult).then_inc(s_fold, 1)
                nc.vector.tensor_scalar(raw[:, 1, :], raw[:, 1, :], g, None, ALU.mult).then_inc(s_fold, 1)
                mean_square(0)
                dve.wait_ge(s_wt, 1)
                wt = ps[:, 6, :]
                nc.vector.tensor_copy(wT[:, 0:3, :], wt[:, 0:3 * P].rearrange("p (w n) -> p w n", w=3)).then_inc(s_wte, 1)
                h = P // 2
                nc.vector.tensor_copy(wT[:, 3, 0:h], wt[:, 2 * P + h:3 * P]).then_inc(s_wte, 1)
                nc.vector.tensor_scalar(wT[:, 3, h:P], wt[:, 2 * P:2 * P + h], -1.0, None, ALU.mult).then_inc(s_wte, 1)
                scale_tokens(0)
                dve.wait_ge(s_wp, 1)
                nc.vector.tensor_copy(bmat[:], ps[:, 7, 0:3 * P].rearrange("p (w n) -> p w n", w=3)).then_inc(s_bm, 1)
                nc.vector.tensor_copy(cvec[:], ps[:, 7, 3 * P:3 * P + 3]).then_inc(s_bm, 1)
                dve.wait_ge(s_load, 16 * len(first_loads))
                nc.vector.tensor_copy(identb[:], ident[:]).then_inc(s_masks, 1)
                nc.vector.tensor_copy(causalb[:], causalf[:]).then_inc(s_masks, 1)
                dve.wait_ge(s_bm, 2)
                rotate(0, 0)
                rotate(1, 0)
                nc.vector.tensor_copy(masksb[:], masksf[:])
                nc.vector.tensor_scalar(wv[:], wv[:], g, None, ALU.mult).then_inc(s_masks, 1)
                nc.vector.tensor_scalar(wg[:], wg[:], g, None, ALU.mult).then_inc(s_masks, 1)
                rowmax(0, 0)
                dve.wait_ge(s_c1, 1)
                for l in range(L):
                    for j in range(6):
                        m = HCH[j % 3][1]
                        nc.vector.tensor_tensor(c1[0:m, l, j:j + 1], ps[0:m, 7, 6 * l + j:6 * l + j + 1],
                                                b1c[0:m, l, j:j + 1], ALU.add).then_inc(s_dve, 1)
                m = HCH[2][1]
                nc.vector.tensor_copy(w2_main[0:m, :, 2, :], w2[0:m, :, 2, :]).then_inc(s_dve, 1)
                dve.wait_ge(s_dve, 6 * L + 1)
                nc.vector.tensor_tensor(w2_rest[0:m, :, 2, :], w2[0:m, :, 2, :], w2_main[0:m, :, 2, :].bitcast(F32), ALU.subtract)
                with dve.Fori(0, B - 1) as b:
                    batch(b, True)
                batch(B - 1, False)

            @block.tensor
            def _(pe):
                def tail(c, k, b):
                    n = FIRST + c + b * NC
                    cs = slice(c * CH, (c + 1) * CH)
                    bank = ps[:, tail_bank(c, k), :]
                    m = k // 2
                    if k in (0, 2):
                        if m == 0:
                            pe.wait_ge(x_r, n)
                        elif c == 0:
                            pe.wait_ge(gt_r, FIRST + 1 + b * 4)
                        else:
                            pe.wait_ge(u_ev, FIRST + NC + b * NC)
                        nc.tensor.matmul(bank, wg[:, m * P:(m + 1) * P], XT[:, cs], start=True, stop=True).then_inc(g_mm, 1)
                    if k in (1, 3):
                        pe.wait_ge(gs_r, FIRST + (2 * c + m + 1) + b * 4)
                        pe.wait_ge(u_ev, n + 1)
                        nc.tensor.matmul(bank, wv[:, m * P:(m + 1) * P], UT[:, c, :], start=True, stop=True).then_inc(wv_mm, 1)
                    if k == 4:
                        pe.wait_ge(gt_r, FIRST + (2 * c + 2) + b * 4)
                        for m in range(VC):
                            last = nc.tensor.matmul(bank, woa[:, m, :], gated[:, m, :], start=(m == 0), stop=(m == VC - 1))
                        last.then_inc(res_mm, 1)
                    if k == 5:
                        pe.wait_ge(y_r, n + 1)
                        nc.tensor.matmul(bank, centre[:], yT[:], start=True, stop=True).then_inc(cen_mm, 1)
                    if k == 6:
                        pe.wait_ge(yc_r, FIRST + 2 * c + 2 + b * (2 * NC))
                        for s in range(TC):
                            last = nc.tensor.matmul(bank[:, s:s + 1], ysq[:, s * P:(s + 1) * P], mean1[:], start=True, stop=True)
                        last.then_inc(st_mm, 1)
                    if k == 7:
                        pe.wait_ge(rstd_r, n + 1)
                        for s in range(TC):
                            last = nc.tensor.transpose(bank[:, s * P:(s + 1) * P], yrs[:, s:s + 1].to_broadcast([P, P]), ident[:])
                        last.then_inc(bc_mm, 1)

                def scores(i, b):
                    if i >= 1:
                        pe.wait_ge(exp_r, FIRST + (i - 1) + b * NT)
                    if i == 1:
                        pe.wait_ge(xr_r, FIRST + 1 + b)
                    qs = slice(i * P, (i + 1) * P)
                    for c in range((i + TC) // TC):
                        n = min(CH, P * (i + 1) - c * CH)
                        o = ps[:, 2 * (i % 2) + c, 0:n]
                        nc.tensor.matmul(o, QA[:, qs], XT[:, c * CH:c * CH + n], start=True, stop=False)
                        diag = c == i // TC
                        last = nc.tensor.matmul(o, QB[:, qs], KEYF[:, c * CH:c * CH + n], start=False, stop=not diag)
                        if diag:
                            last = nc.tensor.matmul(o[:, n - P:n], identb[:], causalb[:], start=False, stop=True)
                    last.then_inc(s_mm, 1)

                def transpose_probs(i, b):
                    pe.wait_ge(p_r, FIRST + (i + 1) + b * NT)
                    for k, (ii, q) in enumerate(QUADS):
                        if ii == i:
                            if k >= 2:
                                pe.wait_ge(pt_ev, FIRST + (k - 1) + b * NQ)
                            for m in range(min(4, i + 1 - 4 * q)):
                                j = 4 * q + m
                                last = nc.tensor.transpose(ps[:, 4 + k % 2, m * P:(m + 1) * P],
                                                           prob[:, i % 2, j * P:(j + 1) * P], ident[:])
                            last.then_inc(pt_mm, 1)

                def mix(i, b):
                    pe.wait_ge(pt_ev, FIRST + quads_upto(i) + b * NQ)
                    if i in (0, TC):
                        pe.wait_ge(u_ev, FIRST + i // TC + b * NC)
                    for j in range(i + 1):
                        last = nc.tensor.matmul(ps[:, 6, (i % TC) * P:(i % TC + 1) * P], xn[:, j, :],
                                                probT[:, i % 2, j, :], start=(j == 0), stop=(j == i))
                    last.then_inc(pv_mm, 1)

                def transpose_tokens(src, bank, ready, done, b):
                    pe.wait_ge(*ready)
                    for t in range(NT):
                        last = nc.tensor.transpose(ps[:, bank + t // TC, (t % TC) * P:(t % TC + 1) * P], src[:, t, :], ident[:])
                    last.then_inc(done, 1)

                def queries(w, bank, done, b):
                    for c in range(NC):
                        last = nc.tensor.matmul(ps[:, bank + c, :], bmat[:, w, :], XT[:, c * CH:(c + 1) * CH],
                                                start=True, stop=True)
                    last.then_inc(done, 1)

                def head(k, b):
                    if k == 0:
                        pe.wait_ge(exp_r, FIRST + b * NT)
                        transpose_tokens(xn, 0, (xn_r, FIRST + 1 + b), xn_t, b)
                    if k == 1:
                        pe.wait_ge(xt_r, FIRST + 1 + b)
                        queries(0, 2, qa_mm, b)
                    if k == 2:
                        pe.wait_ge(pt_ev, FIRST + b * NQ)
                        queries(1, 4, p1_mm, b)
                    if k == 3:
                        queries(2, 0, p2_mm, b)
                    if k == 4:
                        pe.wait_ge(qa_r, FIRST + 1 + b)
                        transpose_tokens(xin, 2, (x_in, 16 + b * 16), raw_t, b)
                    if k == 5:
                        pe.wait_ge(qb_r, FIRST + 1 + b)
                        scores(0, b)

                def batch(b, more):
                    for i in range(NT):
                        if i + 1 < NT:
                            scores(i + 1, b)
                        if i == 0:
                            pe.wait_ge(m_r, FIRST + 1 + b * 2)
                        transpose_probs(i, b)
                        slot = SLOT.get(i, ())
                        for k in slot[:1]:
                            tail(0, k, b)
                        if i >= 1:
                            mix(i - 1, b)
                        for k in slot[1:]:
                            tail(0, k, b)
                    tail(1, 0, b)
                    mix(NT - 1, b)
                    tail(1, 2, b)
                    for heads, k in (((0,), 1), ((), 3), ((1,), 4), ((2,), 5), ((3,), 6), ((4, 5), 7)):
                        for h in heads:
                            if more:
                                head(h, b + 1)
                        tail(1, k, b)

                def maps():
                    pe.wait_ge(s_fold, 2)
                    for w in range(3):
                        last = nc.tensor.transpose(ps[:, 6, w * P:(w + 1) * P], raw[:, w, :], ident[:])
                    last.then_inc(s_wt, 1)
                    pe.wait_ge(s_wte, 3)
                    for w in range(3):
                        nc.tensor.matmul(ps[:, 7, w * P:(w + 1) * P], wT[:, 0, :], wT[:, 1 + w, :], start=True, stop=True)
                    for w in range(3):
                        v = 1 if w == 0 else 2
                        last = nc.tensor.matmul(ps[:, 7, 3 * P + w:3 * P + w + 1], wT[:, 1 + w, :], vecs[:, v:v + 1],
                                                start=True, stop=True)
                    last.then_inc(s_wp, 1)

                def hidden_biases():
                    pe.wait_ge(s_load2, 16 * len(later_loads))
                    for l in range(L):
                        for j in range(6):
                            o, m = HCH[j % 3]
                            o += HID * (j // 3)
                            last = nc.tensor.matmul(ps[0:m, 7, 6 * l + j:6 * l + j + 1], w1[:, l, o:o + m],
                                                    lnv[:, l, 1:2], start=True, stop=True)
                    last.then_inc(s_c1, 1)

                maps()
                head(0, 0)
                pe.wait_ge(s_bm, 2)
                for k in range(1, 5):
                    head(k, 0)
                pe.wait_ge(s_masks, 2)
                head(5, 0)
                hidden_biases()
                pe.wait_ge(s_masks, 4)
                pe.wait_ge(s_dve, 6 * L)
                with pe.Fori(0, B - 1) as b:
                    batch(b, True)
                batch(B - 1, False)
        sa.close()

        sf = ExitStack()
        sf.__enter__()
        ffn(nc, sem, counted, lambda name, shape, dt=F32, stack=None: sb(name, shape, dt, stack or sf), ps, XS, ident, identb, centre, mean1, mhalf, masksb, wqkv_main, wqkv_rest, wo, w1_main, w1_rest, w2_main,
            w2_rest, c1, b2,
            tcos, tsin, x_r, out)
        sf.close()


def ffn(nc, sem, counted, sb, ps, XS, ident, identb, centre, mean1, mhalf, masksb, wqkv_main, wqkv_rest, wo, w1_main, w1_rest, w2_main,
            w2_rest, c1, b2,
        tcos, tsin, x_r, out):
    X1 = sb("X1", [P, B, T + 1])
    VB = sb("VB", [P, 4, H, DH + 1])
    VA = sb("VA", [P, 4, H, DH + 1])
    qT = sb("qT", [P, H, P])
    kT = sb("kT", [P, 2, H // 2, 3, W])
    hid = sb("hid", [P, 3, CH])
    mu = sb("mu", [P, NC, TC])
    zv = sb("zv", [P, NC, TC])
    zr = sb("zr", [P, NC, TC])
    with ExitStack() as turn:
        hT = sb("hT", [P, CH], stack=turn)
        hT_main = sb("hT_main", [P, 2, CH], F32R, turn)
        hT_rest = sb("hT_rest", [P, 2, CH], F32R, turn)
        sq = sb("sq", [P, 2, CH], stack=turn)
        ss16 = sb("ss16", [P, 2, 16], stack=turn)
        rn16 = sb("rn16", [P, 2, 16], stack=turn)
        rc = sb("rc", [P, 2, CH], stack=turn)
        rs = sb("rs", [P, 2, CH], stack=turn)
        qkr = sb("qkr", [P, 2, CH], stack=turn)
        qkn = sb("qkn", [P, 2, 2, CH], stack=turn)
        prb = sb("prb", [P, 2, H, P], stack=turn)
        mx = sb("mx", [P, 2, H], stack=turn)
        pT = sb("pT", [P, H, P], stack=turn)
        oinv = sb("oinv", [P, H], stack=turn)
        on = sb("on", [P, H, DH], stack=turn)
        oT = sb("oT", [P, INNER // P, P], stack=turn)
    with ExitStack() as turn:
        h2 = sb("h2", [P, 2, CH], stack=turn)
        hc = sb("hc", [P, 2, CH], stack=turn)
        hsq = sb("hsq", [P, CH], stack=turn)
        hvar = sb("hvar", [P, TC], stack=turn)
        hrs = sb("hrs", [P, TC], stack=turn)
        hn = sb("hn", [P, CH], stack=turn)
        hn_main = sb("hn_main", [P, 2, CH], F32R, turn)
        hn_rest = sb("hn_rest", [P, 2, CH], F32R, turn)
        gel = sb("gel", [P, 3, CH], stack=turn)
        hid_main = sb("hid_main", [P, 2, 3, CH], F32R, turn)
        hid_rest = sb("hid_rest", [P, 2, 3, CH], F32R, turn)

    ini = sem("ffn_buffers_set")
    hid_set = sem("hidden_set")
    (hs_r, hm_r, h_r, qk_mm, v_mm, sq_r, v_r, ssr, ss_own, rn_r, rc_r, rs_r, add_r, qkn_r, tq_mm, tk_mm, qT_r, kT_r, s_mm,
     mx_r, sub_r, e_r, pt_mm, pt_r, pv_mm, oi_r, on_r, ot_mm, ot_r, wo_mm, x1_r) = (counted(n) for n in (
         "shifted_ready", "shifted_main_ready", "hT_ready", "qk_done", "v_done", "squares_ready", "V_ready", "sumsq_ready", "sumsq_own",
         "rnorm_ready", "cos_part_ready", "sin_part_ready", "rotated_ready", "qk_ready", "qT_done",
         "kT_done", "qT_ready", "kT_ready", "win_scores_done", "win_max_ready", "win_shift_ready", "win_exp_ready",
         "win_pT_done", "win_pT_ready", "win_pv_done", "win_inv_ready", "win_out_ready", "oT_done", "oT_ready",
         "wo_done", "X1_ready"))
    (h2_r, ce_mm, hc_r, sv_mm, hv_r, hr_r, hb_mm, hn_r, hnm_r, hnx_r, w1_mm, ge_r, hid_r, hidm_r, hidx_r,
     w2_mm) = (counted(n) for n in (
        "h2_ready", "h2_centred", "hc_ready", "hvar_done", "hvar_ready", "hrstd_ready", "hrstd_spread", "hn_ready",
        "hn_main_ready", "hn_rest_ready", "w1_done", "gelu_ready", "hidden_ready", "hidden_main_ready",
        "hidden_rest_ready", "w2_done"))
    BQ, BV, BT, BS, BP = 0, 2, 3, 5, 7

    flat = lambda buf: buf[:].rearrange("p a h d -> p (a h d)")
    ys = flat(VA)[:, 0:CH]
    zs = flat(VA)[:, CH:2 * CH].rearrange("p (t d) -> p t d", d=D)
    zc = flat(VB)[:, 0:2 * CH].rearrange("p (c t d) -> p c t d", c=NC, d=D)
    zo = flat(VB)[:, 2 * CH:4 * CH].rearrange("p (c t d) -> p c t d", c=NC, d=D)
    (s_y, s_t, s_m, s_m2, s_c, s_q, s_v, s_v2, s_r, s_o) = (counted(n) for n in (
        "sum_ready", "sum_transposed", "total_ready", "mean_ready", "centred_ready", "zsquares_ready", "zsum_ready",
        "zvar_ready", "zrstd_ready", "result_ready"))
    s_out = [sem(f"result_stored_{c}") for c in range(NC)]
    out_v = out.rearrange("b (t p) d -> p b t d", p=P)
    BZ = 7

    def zn(b, c, k=0):
        return b * NC + (FIRST + c + k)

    def add_input(pool, b, c):
        pool.wait_ge(x_r, b * NC + (FIRST + L * B * NC + c + 1))
        if due(zn(b, c)):
            pool.wait_ge(s_t, zn(b, c))
        nc.gpsimd.tensor_tensor(ys.unsqueeze(1), XS[:, bass.ds(b, 1), 1 + c * CH:1 + (c + 1) * CH],
                                XS[:, bass.ds(b + B, 1), 1 + c * CH:1 + (c + 1) * CH], ALU.add).then_inc(s_y, 1)

    def transpose_sum(pe, b, c):
        pe.wait_ge(s_y, zn(b, c, 1))
        if due(zn(b, c)):
            pe.wait_ge(s_c, zn(b, c))
        for t in range(TC):
            last = nc.tensor.transpose(ps[:, BZ, t * P:(t + 1) * P], ys[:, t * P:(t + 1) * P], ident[:])
        last.then_inc(s_t, 1)

    def transpose_last(pe, b, c):
        pe.wait_ge(x_r, FIRST + (L + 1) * B * NC)
        transpose_sum(pe, b, c)

    def centre_sum(dve, b, c):
        z = ps[:, BZ, :].rearrange("p (t d) -> p t d", d=D)
        dve.wait_ge(s_t, zn(b, c, 1))
        nc.vector.tensor_reduce(mu[:, c, :], z, AX.X, ALU.add).then_inc(s_m, 1)
        dve.wait_ge(s_m, zn(b, c, 1))
        nc.vector.tensor_scalar(mu[:, c, :], mu[:, c, :], 1.0 / D, None, ALU.mult).then_inc(s_m2, 1)
        dve.wait_ge(s_m2, zn(b, c, 1))
        nc.vector.tensor_tensor(zc[:, c], z, mu[:, c, :].unsqueeze(2).to_broadcast([P, TC, D]),
                                ALU.subtract).then_inc(s_c, 1)

    def square_sum(act, b, c):
        act.wait_ge(s_c, zn(b, c, 1))
        if due(zn(b, c)):
            act.wait_ge(s_v, zn(b, c))
        nc.scalar.activation(zs, zc[:, c], ACT.Square).then_inc(s_q, 1)

    def sum_variance(dve, b, c):
        dve.wait_ge(s_q, zn(b, c, 1))
        nc.vector.tensor_reduce(zv[:, c, :], zs, AX.X, ALU.add).then_inc(s_v, 1)
        dve.wait_ge(s_v, zn(b, c, 1))
        nc.vector.tensor_scalar(zv[:, c, :], zv[:, c, :], 1.0 / D, 1e-5, ALU.mult, ALU.add).then_inc(s_v2, 1)

    def sum_rstd(pool, b, c):
        pool.wait_ge(s_v2, zn(b, c, 1))
        nc.gpsimd.tensor_tensor(zr[:, c, :], zv[:, c, :], mhalf[:, 0:TC], ALU.pow).then_inc(s_r, 1)

    def scale_sum(dve, b, c):
        dve.wait_ge(s_r, zn(b, c, 1))
        if not isinstance(b, int) or b:
            dve.wait_ge(s_out[c], b * 16)
        nc.vector.tensor_tensor(zo[:, c], zc[:, c], zr[:, c, :].unsqueeze(2).to_broadcast([P, TC, D]),
                                ALU.mult).then_inc(s_o, 1)

    def store_sums(sp, b):
        for c in range(NC):
            sp.wait_ge(s_o, zn(b, c, 1))
            sp.dma_start(out_v[:, bass.ds(b, 1), c * TC:(c + 1) * TC, :], zo[:, c:c + 1]).then_inc(s_out[c], 16)

    def due(v):
        return not isinstance(v, int) or v > FIRST

    def tiles(t):
        return t // NT, t % NT

    attend, project = {}, {}

    def loops(eng, name, step):
        attend[name] = step
        for t in range(-4, 0):
            step(0, t, NT)
            if t == -4 and name in project:
                project[name](B - 1, NC - 1, NC)
        with eng.Fori(0, B - 1) as b:
            for t in range(NT):
                step(b, t, 2 * NT)
        for t in range(NT - 2):
            step(B - 1, t, NT)

    with nc.Block() as block:
        def layer(l):
            n0 = l * B * NT

            def cnt(b, t, per=1, k=0):
                return b * (NT * per) + (FIRST + (n0 + t) * per + k)

            def chunk(b, t, per=1, k=0):
                return b * (NC * per) + (FIRST + (l * B * NC + t // TC) * per + k)

            @block.gpsimd
            def _(pool):
                def split(b, t):
                    c = t // TC % NC
                    pool.wait_ge(hm_r, chunk(b, t, 1, 1))
                    nc.gpsimd.tensor_tensor(hT_rest[:, c, :], hT[:], hT_main[:, c, :].bitcast(F32),
                                            ALU.subtract).then_inc(h_r, 1)

                def step(b, t, end):
                    if t == -4:
                        split(b, 0)
                    j = t + 5
                    if j % TC == 0 and j < end:
                        split(b, j)
                    j = t + 4
                    if j < end:
                        pool.wait_ge(rc_r, cnt(b, j, 1, 1))
                        pool.wait_ge(rs_r, cnt(b, j, 2, 2))
                        if due(cnt(b, j)):
                            pool.wait_ge(qkn_r, cnt(b, j))
                        nc.gpsimd.tensor_tensor(qkr[:], rc[:], rs[:], ALU.add).then_inc(add_r, 1)
                        pool.wait_ge(ssr, cnt(b, j, 1, 1))
                        nc.gpsimd.tensor_tensor(rn16[:, j % 2, :], ss16[:, j % 2, :], mhalf[:], ALU.pow).then_inc(rn_r, 1)

                loops(pool, "pool", step)

            @block.scalar
            def _(act):
                def shift(b, t):
                    db, tt = tiles(t)
                    c = tt // TC
                    g = b * NC + (FIRST + l * B * NC + db * NC + c)
                    act.wait_ge(x_r, g + 1)
                    if due(cnt(b, t - TC)):
                        act.wait_ge(qk_mm, cnt(b, t - TC))
                        act.wait_ge(v_mm, cnt(b, t - TC))
                    if due(chunk(b, t)):
                        act.wait_ge(h_r, chunk(b, t))
                    src = b + (l * B + db)
                    lo, up = (0, D // 2), (D // 2, D)
                    nc.scalar.activation(hT[lo[0]:lo[1]].unsqueeze(1),
                                         XS[lo[0]:lo[1], bass.ds(src, 1), 1 + c * CH:1 + (c + 1) * CH], ACT.Copy).then_inc(hs_r, 1)
                    nc.scalar.activation(hT[up[0]:up[1]].unsqueeze(1),
                                         XS[up[0]:up[1], bass.ds(src, 1), c * CH:(c + 1) * CH], ACT.Copy).then_inc(hs_r, 1)
                    act.wait_ge(hs_r, chunk(b, t, 2, 2))
                    nc.scalar.activation(hT_main[:, c, :], hT[:], ACT.Copy).then_inc(hm_r, 1)

                def keep_pT(b, j, f):
                    act.wait_ge(pt_mm, cnt(b, j, 2, f + 1))
                    nc.scalar.activation(pT[:, 4 * f:4 * f + 4, :], ps[:, BP, :].rearrange("p (h n) -> p h n", n=P),
                                         ACT.Copy).then_inc(pt_r, 1)

                def step(b, t, end):
                    if t == -4:
                        shift(b, 0)
                        act.wait_ge(ini, 6)
                    j = t + 5
                    if j % TC == 0 and j < end:
                        shift(b, j)
                    j = t + 2
                    if 0 <= j < end:
                        qp = ps[:, BT, :].rearrange("p (h n) -> p h n", n=P)
                        kp = ps[:, BT + 1, :].rearrange("p (h s n) -> p h s n", s=2, n=W)
                        act.wait_ge(tq_mm, cnt(b, j, 1, 1))
                        nc.scalar.activation(qT[0:DH, 0:H:2, :], qp[0:DH], ACT.Copy).then_inc(qT_r, 1)
                        act.wait_ge(tk_mm, cnt(b, j, 1, 1))
                        nc.scalar.activation(kT[:, j % 2, :, 0:3:2, :], kp, ACT.Copy).then_inc(kT_r, 1)
                        nc.scalar.activation(qT[DH:P, 1:H:2, :], qp[DH:P], ACT.Copy).then_inc(qT_r, 1)
                    j = t + 1
                    if 0 <= j < end:
                        keep_pT(b, j, 0)
                    j = t + 2
                    if 0 <= j < end:
                        nc.scalar.activation(kT[:, (j + 1) % 2, :, 1:2, :], kp[:, :, 1:2, :], ACT.Copy).then_inc(kT_r, 1)
                    j = t + 3
                    if 0 <= j < end:
                        act.wait_ge(v_mm, cnt(b, j, 1, 1))
                        if due(cnt(b, j - 2, 2)):
                            act.wait_ge(pv_mm, cnt(b, j - 2, 2))
                        v = ps[:, BV, :].rearrange("p (h d) -> p h d", h=H)
                        nc.scalar.activation(VB[:, j % 4, :, 0:DH], v, ACT.Copy).then_inc(v_r, 1)
                        nc.scalar.activation(VA[0:W, j % 4, :, 0:DH], v[0:W], ACT.Copy).then_inc(v_r, 1)
                        nc.scalar.activation(VA[W:P, (j + 1) % 4, :, 0:DH], v[W:P], ACT.Copy).then_inc(v_r, 1)
                    j = t + 1
                    if 0 <= j < end:
                        keep_pT(b, j, 1)
                    j = t + 4
                    if j < end:
                        act.wait_ge(rc_r, cnt(b, j, 1, 1))
                        act.wait_ge(rs_r, cnt(b, j, 2, 2))
                        if due(cnt(b, j)):
                            act.wait_ge(ssr, cnt(b, j))
                        nc.scalar.activation(sq[:], ps[:, BQ:BQ + 2, :], ACT.Square).then_inc(sq_r, 1)
                    if t >= 0:
                        act.wait_ge(ot_mm, cnt(b, t, 1, 1))
                        nc.scalar.activation(oT[:], ps[:, BP, :].rearrange("p (m n) -> p m n", n=P), ACT.Copy).then_inc(ot_r, 1)
                    for f in range(2):
                        j = t + 2
                        if 0 <= j < end:
                            act.wait_ge(sub_r, cnt(b, j, 2, f + 1))
                            p = prb[:, j % 2, 4 * f:4 * f + 4, :]
                            nc.scalar.activation(p, p, ACT.Exp).then_inc(e_r, 1)

                loops(act, "act", step)

            @block.vector
            def _(dve):
                if l == 0:
                    nc.vector.memset(qT[:], 0.0).then_inc(ini, 1)
                    nc.vector.memset(kT[:], 0.0).then_inc(ini, 1)
                    nc.vector.memset(VA[:, :, :, 0:DH], 0.0).then_inc(ini, 1)
                    nc.vector.memset(VA[:, :, :, DH:DH + 1], 1.0).then_inc(ini, 1)
                    nc.vector.memset(VB[:, :, :, DH:DH + 1], 1.0).then_inc(ini, 1)
                    nc.vector.memset(X1[:, :, 0:1], 0.0).then_inc(ini, 1)

                def largest_off(b, j, f):
                    dve.wait_ge(s_mm, cnt(b, j, 2, f + 1))
                    s = ps[:, BS + f, :].rearrange("p (h n) -> p h n", n=P)
                    m = mx[:, f, 0:4]
                    nc.vector.tensor_reduce(m, s, AX.X, ALU.max).then_inc(mx_r, 1)
                    dve.wait_ge(mx_r, cnt(b, j, 2, f + 1))
                    nc.vector.tensor_tensor(prb[:, j % 2, 4 * f:4 * f + 4, :], s,
                                            m.unsqueeze(2).to_broadcast([P, 4, P]), ALU.subtract).then_inc(sub_r, 1)

                def step(b, t, end):
                    j = t + 4
                    if j < end:
                        tt = j % NT
                        qk = ps[:, BQ:BQ + 2, :].rearrange("p a (h d) -> p a h d", h=H)
                        dve.wait_ge(qk_mm, cnt(b, j, 1, 1))
                        if due(cnt(b, j)):
                            dve.wait_ge(add_r, cnt(b, j))
                        nc.vector.tensor_tensor(rc[:].rearrange("p a (h d) -> p a h d", h=H), qk,
                                                tcos[:, l, tt].unsqueeze(2).to_broadcast([P, 2, H, DH]),
                                                ALU.mult).then_inc(rc_r, 1)
                        ro = rs[:].rearrange("p a (h d) -> p a h d", h=H)
                        for f in range(2):
                            i0, o0 = f * HH, (1 - f) * HH
                            nc.vector.tensor_tensor(
                                ro[:, :, :, o0:o0 + HH], qk[:, :, :, i0:i0 + HH],
                                tsin[:, l, tt, :, i0:i0 + HH].unsqueeze(2).to_broadcast([P, 2, H, HH]),
                                ALU.mult).then_inc(rs_r, 1)
                    j = t + 3
                    if 0 <= j < end:
                        dve.wait_ge(add_r, cnt(b, j, 1, 1))
                        dve.wait_ge(rn_r, cnt(b, j, 1, 1))
                        nc.vector.tensor_tensor(qkn[:, j % 2].rearrange("p a (h d) -> p (a h) d", h=H),
                                                qkr[:].rearrange("p a (h d) -> p (a h) d", h=H),
                                                rn16[:, j % 2, :].unsqueeze(2).to_broadcast([P, 16, DH]),
                                                ALU.mult).then_inc(qkn_r, 1)
                    j = t + 2
                    if 0 <= j < end:
                        largest_off(b, j, 0)
                    j = t + 2
                    if 0 <= j < end:
                        largest_off(b, j, 1)
                    j = t + 4
                    if j < end:
                        r = ss16[:, j % 2, :]
                        dve.wait_ge(sq_r, cnt(b, j, 1, 1))
                        nc.vector.tensor_reduce(r, sq[:].rearrange("p a (h d) -> p (a h) d", h=H), AX.X, ALU.add).then_inc(ss_own, 1)
                        dve.wait_ge(ss_own, cnt(b, j, 1, 1))
                        nc.vector.tensor_scalar(r, r, 1e-24, None, ALU.max).then_inc(ssr, 1)
                    j = t + 1
                    if 0 <= j < end:
                        for f in range(2):
                            dve.wait_ge(pv_mm, cnt(b, j, 2, f + 1))
                            o = ps[:, BT + f, 0:4 * (DH + 1)].rearrange("p (h d) -> p h d", h=4)
                            r = oinv[:, 4 * f:4 * f + 4]
                            nc.vector.reciprocal(r.unsqueeze(2), o[:, :, DH:DH + 1]).then_inc(oi_r, 1)
                            dve.wait_ge(oi_r, cnt(b, j, 2, f + 1))
                            nc.vector.tensor_tensor(on[:, f:H:2, :], o[:, :, 0:DH],
                                                    r.unsqueeze(2).to_broadcast([P, 4, DH]), ALU.mult).then_inc(on_r, 1)
                    if t >= 0:
                        dve.wait_ge(wo_mm, cnt(b, t, 1, 1))
                        nc.vector.tensor_tensor(X1[:, bass.ds(b, 1), 1 + t * P:1 + (t + 1) * P],
                                                ps[:, BV:BV + 1, 0:P],
                                                XS[:, bass.ds(b + l * B, 1), 1 + t * P:1 + (t + 1) * P],
                                                ALU.add).then_inc(x1_r, 1)

                loops(dve, "dve", step)

            @block.tensor
            def _(pe):
                def project(j, bank, m):
                    at_h = (j % NT) // TC, slice(j % TC * P, (j % TC + 1) * P)
                    main, rest = hT_main[:, at_h[0], at_h[1]], hT_rest[:, at_h[0], at_h[1]]
                    w = slice(m * INNER, (m + 1) * INNER)
                    nc.tensor.matmul(ps[:, bank, :], rest, wqkv_main[:, l, w], start=True, stop=False)
                    nc.tensor.matmul(ps[:, bank, :], main, wqkv_rest[:, l, w], start=False, stop=False)
                    return nc.tensor.matmul(ps[:, bank, :], main, wqkv_main[:, l, w], start=False, stop=True)

                def step(b, t, end):
                    j = t + 4
                    if j < end:
                        pe.wait_ge(h_r, chunk(b, j, 1, 1))
                        if l and t == -4:
                            pe.wait_ge(hid_r, FIRST + 3 * l * B * NC)
                        if due(cnt(b, j)):
                            pe.wait_ge(rc_r, cnt(b, j))
                        if due(cnt(b, j, 2)):
                            pe.wait_ge(rs_r, cnt(b, j, 2))
                        if due(cnt(b, j)):
                            pe.wait_ge(sq_r, cnt(b, j))
                        for m in range(2):
                            last = project(j, BQ + m, m)
                        last.then_inc(qk_mm, 1)
                    j = t + 2
                    if 0 <= j < end:
                        pe.wait_ge(qkn_r, cnt(b, j, 1, 1))
                        for qk, done in ((0, tq_mm), (1, tk_mm)):
                            if due(cnt(b, j - 1, 2, qk - 1)):
                                pe.wait_ge(on_r, cnt(b, j - 1, 2, qk - 1))
                            for hp in range(H // 2):
                                last = nc.tensor.transpose(ps[:, BT + qk, hp * P:(hp + 1) * P],
                                                           qkn[:, j % 2, qk, hp * P:(hp + 1) * P], ident[:])
                            last.then_inc(done, 1)
                    for f in range(2):
                        j = t + 1
                        if 0 <= j < end:
                            pe.wait_ge(e_r, cnt(b, j, 2, f + 1))
                            if due(cnt(b, j, 2, f)):
                                pe.wait_ge(pt_r, cnt(b, j, 2, f))
                            if due(cnt(b, t)):
                                pe.wait_ge(ot_r, cnt(b, t))
                            for h in range(4):
                                last = nc.tensor.transpose(ps[:, BP, h * P:(h + 1) * P], prb[:, j % 2, 4 * f + h, :], ident[:])
                            last.then_inc(pt_mm, 1)
                        j = t + 3
                        if f == 0 and 0 <= j < end:
                            if due(cnt(b, max(t, 0))):
                                pe.wait_ge(x1_r, cnt(b, max(t, 0)))
                            if due(cnt(b, j, 3)):
                                pe.wait_ge(v_r, cnt(b, j, 3))
                            project(j, BV, 2).then_inc(v_mm, 1)
                        j = t + 2
                        if 0 <= j < end:
                            pe.wait_ge(qT_r, cnt(b, j, 2, f + 1))
                            pe.wait_ge(kT_r, cnt(b, j, 2, 1))
                            if due(cnt(b, j - 1, 2, f + 1)):
                                pe.wait_ge(sub_r, cnt(b, j - 1, 2, f + 1))
                            nc.tensor.matmul(ps[:, BS + f, :], identb[:], masksb[:, 0 if j % NT == 0 else 1, :],
                                             start=True, stop=False, skip_group_check=True)
                            for h in range(4):
                                for w in range(2):
                                    keys = kT[:, j % 2, h, 0:2, :] if w == 0 else kT[:, j % 2, h, 0:3:2, :]
                                    last = nc.tensor.matmul(ps[w * W:(w + 1) * W, BS + f, h * P:(h + 1) * P],
                                                            qT[:, 2 * h + f, w * W:(w + 1) * W], keys,
                                                            start=False, stop=(h == 3), skip_group_check=True)
                            last.then_inc(s_mm, 1)
                    if t >= 0:
                        pe.wait_ge(on_r, cnt(b, t, 2, 2))
                        if due(cnt(b, min(t + 2, end), 2)):
                            pe.wait_ge(pt_r, cnt(b, min(t + 2, end), 2))
                        for m in range(INNER // P):
                            last = nc.tensor.transpose(ps[:, BP, m * P:(m + 1) * P], on[:, 2 * m:2 * m + 2, :].rearrange("p h d -> p (h d)"), ident[:])
                        last.then_inc(ot_mm, 1)
                    j = t + 1
                    if 0 <= j < end:
                        pe.wait_ge(v_r, cnt(b, j, 3, 3))
                        for f in range(2):
                            pe.wait_ge(pt_r, cnt(b, j, 2, f + 1))
                            if f == 0:
                                if due(cnt(b, min(j + 2, end), 2)):
                                    pe.wait_ge(qT_r, cnt(b, min(j + 2, end), 2))
                            else:
                                if due(cnt(b, min(j + 2, end), 2)):
                                    pe.wait_ge(kT_r, cnt(b, min(j + 2, end), 2))
                            for h in range(4):
                                for w, val in ((0, VA), (1, VB)):
                                    last = nc.tensor.matmul(ps[w * W:(w + 1) * W, BT + f, h * (DH + 1):(h + 1) * (DH + 1)],
                                                            pT[:, 4 * f + h, w * W:(w + 1) * W], val[:, j % 4, 2 * h + f, :],
                                                            start=True, stop=True)
                            last.then_inc(pv_mm, 1)
                    if t >= 0:
                        pe.wait_ge(ot_r, cnt(b, t, 1, 1))
                        if due(cnt(b, min(t + 4, end), 3)):
                            pe.wait_ge(v_r, cnt(b, min(t + 4, end), 3))
                        if due(cnt(b, t)):
                            pe.wait_ge(x1_r, cnt(b, t))
                        for m in range(INNER // P):
                            last = nc.tensor.matmul(ps[:, BV, 0:P], wo[:, l, m, :], oT[:, m, :],
                                                    start=(m == 0), stop=(m == INNER // P - 1))
                        last.then_inc(wo_mm, 1)

                loops(pe, "pe", step)

            g0 = l * B * NC
            BC, BW2 = 6, 7

            def at(b, c, per=1, k=0):
                return b * (NC * per) + (FIRST + (g0 + c) * per + k)

            def rounds(eng, name, norm, step, parts):
                norm(0, 0, 0)
                attend[name](B - 1, NT - 2, NT)
                norm(0, 0, 1)
                attend[name](B - 1, NT - 1, NT)
                norm(0, 0, 2)
                step(0, -1, NC)
                if l < L - 1:
                    project[name] = step
                    with eng.Fori(0, B - 1) as b:
                        for c in range(NC):
                            step(b, c, 2 * NC)
                    for c in range(NC - 1):
                        step(B - 1, c, NC)
                else:
                    for c in range(NC):
                        step(0, c, 2 * NC)
                    with eng.Fori(0, B - 2) as done:
                        for c in range(NC):
                            step(done + 1, c, 2 * NC, done)
                    for c in range(NC):
                        step(B - 1, c, NC, B - 2)
                    for part in parts:
                        for c in range(NC):
                            part(eng, B - 1, c)

            if l == L - 1:
                @block.sync
                def _(sp):
                    with sp.Fori(0, B) as b:
                        store_sums(sp, b)
                    for c in range(NC):
                        sp.wait_ge(s_out[c], 16 * B)

            @block.gpsimd
            def _(pool):
                def norm(b, j, stage):
                    if stage == 2:
                        pool.wait_ge(hv_r, at(b, j, 1, 1))
                        nc.gpsimd.tensor_tensor(hrs[:], hvar[:], mhalf[:, 0:TC], ALU.pow).then_inc(hr_r, 1)

                def step(b, c, end, done=None):
                    if done is not None:
                        add_input(pool, done, c)
                    if c + 2 < end:
                        norm(b, c + 2, 2)
                    j = c + 1
                    if 0 <= j < end:
                        for k in range(3):
                            if k == 2 and done is not None:
                                sum_rstd(pool, done, c)
                            pool.wait_ge(hidm_r, at(b, j, 3, k + 1))
                            nc.gpsimd.tensor_tensor(hid_rest[:, j % 2, k, :], hid[:, k, :],
                                                    hid_main[:, j % 2, k, :].bitcast(F32), ALU.subtract).then_inc(hidx_r, 1)
                    elif done is not None:
                        sum_rstd(pool, done, c)

                rounds(pool, "pool", norm, step, (add_input, sum_rstd))

            @block.scalar
            def _(act):
                def gelu(b, j, k):
                    m = HCH[k][1]
                    act.wait_ge(w1_mm, at(b, j, 3, k + 1))
                    if due(at(b, j, 3, k - 2)):
                        act.wait_ge(hid_r, at(b, j, 3, k - 2))
                    nc.scalar.activation(gel[0:m, k, :], ps[0:m, 2 * k + 1, :], ACT.Gelu,
                                         bias=c1[0:m, l, 3 + k:4 + k]).then_inc(ge_r, 1)

                def main_of_hidden(b, j, k):
                    act.wait_ge(hid_r, at(b, j, 3, k + 1))
                    if due(at(b, j - 1)):
                        act.wait_ge(w2_mm, at(b, j - 1))
                    nc.scalar.activation(hid_main[:, j % 2, k, :], hid[:, k, :], ACT.Copy).then_inc(hidm_r, 1)

                def norm(b, j, stage):
                    if stage == 0:
                        r = j % NC
                        x = bass.ds(b + j // NC, 1)
                        act.wait_ge(x1_r, b * NT + (FIRST + l * B * NT + (j + 1) * TC))
                        if due(at(b, j - 1)):
                            act.wait_ge(ce_mm, at(b, j - 1))
                        nc.scalar.activation(h2[0:D // 2, r:r + 1, :], X1[0:D // 2, x, 1 + r * CH:1 + (r + 1) * CH],
                                             ACT.Copy).then_inc(h2_r, 1)
                        nc.scalar.activation(h2[D // 2:D, r:r + 1, :], X1[D // 2:D, x, r * CH:(r + 1) * CH],
                                             ACT.Copy).then_inc(h2_r, 1)
                    if stage == 1:
                        act.wait_ge(ce_mm, at(b, j, 1, 1))
                        if due(at(b, j - 1)):
                            act.wait_ge(hn_r, at(b, j - 1))
                        nc.scalar.activation(hc[:, j % 2, :], ps[:, BC, :], ACT.Copy).then_inc(hc_r, 1)
                        nc.scalar.activation(hsq[:], ps[:, BC, :], ACT.Square).then_inc(hc_r, 1)
                    if stage == 2:
                        act.wait_ge(hn_r, at(b, j, 1, 1))
                        nc.scalar.activation(hn_main[:, j % 2, :], hn[:], ACT.Copy).then_inc(hnm_r, 1)

                def step(b, c, end, done=None):
                    ahead, mid = c + 2 < end, 0 <= c + 1 < end
                    if ahead:
                        norm(b, c + 2, 0)
                    if mid:
                        gelu(b, c + 1, 0)
                    if ahead:
                        norm(b, c + 2, 1)
                    if mid:
                        main_of_hidden(b, c + 1, 0)
                        gelu(b, c + 1, 1)
                        main_of_hidden(b, c + 1, 1)
                    if done is not None:
                        square_sum(act, done, c)
                    if mid:
                        gelu(b, c + 1, 2)
                    if ahead:
                        norm(b, c + 2, 2)
                    if mid:
                        main_of_hidden(b, c + 1, 2)

                if l == 0:
                    act.wait_ge(hid_set, 1)
                rounds(act, "act", norm, step, (square_sum,))

            @block.vector
            def _(dve):
                def hidden(b, j, k):
                    m = HCH[k][1]
                    dve.wait_ge(ge_r, at(b, j, 3, k + 1))
                    if due(at(b, j, 3, k - 2)):
                        dve.wait_ge(hidx_r, at(b, j, 3, k - 2))
                    nc.vector.scalar_tensor_tensor(hid[0:m, k, :], ps[0:m, 2 * k, :], c1[0:m, l, k:k + 1],
                                                   gel[0:m, k, :], ALU.add, ALU.mult).then_inc(hid_r, 1)

                def norm(b, j, stage):
                    if stage == 1:
                        dve.wait_ge(sv_mm, at(b, j, 1, 1))
                        nc.vector.tensor_scalar(hvar[:], ps[:, BC, 0:TC], 1e-5, None, ALU.add).then_inc(hv_r, 1)
                    if stage == 2:
                        dve.wait_ge(hb_mm, at(b, j, 1, 1))
                        dve.wait_ge(hc_r, at(b, j, 2, 1))
                        nc.vector.tensor_tensor(hn[:], ps[:, BC, :], hc[:, j % 2, :], ALU.mult).then_inc(hn_r, 1)

                def rest_of_norm(b, j):
                    dve.wait_ge(hnm_r, at(b, j, 1, 1))
                    nc.vector.tensor_tensor(hn_rest[:, j % 2, :], hn[:], hn_main[:, j % 2, :].bitcast(F32),
                                            ALU.subtract).then_inc(hnx_r, 1)

                def step(b, c, end, done=None):
                    ahead, mid = c + 2 < end, 0 <= c + 1 < end
                    if c == -1:
                        rest_of_norm(0, 0)
                    if mid:
                        hidden(b, c + 1, 0)
                    if ahead:
                        norm(b, c + 2, 1)
                    if mid:
                        hidden(b, c + 1, 1)
                    if done is not None:
                        centre_sum(dve, done, c)
                    if ahead:
                        norm(b, c + 2, 2)
                    if mid:
                        hidden(b, c + 1, 2)
                    if done is not None:
                        sum_variance(dve, done, c)
                    if ahead:
                        rest_of_norm(b, c + 2)
                    if c >= 0:
                        dve.wait_ge(w2_mm, at(b, c, 1, 1))
                        nc.vector.scalar_tensor_tensor(
                            XS[:, bass.ds(b + B, 1), 1 + c * CH:1 + (c + 1) * CH], ps[:, BW2:BW2 + 1, :],
                            b2[:, l:l + 1], X1[:, bass.ds(b, 1), 1 + c * CH:1 + (c + 1) * CH],
                            ALU.add, ALU.add).then_inc(x_r, 1)
                    if done is not None:
                        scale_sum(dve, done, c)

                if l == 0:
                    nc.vector.memset(hid[:, 2, :], 0.0).then_inc(hid_set, 1)
                    dve.wait_ge(hid_set, 1)
                rounds(dve, "dve", norm, step, (centre_sum, sum_variance, scale_sum))

            @block.tensor
            def _(pe):
                def three(out, w_main, w_rest, x_main, x_rest, first=True, last=True):
                    nc.tensor.matmul(out, w_main, x_rest, start=first, stop=False)
                    nc.tensor.matmul(out, w_rest, x_main, start=False, stop=False)
                    return nc.tensor.matmul(out, w_main, x_main, start=False, stop=last)

                def project_in(b, j, k):
                    o, m = HCH[k]
                    if k == 0:
                        pe.wait_ge(hnx_r, at(b, j, 1, 1))
                    if due(at(b, j, 3, k - 2)):
                        pe.wait_ge(hid_r, at(b, j, 3, k - 2))
                    for half in range(2):
                        w = slice(half * HID + o, half * HID + o + m)
                        last = three(ps[0:m, 2 * k + half, :], w1_main[:, l, w], w1_rest[:, l, w],
                                     hn_main[:, j % 2, :], hn_rest[:, j % 2, :])
                    last.then_inc(w1_mm, 1)

                def norm(b, j, stage):
                    if stage == 0:
                        pe.wait_ge(h2_r, at(b, j, 2, 2))
                        if j == 0 and isinstance(b, int):
                            pe.wait_ge(sub_r, cnt(B - 1, NT, 2))
                        if due(at(b, j)):
                            pe.wait_ge(hn_r, at(b, j))
                        nc.tensor.matmul(ps[:, BC, :], centre[:], h2[:, j % NC, :], start=True, stop=True).then_inc(ce_mm, 1)
                    if stage == 1:
                        pe.wait_ge(hc_r, at(b, j, 2, 2))
                        for s in range(TC):
                            last = nc.tensor.matmul(ps[:, BC, s:s + 1], hsq[:, s * P:(s + 1) * P], mean1[:],
                                                    start=True, stop=True)
                        last.then_inc(sv_mm, 1)
                    if stage == 2:
                        pe.wait_ge(hr_r, at(b, j, 1, 1))
                        for s in range(TC):
                            last = nc.tensor.transpose(ps[:, BC, s * P:(s + 1) * P], hrs[:, s:s + 1].to_broadcast([P, P]), ident[:])
                        last.then_inc(hb_mm, 1)

                def step(b, c, end, done=None):
                    ahead, mid = c + 2 < end, 0 <= c + 1 < end
                    if mid:
                        project_in(b, c + 1, 0)
                    if ahead:
                        norm(b, c + 2, 0)
                    if mid:
                        project_in(b, c + 1, 1)
                    if done is not None:
                        pe.wait_ge(x_r, at(b, c) + B * NC)
                        transpose_sum(pe, done, c)
                    if ahead:
                        norm(b, c + 2, 1)
                    if mid:
                        project_in(b, c + 1, 2)
                    if ahead:
                        norm(b, c + 2, 2)
                    if c >= 0:
                        pe.wait_ge(hidx_r, at(b, c, 3, 3))
                        if done is not None:
                            pe.wait_ge(s_c, zn(done, c, 1))
                        elif due(at(b, c) + B * NC):
                            pe.wait_ge(x_r, at(b, c) + B * NC)
                        for k, (o, m) in enumerate(HCH):
                            last = three(ps[:, BW2, :], w2_main[0:m, l, k, :], w2_rest[0:m, l, k, :],
                                         hid_main[0:m, c % 2, k, :], hid_rest[0:m, c % 2, k, :], k == 0, k == 2)
                        last.then_inc(w2_mm, 1)

                rounds(pe, "pe", norm, step, (transpose_last,))

        for l in range(L):
            layer(l)


def kernel(**inputs):
    import numpy as _np
    import concourse.bacc as _bacc
    from concourse import mybir as _mybir
    from concourse.bass_utils import run_bass_kernel_spmd as _run

    nc = _bacc.Bacc("TRN2", target_bir_lowering=False, num_devices=1)
    arrays, aps = {}, {}
    for name, value in {**inputs, **constants()}.items():
        arr = _np.ascontiguousarray(value)
        arrays[f"in_{name}"] = arr
        aps[name] = nc.dram_tensor(f"in_{name}", arr.shape, _mybir.dt.from_np(arr.dtype), kind="ExternalInput").ap()
    out = nc.dram_tensor("out", (B, T, D), _mybir.dt.float32, kind="ExternalOutput").ap()
    build(nc, aps, out)
    r = _run(nc, [arrays], core_ids=[0])
    return r.results[0]["out"]
```
